# Optimizing a Trainium2 kernel written in Bass

```python
import numpy as np
import jax
import jax.numpy as jnp

def _softmax(x, axis=-1):
    return jax.nn.softmax(x, axis=axis)

def _gelu(x):
    return jax.nn.gelu(x, approximate=True)

def _silu(x):
    return jax.nn.silu(x)

def _sigmoid(x):
    return jax.nn.sigmoid(x)

def _layernorm(x, axis=-1, eps=1e-05):
    m = jnp.mean(x, axis=axis, keepdims=True)
    v = jnp.var(x, axis=axis, keepdims=True)
    return (x - m) / jnp.sqrt(v + eps)

def _scatter_add(tgt, idx, src, axis=0):
    return tgt.at[idx].add(src)

def _segment_sum(src, seg, n):
    return jax.ops.segment_sum(src, seg, n)
kernel_name = 'mk_gnn_resnorm_d4_gnn_r64_9c03ea'

def setup_inputs(seed: int=0):
    np.random.seed(seed)
    _w = jnp.asarray

    def _rec_inputs():
        import jax
        import jax.numpy as jnp
        _gk = jax.random.key(seed)
        x = -0.000202 + 1 * jax.random.normal(jax.random.fold_in(_gk, 1), (50000, 128), jnp.float32)
        src = jax.random.randint(jax.random.fold_in(_gk, 2), (12500,), 0, 50000, jnp.int32)
        dst = jnp.minimum((50000 * jax.random.uniform(jax.random.fold_in(_gk, 3), (12500,)) ** 2.0).astype(jnp.int32), 49999)
        _o = jnp.argsort(dst, stable=True)
        src = src[_o]
        dst = dst[_o]
        edge_attr_128 = -5.16925e-05 + 1.00005 * jax.random.normal(jax.random.fold_in(_gk, 12), (12500, 128), jnp.float32)
        edge_type_8 = jax.random.randint(jax.random.fold_in(_gk, 14), (12500,), 0, 8, jnp.int32)
        return (x, src, dst, edge_attr_128, edge_type_8)
    x, src, dst, edge_attr_128, edge_type_8 = _rec_inputs()

    def _L0_gnn_setup():
        import jax, jax.numpy as jnp
        import numpy as np
        N = 50000
        E = 12500
        D_NODE = 128
        D_EDGE = 128
        HID = 256
        D_OUT = 128
        key = jax.random.key(seed)
        ks = jax.random.split(key, 12)
        x = jax.random.normal(ks[0], (N, D_NODE), dtype=jnp.float32)
        edge_index = jax.random.randint(ks[1], (2, E), 0, N, dtype=jnp.int64)
        edge_attr = jax.random.normal(ks[2], (E, D_EDGE), dtype=jnp.float32)
        u = jax.random.normal(ks[3], (1, 64), dtype=jnp.float32)
        batch = jnp.zeros((N,), dtype=jnp.int64)
        s1 = 1.0 / np.sqrt(D_NODE + D_EDGE)
        W1a = jax.random.uniform(ks[4], (D_NODE + D_EDGE, HID), minval=-s1, maxval=s1, dtype=jnp.float32)
        b1a = jax.random.uniform(ks[5], (HID,), minval=-s1, maxval=s1, dtype=jnp.float32)
        s2 = 1.0 / np.sqrt(HID)
        W1b = jax.random.uniform(ks[6], (HID, HID), minval=-s2, maxval=s2, dtype=jnp.float32)
        b1b = jax.random.uniform(ks[7], (HID,), minval=-s2, maxval=s2, dtype=jnp.float32)
        s3 = 1.0 / np.sqrt(D_NODE + HID)
        W2a = jax.random.uniform(ks[8], (D_NODE + HID, HID), minval=-s3, maxval=s3, dtype=jnp.float32)
        b2a = jax.random.uniform(ks[9], (HID,), minval=-s3, maxval=s3, dtype=jnp.float32)
        W2b = jax.random.uniform(ks[10], (HID, D_OUT), minval=-s2, maxval=s2, dtype=jnp.float32)
        b2b = jax.random.uniform(ks[11], (D_OUT,), minval=-s2, maxval=s2, dtype=jnp.float32)
        return dict(x=x, edge_index=edge_index, edge_attr=edge_attr, u=u, batch=batch, W1a=W1a, b1a=b1a, W1b=W1b, b1b=b1b, W2a=W2a, b2a=b2a, W2b=W2b, b2b=b2b)
    _L0_gnn_all = _L0_gnn_setup()
    _L0_gnn_in = {k: v for k, v in _L0_gnn_all.items() if k in ('u', 'W1a', 'b1a', 'W1b', 'b1b', 'W2a', 'b2a', 'W2b', 'b2b')}
    del _L0_gnn_all

    def _L1_gnn_setup():
        import jax, jax.numpy as jnp
        import numpy as np
        N = 100000
        E = 25000
        C_IN = 128
        C_OUT = 128
        key = jax.random.key(seed)
        k1, k2, k3 = jax.random.split(key, 3)
        x = jax.random.normal(k1, (N, C_IN), dtype=jnp.float32)
        edge_index = jax.random.randint(k2, (2, E), 0, N, dtype=jnp.int64)
        W = jax.random.normal(k3, (C_OUT, C_IN), dtype=jnp.float32) * (1.0 / np.sqrt(C_IN))
        return {'x': x, 'edge_index': edge_index, 'W': W}
    _L1_gnn_all = _L1_gnn_setup()
    _L1_gnn_in = {k: v for k, v in _L1_gnn_all.items() if k in ('W',)}
    del _L1_gnn_all

    def _L2_gnn_setup():
        import jax, jax.numpy as jnp
        import numpy as np
        N_NODES = 100000
        N_EDGES = 9375
        H = 128
        T = 8
        L = 2

        def _gru_cell(x, h, wih, whh, bih, bhh):
            gi = x @ wih.T + bih
            gh = h @ whh.T + bhh
            i_r, i_z, i_n = jnp.split(gi, 3, axis=-1)
            h_r, h_z, h_n = jnp.split(gh, 3, axis=-1)
            r = jax.nn.sigmoid(i_r + h_r)
            z = jax.nn.sigmoid(i_z + h_z)
            n = jnp.tanh(i_n + r * h_n)
            return (1.0 - z) * n + z * h
        key = jax.random.key(seed)
        ks = jax.random.split(key, 12)
        s = 1.0 / np.sqrt(H)
        inp = {'node_features': jax.random.normal(ks[0], (N_NODES, H), dtype=jnp.float32), 'edge_index': jax.random.randint(ks[1], (2, N_EDGES), 0, N_NODES, dtype=jnp.int64), 'edge_type': jax.random.randint(ks[2], (N_EDGES,), 0, T, dtype=jnp.int64), 'node_proj_w': jax.random.uniform(ks[3], (H, H), jnp.float32, -s, s), 'node_proj_b': jax.random.uniform(ks[4], (H,), jnp.float32, -s, s), 'edge_W': jax.random.uniform(ks[5], (L, T, H, H), jnp.float32, -s, s), 'edge_b': jax.random.uniform(ks[6], (L, T, H), jnp.float32, -s, s), 'gru_wih': jax.random.uniform(ks[7], (L, 3 * H, H), jnp.float32, -s, s), 'gru_whh': jax.random.uniform(ks[8], (L, 3 * H, H), jnp.float32, -s, s), 'gru_bih': jax.random.uniform(ks[9], (L, 3 * H), jnp.float32, -s, s), 'gru_bhh': jax.random.uniform(ks[10], (L, 3 * H), jnp.float32, -s, s), 'out_w': jax.random.uniform(ks[11], (H, H), jnp.float32, -s, s), 'out_b': jnp.zeros((H,), jnp.float32)}
        return inp
    _L2_gnn_all = _L2_gnn_setup()
    _L2_gnn_in = {k: v for k, v in _L2_gnn_all.items() if k in ('node_proj_w', 'node_proj_b', 'edge_W', 'edge_b', 'gru_wih', 'gru_whh', 'gru_bih', 'gru_bhh', 'out_w', 'out_b')}
    del _L2_gnn_all

    def _L3_gnn_setup():
        import jax, jax.numpy as jnp
        import numpy as np
        N = 50000
        E = 12500
        D = 128
        MAX_NODES = 4
        EPS = 1e-05

        def sort_conv(x, edge_index, blank, W, b, cw, cb, a):
            n, d = x.shape
            e = edge_index.shape[1]
            src, dst = (edge_index[0], edge_index[1])
            msgs = x[src]
            order = jnp.argsort(dst)
            dst_s = dst[order]
            counts = jax.ops.segment_sum(jnp.ones((e,), jnp.int32), dst, num_segments=n + 1)
            starts = jnp.concatenate([jnp.zeros((1,), jnp.int32), jnp.cumsum(counts)[:-1].astype(jnp.int32)])
            pos = jnp.arange(e, dtype=jnp.int32) - starts[dst_s]
            slot = jnp.where(pos < MAX_NODES, pos, MAX_NODES)
            dense = jnp.zeros((n + 1, MAX_NODES + 1, d), x.dtype).at[dst_s, slot].set(msgs[order])
            mask = jnp.zeros((n + 1, MAX_NODES + 1), bool).at[dst_s, slot].set(True)
            dense, mask = (dense[:, :MAX_NODES], mask[:, :MAX_NODES])
            blank_p = W @ blank + b
            filled = dense + (~mask)[..., None].astype(x.dtype) * blank_p
            srt = jnp.sort(filled, axis=1)
            out = jnp.einsum('nmd,m->nd', srt, cw) + cb
            node_out, blank_new = (out[:-1], out[-1])
            return (a * x + node_out, a * blank + blank_new)

        def batch_norm(h, g, be):
            mu = h.mean(0)
            var = h.var(0)
            return (h - mu) / jnp.sqrt(var + EPS) * g + be
        key = jax.random.key(seed)
        ks = jax.random.split(key, 16)
        inp = {'x': jax.random.normal(ks[0], (N, D), jnp.float32), 'edge_index': jax.random.randint(ks[1], (2, E), 0, N, jnp.int32)}
        for i in range(2):
            o = 2 + 6 * i
            W = jax.random.normal(ks[o], (D, D), jnp.float32) * (2.0 / (D + D)) ** 0.5
            W = W / jnp.linalg.norm(W, axis=1, keepdims=True)
            inp[f'W{i}'] = W
            inp[f'b{i}'] = jnp.zeros((D,), jnp.float32)
            inp[f'cw{i}'] = jax.random.normal(ks[o + 1], (MAX_NODES,), jnp.float32) * (2.0 / (MAX_NODES + 1)) ** 0.5
            inp[f'cb{i}'] = jnp.zeros((1,), jnp.float32)
            inp[f'a{i}'] = jax.random.uniform(ks[o + 2], (1,), jnp.float32, -1.0, 1.0)
            inp[f'g{i}'] = jnp.ones((D,), jnp.float32)
            inp[f'be{i}'] = jnp.zeros((D,), jnp.float32)
            inp[f'blank{i}'] = jnp.zeros((D,), jnp.float32)
        return inp
    _L3_gnn_all = _L3_gnn_setup()
    _L3_gnn_in = {k: v for k, v in _L3_gnn_all.items() if k in ('W0', 'b0', 'cw0', 'cb0', 'a0', 'g0', 'be0', 'blank0', 'W1', 'b1', 'cw1', 'cb1', 'a1', 'g1', 'be1', 'blank1')}
    del _L3_gnn_all
    return {'x': x, 'src': src, 'dst': dst, 'edge_attr_128': edge_attr_128, 'edge_type_8': edge_type_8, 'L0_gnn_u': _L0_gnn_in['u'], 'L0_gnn_W1a': _L0_gnn_in['W1a'], 'L0_gnn_b1a': _L0_gnn_in['b1a'], 'L0_gnn_W1b': _L0_gnn_in['W1b'], 'L0_gnn_b1b': _L0_gnn_in['b1b'], 'L0_gnn_W2a': _L0_gnn_in['W2a'], 'L0_gnn_b2a': _L0_gnn_in['b2a'], 'L0_gnn_W2b': _L0_gnn_in['W2b'], 'L0_gnn_b2b': _L0_gnn_in['b2b'], 'L1_gnn_W': _L1_gnn_in['W'], 'L2_gnn_node_proj_w': _L2_gnn_in['node_proj_w'], 'L2_gnn_node_proj_b': _L2_gnn_in['node_proj_b'], 'L2_gnn_edge_W': _L2_gnn_in['edge_W'], 'L2_gnn_edge_b': _L2_gnn_in['edge_b'], 'L2_gnn_gru_wih': _L2_gnn_in['gru_wih'], 'L2_gnn_gru_whh': _L2_gnn_in['gru_whh'], 'L2_gnn_gru_bih': _L2_gnn_in['gru_bih'], 'L2_gnn_gru_bhh': _L2_gnn_in['gru_bhh'], 'L2_gnn_out_w': _L2_gnn_in['out_w'], 'L2_gnn_out_b': _L2_gnn_in['out_b'], 'L3_gnn_W0': _L3_gnn_in['W0'], 'L3_gnn_b0': _L3_gnn_in['b0'], 'L3_gnn_cw0': _L3_gnn_in['cw0'], 'L3_gnn_cb0': _L3_gnn_in['cb0'], 'L3_gnn_a0': _L3_gnn_in['a0'], 'L3_gnn_g0': _L3_gnn_in['g0'], 'L3_gnn_be0': _L3_gnn_in['be0'], 'L3_gnn_blank0': _L3_gnn_in['blank0'], 'L3_gnn_W1': _L3_gnn_in['W1'], 'L3_gnn_b1': _L3_gnn_in['b1'], 'L3_gnn_cw1': _L3_gnn_in['cw1'], 'L3_gnn_cb1': _L3_gnn_in['cb1'], 'L3_gnn_a1': _L3_gnn_in['a1'], 'L3_gnn_g1': _L3_gnn_in['g1'], 'L3_gnn_be1': _L3_gnn_in['be1'], 'L3_gnn_blank1': _L3_gnn_in['blank1']}

def reference(x, src, dst, edge_attr_128, edge_type_8, L0_gnn_u, L0_gnn_W1a, L0_gnn_b1a, L0_gnn_W1b, L0_gnn_b1b, L0_gnn_W2a, L0_gnn_b2a, L0_gnn_W2b, L0_gnn_b2b, L1_gnn_W, L2_gnn_node_proj_w, L2_gnn_node_proj_b, L2_gnn_edge_W, L2_gnn_edge_b, L2_gnn_gru_wih, L2_gnn_gru_whh, L2_gnn_gru_bih, L2_gnn_gru_bhh, L2_gnn_out_w, L2_gnn_out_b, L3_gnn_W0, L3_gnn_b0, L3_gnn_cw0, L3_gnn_cb0, L3_gnn_a0, L3_gnn_g0, L3_gnn_be0, L3_gnn_blank0, L3_gnn_W1, L3_gnn_b1, L3_gnn_cw1, L3_gnn_cb1, L3_gnn_a1, L3_gnn_g1, L3_gnn_be1, L3_gnn_blank1):
    import jax
    import jax.numpy as jnp

    def _L0_gnn_ref(x, edge_index, edge_attr, u, batch, W1a, b1a, W1b, b1b, W2a, b2a, W2b, b2b):
        import jax, jax.numpy as jnp
        import numpy as np
        N = 50000
        E = 12500
        D_NODE = 128
        D_EDGE = 128
        HID = 256
        D_OUT = 128
        row, col = (edge_index[0], edge_index[1])
        n = x.shape[0]
        msg = jnp.concatenate([x[row], edge_attr], axis=1)
        h = jax.nn.elu(msg @ W1a + b1a) @ W1b + b1b
        summed = jax.ops.segment_sum(h, col, num_segments=n)
        counts = jax.ops.segment_sum(jnp.ones((h.shape[0],), dtype=h.dtype), col, num_segments=n)
        agg = summed / jnp.maximum(counts, 1.0)[:, None]
        z = jnp.concatenate([x, agg], axis=1)
        return jax.nn.elu(z @ W2a + b2a) @ W2b + b2b

    def _L1_gnn_ref(x, edge_index, W):
        import jax, jax.numpy as jnp
        import numpy as np
        N = 100000
        E = 25000
        C_IN = 128
        C_OUT = 128
        n_nodes = x.shape[0]
        row, col = (edge_index[0], edge_index[1])
        deg = jax.ops.segment_sum(jnp.ones((row.shape[0],), dtype=x.dtype), row, num_segments=n_nodes)
        inv_sqrt = jax.lax.rsqrt(deg + 1.0)
        xs = x * inv_sqrt[:, None]
        agg = jax.ops.segment_sum(xs[col], row, num_segments=n_nodes) + xs
        out = agg * inv_sqrt[:, None]
        return jnp.matmul(out, W.T)

    def _L2_gnn_ref(node_features, edge_index, edge_type, node_proj_w, node_proj_b, edge_W, edge_b, gru_wih, gru_whh, gru_bih, gru_bhh, out_w, out_b):
        import jax, jax.numpy as jnp
        import numpy as np
        N_NODES = 100000
        N_EDGES = 9375
        H = 128
        T = 8
        L = 2

        def _gru_cell(x, h, wih, whh, bih, bhh):
            gi = x @ wih.T + bih
            gh = h @ whh.T + bhh
            i_r, i_z, i_n = jnp.split(gi, 3, axis=-1)
            h_r, h_z, h_n = jnp.split(gh, 3, axis=-1)
            r = jax.nn.sigmoid(i_r + h_r)
            z = jax.nn.sigmoid(i_z + h_z)
            n = jnp.tanh(i_n + r * h_n)
            return (1.0 - z) * n + z * h
        num_nodes = node_features.shape[0]
        src, dst = (edge_index[0], edge_index[1])
        h = jax.nn.relu(node_features @ node_proj_w.T + node_proj_b)
        for l in range(L):
            trans = jnp.einsum('nh,tdh->tnd', h, edge_W[l])
            msgs = trans[edge_type, src]
            agg = jax.ops.segment_sum(msgs, dst, num_segments=num_nodes)
            h = _gru_cell(agg, h, gru_wih[l], gru_whh[l], gru_bih[l], gru_bhh[l])
            h = jax.nn.relu(h)
        return h @ out_w.T + out_b

    def _L3_gnn_ref(x, edge_index, W0, b0, cw0, cb0, a0, g0, be0, blank0, W1, b1, cw1, cb1, a1, g1, be1, blank1):
        import jax, jax.numpy as jnp
        import numpy as np
        N = 50000
        E = 12500
        D = 128
        MAX_NODES = 4
        EPS = 1e-05

        def sort_conv(x, edge_index, blank, W, b, cw, cb, a):
            n, d = x.shape
            e = edge_index.shape[1]
            src, dst = (edge_index[0], edge_index[1])
            msgs = x[src]
            order = jnp.argsort(dst)
            dst_s = dst[order]
            counts = jax.ops.segment_sum(jnp.ones((e,), jnp.int32), dst, num_segments=n + 1)
            starts = jnp.concatenate([jnp.zeros((1,), jnp.int32), jnp.cumsum(counts)[:-1].astype(jnp.int32)])
            pos = jnp.arange(e, dtype=jnp.int32) - starts[dst_s]
            slot = jnp.where(pos < MAX_NODES, pos, MAX_NODES)
            dense = jnp.zeros((n + 1, MAX_NODES + 1, d), x.dtype).at[dst_s, slot].set(msgs[order])
            mask = jnp.zeros((n + 1, MAX_NODES + 1), bool).at[dst_s, slot].set(True)
            dense, mask = (dense[:, :MAX_NODES], mask[:, :MAX_NODES])
            blank_p = W @ blank + b
            filled = dense + (~mask)[..., None].astype(x.dtype) * blank_p
            srt = jnp.sort(filled, axis=1)
            out = jnp.einsum('nmd,m->nd', srt, cw) + cb
            node_out, blank_new = (out[:-1], out[-1])
            return (a * x + node_out, a * blank + blank_new)

        def batch_norm(h, g, be):
            mu = h.mean(0)
            var = h.var(0)
            return (h - mu) / jnp.sqrt(var + EPS) * g + be
        layers = [(W0, b0, cw0, cb0, a0, g0, be0, blank0), (W1, b1, cw1, cb1, a1, g1, be1, blank1)]
        for W, b, cw, cb, a, g, be, blank in layers:
            h, _ = sort_conv(x, edge_index, blank, W, b, cw, cb, a)
            h = batch_norm(h, g, be)
            x = x + h
        return x
    edge_index = jnp.stack([src, dst])
    batch0 = jnp.zeros((50000,), jnp.int32)
    x = _layernorm(x + _L0_gnn_ref(x, edge_index, edge_attr_128, L0_gnn_u, batch0, L0_gnn_W1a, L0_gnn_b1a, L0_gnn_W1b, L0_gnn_b1b, L0_gnn_W2a, L0_gnn_b2a, L0_gnn_W2b, L0_gnn_b2b), axis=-1)
    x = _layernorm(x + _L1_gnn_ref(x, edge_index, L1_gnn_W), axis=-1)
    x = _layernorm(x + _L2_gnn_ref(x, edge_index, edge_type_8, L2_gnn_node_proj_w, L2_gnn_node_proj_b, L2_gnn_edge_W, L2_gnn_edge_b, L2_gnn_gru_wih, L2_gnn_gru_whh, L2_gnn_gru_bih, L2_gnn_gru_bhh, L2_gnn_out_w, L2_gnn_out_b), axis=-1)
    x = _layernorm(x + _L3_gnn_ref(x, edge_index, L3_gnn_W0, L3_gnn_b0, L3_gnn_cw0, L3_gnn_cb0, L3_gnn_a0, L3_gnn_g0, L3_gnn_be0, L3_gnn_blank0, L3_gnn_W1, L3_gnn_b1, L3_gnn_cw1, L3_gnn_cb1, L3_gnn_a1, L3_gnn_g1, L3_gnn_be1, L3_gnn_blank1), axis=-1)
    return x

_drawn_inputs = setup_inputs


def setup_inputs(seed=0):
    import zlib

    import numpy as np

    out = dict(_drawn_inputs(seed))
    spreads = {'L2_gnn_out_b': (0.0, 0.1),
     'L3_gnn_b0': (0.0, 0.283),
     'L3_gnn_g0': (1.0, 0.2),
     'L3_gnn_be0': (0.0, 0.1),
     'L3_gnn_blank0': (0.0, 0.1),
     'L3_gnn_b1': (0.0, 0.1),
     'L3_gnn_g1': (1.0, 0.2),
     'L3_gnn_be1': (0.0, 0.1),
     'L3_gnn_blank1': (0.0, 0.1)}
    factors = {'edge_attr_128': 2.872,
     'L0_gnn_b1a': 22.782,
     'L0_gnn_b1b': 8.0,
     'L2_gnn_node_proj_b': 5.771,
     'L2_gnn_edge_W': 7.526,
     'L2_gnn_gru_wih': 7.572,
     'L2_gnn_gru_bhh': 3.763}
    for name, (base, spread) in spreads.items():
        noise = np.random.default_rng([zlib.crc32(name.encode()), seed]).standard_normal(out[name].shape)
        drawn = base * np.exp(spread * noise) if base else spread * noise
        out[name] = jnp.asarray(drawn.astype(out[name].dtype))
    for name, factor in factors.items():
        out[name] = (out[name] * factor).astype(out[name].dtype)
    return out
```

```python
from contextlib import ExitStack

import numpy as np
import concourse.bass as bass
from concourse import mybir

F32, BF16, I32 = mybir.dt.float32, mybir.dt.bfloat16, mybir.dt.int32
ALU, ACT = mybir.AluOpType, mybir.ActivationFunctionType
ADD, SUB, MUL, MAX, MIN, EQ = ALU.add, ALU.subtract, ALU.mult, ALU.max, ALU.min, ALU.is_equal

P = 128
N, E, D, HID = 50000, 12500, 128, 256
NTYPE, NLAYER, TOP = 8, 2, 4
J = 4
GR = J * P
NG = -(-N // GR)
NPAD = NG * GR
TAILP = (N - (NG - 1) * GR) // J
EG = -(-E // GR)
EG += EG % 2
EP = EG * GR
ET = EP // P
EFULL = E // P
NPAIR, EPAIR = NG // 2, EG // 2
LO = 256
PADKEY = NPAD - 1
SKIP = 1 << 20
FRONT = 16
ROWLEN = FRONT + EP + FRONT
EPS = 1e-5
NHI = 2 * P * LO
assert N <= NPAD and N % J == 0 and PADKEY >= N and PADKEY < NHI


def pairs(eng, n, body, last=False):
    body(0)
    end = n - 1 if last else n
    if end > 1:
        with eng.Fori(1, end) as i:
            body(i)
    if last:
        body(n - 1)


def ready(i, u, base=0):
    return 2 * i + (base + u + 1)


def first(i):
    return isinstance(i, int) and i == 0


def free(eng, sem, i, base=0, k=2):
    if not first(i):
        landed(eng, sem, k * i + base)


class Swdge:

    def __init__(self, sem):
        self.sem, self.base = sem, 0

    def end(self, total):
        self.base += total


def landed(eng, s, count):
    if isinstance(s, Swdge):
        eng.wait_ge(s.sem, s.base + count)
    else:
        eng.wait_ge(s, count)


def build(nc, a, out):
    ctx = ExitStack()
    with ctx:
        def sb(name, shape, dt=F32):
            return ctx.enter_context(nc.sbuf_tensor(name, shape, dt))

        def sem(name):
            return ctx.enter_context(nc.semaphore(name))

        def dram(name, shape, dt=F32):
            return nc.dram_tensor(name, shape, dt, kind="Internal").ap()

        x1_tab = dram("x1_tab", (NPAD, D))
        x2_tab = dram("x2_tab", (NPAD, D))
        h1_tab = dram("h1_tab", (NPAD, D))
        x3_tab = dram("x3_tab", (NPAD, D))
        raw_rows = dram("raw_rows", (4, EP))
        meta = [dram(f"meta{k}", (EP, 4)) for k in range(2)]
        key_row = [dram(f"key_row{k}", (1, ROWLEN)) for k in range(2)]
        cnt_row = [dram(f"cnt_row{k}", (1, EP)) for k in range(2)]
        inv_row = dram("inv_row", (1, EP))
        type_row = dram("type_row", (1, EP))
        last_row = dram("last_row", (1, EP))
        inv_tab = dram("inv_tab", (NHI, 1))
        slot_tab = dram("slot_tab", (NHI, 1))
        agg0 = dram("agg_t0", (EG, P, 2 * GR))
        agg1 = dram("agg_t1", (EG, P, GR))
        agg2 = dram("agg_t2", (EG, P, GR))
        agg3 = dram("agg_t3", (EG, P, GR))
        x2_c = dram("x2_c", (EG, P, GR))
        h1_c = dram("h1_c", (EG, P, GR))
        x3_c = dram("x3_c", (EG, P, GR))
        x3src_t = dram("x3src_t", (EG, P, GR))
        d1_t = dram("d1_t", (EG, P, GR))
        d2_t = dram("d2_t", (EG, P, GR))
        d1_tab = dram("d1_tab", (EP + 1, D))

        PS = [ctx.enter_context(nc.psum_tensor(f"ps{b}", [P, GR], F32)) for b in range(8)]
        A = [PS[0], PS[1]]
        H = [[PS[2], PS[3]], [PS[4], PS[5]]]
        B = [PS[6], PS[7]]

        ident = sb("ident", [P, P])
        ones = sb("ones", [P, P])
        mhalf = sb("mhalf", [P, GR])
        before = sb("before", [P, P])
        iota_lo = sb("iota_lo", [P, LO])
        pidx = sb("pidx", [P, 2])
        mask = sb("mask", [P, 7 * P])
        scratch_i = sb("scratch_i", [P, 7 * P], I32)
        W1a = sb("W1a", [P, 2, HID])
        W1bT = sb("W1bT", [P, 2, HID])
        W2a = sb("W2a", [P, 3, HID])
        W2b = sb("W2b", [P, 2, D])
        Wf = sb("Wf", [P, 2, HID])
        b0 = sb("b0", [P, 10])
        b2b_bc = sb("b2b_bc", [P, J, D])
        WL1 = sb("WL1", [P, D])
        Wp = sb("Wp", [P, D])
        bp = sb("bp", [P, 1])
        We = sb("We", [P, NLAYER * NTYPE, D])
        Wih = sb("Wih", [P, NLAYER, 3 * D])
        Whh = sb("Whh", [P, NLAYER, 3 * D])
        bih = sb("bih", [P, NLAYER, 3])
        bhh = sb("bhh", [P, NLAYER, 3])
        brz = sb("brz", [P, NLAYER, 3])
        Wo = sb("Wo", [P, D])
        bo_bc = sb("bo_bc", [P, J, D])
        W3 = sb("W3", [P, 2, D])
        v3 = sb("v3", [P, 2, 16])
        f3 = sb("f3", [P, 64])
        C_bc = sb("C_bc", [P, J, D])
        D_bc = sb("D_bc", [P, J, D])

        ef = sb("ef", [P, 7, ET])
        me = sb("me", [P, ET, 4])
        ix = sb("ix", [P, 9, ET], I32)
        inv_e = sb("inv_e", [P, ET])
        IX_SRC, IX_EDGE, IX_DST, IX_DSTW, IX_SDST, IX_SSRC, IX_SSRCW, IX_SLOT = range(8)

        big = sb("big", [P, 16, GR])
        xN = [sb(f"xN{u}", [P, J, D]) for u in range(2)]
        xT = [sb(f"xT{u}", [P, GR]) for u in range(2)]
        rN = [sb(f"rN{u}", [P, J, D]) for u in range(2)]
        yN = [sb(f"yN{u}", [P, J, D]) for u in range(2)]
        zN = [sb(f"zN{u}", [P, J, D]) for u in range(2)]
        xb = [sb(f"xb{u}", [P, J, D]) for u in range(2)]
        hid = [sb(f"hid{u}", [P, 2, GR]) for u in range(2)]
        agg = [sb(f"agg{u}", [P, 2, GR]) for u in range(2)]
        st6 = [sb(f"st6{u}", [P, J, 6]) for u in range(2)]
        mv = [sb(f"mv{u}", [P, J, 2]) for u in range(2)]
        ve = [sb(f"ve{u}", [P, J]) for u in range(2)]
        rs = [sb(f"rs{u}", [P, J]) for u in range(2)]
        islot = [sb(f"islot{u}", [P, 3, J], I32) for u in range(2)]
        krow = [sb(f"krow{u}", [P, GR + 4]) for u in range(2)]

        padv = sb("padv", [P, FRONT + D])
        carry = sb("carry", [P, 2])
        stat3 = sb("stat3", [P, NG * 6])
        winb = [sb(f"win{u}", [P, GR + 4]) for u in range(2)]
        sum3 = [sb(f"sum3{u}", [P, 3]) for u in range(2)]
        sums = sb("sums", [P, EG, 3])
        ginv = [sb(f"ginv{u}", [P, J, 1]) for u in range(2)]
        gate, dve_gate, sp_gate = sem("gate"), sem("dve_gate"), sem("sp_gate")
        gat_a, gat_b, sca_a, sca_b = ([Swdge(sem(f"{n}{u}")) for u in range(2)] for n in ("gather_a", "gather_b", "scatter_a", "scatter_b"))
        sets = [[sem(f"even{n}") for n in range(60)], [sem(f"odd{n}") for n in range(60)]]
        phase = [0]

        class Phase:

            def __init__(self):
                self.taken = 0
                self.own = sets[phase[0] % 2]
                self.other = sets[(phase[0] + 1) % 2] if phase[0] else []
                phase[0] += 1

            def sem(self):
                self.taken += 1
                return self.own[self.taken - 1]

            def sems(self, n):
                return [self.sem() for _ in range(n)]

            def clear_other(self, sp):
                for s in self.other:
                    sp.sem_clear(s)

        def group(tab, g, n=1):
            return tab[bass.ds(g * GR, GR), :].rearrange("(p j) d -> p (j d)", j=J)

        def tail(tab):
            return tab[(NG - 1) * GR:N, :].rearrange("(p j) d -> p (j d)", j=J)

        def plane(tab, g):
            return tab[bass.ds(g, 1), :, :].rearrange("g p c -> (g p) c")

        def row_bc(row, start, n):
            return row[0, bass.ds(start, n)].partition_broadcast(P)

        def flat(t):
            return t[:, :, :].rearrange("p j d -> p (j d)")

        ph = Phase()
        w_in, keys_in, consts, ints, floats, tp, tpe, raw_st, iot, made, wf_p, wf_c, mset, raw_out = ph.sems(14)
        raw_i = big[:, 0:3, 0:P].bitcast(I32)
        raw_h = big[:, 3:7, 0:P].bitcast(I32)
        raw_f = big[:, 8:15, 0:P]
        with nc.Block() as block:

            @block.sync
            def _(sp):
                sp.wait_ge(mset, 1)
                for f, name in enumerate(("src", "dst", "edge_type_8")):
                    sp.dma_start(raw_i[0:EFULL, f, :], a[name][0:EFULL * P].rearrange("(t p) -> t p", p=P)).then_inc(keys_in, 16)
                    sp.dma_start(raw_i[EFULL:EFULL + 1, f, 0:E - EFULL * P],
                                 a[name][EFULL * P:E].rearrange("(o p) -> o p", o=1)).then_inc(keys_in, 16)
                loads = [
                    (W1a, a["W1a"].rearrange("(c p) h -> p c h", p=P)), (W1bT, a["W1bT"].rearrange("(c p) h -> p c h", p=P)),
                    (W2a, a["W2a"].rearrange("(c p) h -> p c h", p=P)), (W2b, a["W2b"].rearrange("(c p) h -> p c h", p=P)),
                    (WL1, a["WL1"]), (Wp, a["Wp"]), (We, a["We"].rearrange("t h d -> h t d")),
                    (Wih, a["Wih"].rearrange("l h d -> h l d")), (Whh, a["Whh"].rearrange("l h d -> h l d")),
                    (Wo, a["Wo"]), (W3, a["W3"].rearrange("l h d -> h l d"))]
                for t, src in loads:
                    sp.dma_start(t[:], src).then_inc(w_in, 16)
                sp.wait_ge(raw_st, 1)
                for r, f in enumerate((3, 5, 0, 1)):
                    sp.dma_start(raw_rows[r, :].rearrange("(t p) -> t p", p=P), raw_f[0:ET, f, :]).then_inc(raw_out, 16)
                sp.wait_ge(w_in, 16 * len(loads))
                sp.wait_ge(raw_out, 16 * 4)

            @block.scalar
            def _(act):
                n = [0]

                def load(t, src):
                    act.dma_start(t, src, allow_slow_non_contiguous=True).then_inc(keys_in, 16)
                    n[0] += 1

                for o, name in ((0, "b1a"), (2, "b1b"), (4, "b2a")):
                    load(b0[:, o:o + 2], a[name].rearrange("(c p) -> p c", p=P))
                load(bp[:, :], a["bp"].rearrange("(c p) -> p c", p=P))
                load(bih[:, :, :], a["bih"].rearrange("l (g p) -> p l g", p=P))
                load(bhh[:, :, :], a["bhh"].rearrange("l (g p) -> p l g", p=P))
                for j in range(J):
                    load(b2b_bc[:, j, :], a["b2b"].partition_broadcast(P))
                    load(bo_bc[:, j, :], a["bo"].partition_broadcast(P))
                for l in range(2):
                    for c, name in enumerate(("b", "g", "be", "blank")):
                        load(v3[:, l, c:c + 1], a[f"{name}{l}"].rearrange("(c p) -> p c", p=P))
                    load(v3[:, l, 4:5], a[f"a{l}"].partition_broadcast(P))
                    load(v3[:, l, 5:6], a[f"cb{l}"].partition_broadcast(P))
                    load(v3[:, l, 6:10], a[f"cw{l}"].partition_broadcast(P))
                act.wait_ge(keys_in, 16 * (6 + n[0]))
                act.sem_inc(consts, 1)
                act.wait_ge(wf_p, 1)
                nc.scalar.activation(Wf[:, 0, :], H[0][0][:, 0:HID], ACT.Copy)
                nc.scalar.activation(Wf[:, 1, :], H[0][1][:, 0:HID], ACT.Copy).then_inc(wf_c, 1)
                for f in range(7):
                    act.wait_ge(tp, f + 1)
                    nc.scalar.activation(ef[:, f, :], PS[f % 2][:, 0:ET], ACT.Copy).then_inc(tpe, 1)

            @block.gpsimd
            def _(pool):
                nc.gpsimd.iota(scratch_i[:, 0:LO], [[1, LO]], base=0, channel_multiplier=0).then_inc(iot, 1)
                nc.gpsimd.iota(scratch_i[:, LO:LO + 2], [[P, 2]], base=0, channel_multiplier=1).then_inc(iot, 1)
                pool.wait_ge(iot, 2)
                nc.gpsimd.tensor_copy(iota_lo[:, :], scratch_i[:, 0:LO])
                nc.gpsimd.tensor_copy(pidx[:, :], scratch_i[:, LO:LO + 2]).then_inc(iot, 1)
                nc.gpsimd.memset(mhalf[:, :], -0.5)
                nc.gpsimd.memset(ident[:, :], 0.0)
                nc.gpsimd.memset(before[:, :], 1.0)
                nc.gpsimd.memset(mask[:, :], 1.0)
                nc.gpsimd.memset(ones[:, :], 1.0).then_inc(iot, 1)
                pool.wait_ge(iot, 4)
                nc.gpsimd.affine_select(out=ident[:, :], in_=ident[:, :], compare_op=ALU.not_equal, fill=1.0, base=0,
                                        pattern=[[-1, P]], channel_multiplier=1)
                nc.gpsimd.affine_select(out=before[:, :], in_=before[:, :], compare_op=ALU.is_gt, fill=0.0, base=0,
                                        pattern=[[1, P]], channel_multiplier=-1)
                nc.gpsimd.affine_select(out=mask[:, :], in_=mask[:, :], compare_op=ALU.is_gt, fill=0.0, base=3 * P,
                                        pattern=[[-1, 7 * P]], channel_multiplier=1).then_inc(made, 1)
                nc.gpsimd.iota(scratch_i[:, 0:ET], [[P, ET]], base=0, channel_multiplier=1).then_inc(iot, 1)
                pool.wait_ge(iot, 5)
                nc.gpsimd.tensor_copy(me[:, :, 3], scratch_i[:, 0:ET]).then_inc(iot, 1)
                pool.wait_ge(iot, 6)

            @block.vector
            def _(dve):
                nc.vector.memset(raw_i[:, :, :], PADKEY).then_inc(mset, 1)
                dve.wait_ge(keys_in, 16 * 6)
                dve.wait_ge(consts, 1)
                for k in range(2):
                    nc.vector.tensor_scalar(raw_h[:, 2 * k, :], raw_i[:, k, :], 8, None, ALU.arith_shift_right)
                    nc.vector.tensor_scalar(raw_h[:, 2 * k + 1, :], raw_i[:, k, :], LO - 1, None, ALU.bitwise_and).then_inc(ints, 1)
                dve.wait_ge(ints, 2)
                nc.vector.tensor_copy(raw_f[:, 0:3, :], raw_i[:, :, :])
                nc.vector.tensor_copy(raw_f[:, 3:7, :], raw_h[:, :, :]).then_inc(raw_st, 1)
                nc.vector.tensor_tensor(brz[:, :, :], bih[:, :, :], bhh[:, :, :], ADD).then_inc(floats, 1)
                dve.wait_ge(wf_p, 1)
                nc.vector.tensor_tensor(b0[:, 6:8], b0[:, 4:6], B[0][:, 0:2], ADD).then_inc(floats, 1)
                dve.wait_ge(tpe, 3)
                nc.vector.tensor_copy(me[:, :, 0:3].rearrange("p t f -> p f t"), ef[:, 0:3, :]).then_inc(floats, 1)
                dve.wait_ge(floats, 3)

            @block.tensor
            def _(pe):
                pe.wait_ge(made, 1)
                pe.wait_ge(raw_st, 1)
                for f in range(7):
                    if f >= 2:
                        pe.wait_ge(tpe, f - 1)
                    if f == 0:
                        pe.wait_ge(consts, 1)
                        pe.wait_ge(w_in, 16 * 11)
                        for c in range(2):
                            for q in range(2):
                                nc.tensor.matmul(H[0][c][:, 0:HID], W1bT[:, q, c * P:(c + 1) * P], W2a[:, 1 + q, :],
                                                 start=(q == 0), stop=(q == 1))
                        for c in range(2):
                            for q in range(2):
                                last = nc.tensor.matmul(B[0][:, c:c + 1], W2a[:, 1 + q, c * P:(c + 1) * P], b0[:, 2 + q:3 + q],
                                                        start=(q == 0), stop=(q == 1))
                        last.then_inc(wf_p, 1)
                    nc.tensor.transpose(PS[f % 2][:, 0:ET], raw_f[0:ET, f, :], ident[0:ET, 0:ET]).then_inc(tp, 1)

        ph = Phase()
        hot, hist, cum, tot, tots, off, offs, start_, tabs, tab_st, inv1, slot1, slot2, jg = ph.sems(14)
        one_lo = [big[:, 2 * k, :].bitcast(BF16).rearrange("p (j c) -> p j c", j=J) for k in range(2)]
        one_hi = [big[:, 2 * k + 1, :].bitcast(BF16).rearrange("p (j c) -> p j c", j=J) for k in range(2)]
        R = big[:, 4:6, :].rearrange("p k (h c) -> p k h c", h=2)
        cumul = big[:, 6:8, :].rearrange("p k (h c) -> p k h c", h=2)
        count = big[:, 8:10, :].rearrange("p k (h c) -> p k h c", h=2)
        inv_w = big[:, 10, :].rearrange("p (h c) -> p h c", h=2)
        slot_w = big[:, 11, :].rearrange("p (h c) -> p h c", h=2)
        has_w = big[:, 12, :].rearrange("p (h c) -> p h c", h=2)
        rowtot = f3[:, 0:4]
        lowtot = f3[:, 4:8]
        offset = f3[:, 8:12]

        def one_hots(dve, i, k, done):
            for j in range(J):
                nc.vector.tensor_scalar(one_hi[k][:, j, :], iota_lo[:, :], ef[:, 3 + 2 * k, bass.ds(J * i + j, 1)], None, EQ)
                last = nc.vector.tensor_scalar(one_lo[k][:, j, :], iota_lo[:, :], ef[:, 4 + 2 * k, bass.ds(J * i + j, 1)], None, EQ)
            last.then_inc(done, 1)

        with nc.Block() as block:

            @block.sync
            def _(sp):
                ph.clear_other(sp)
                sp.wait_ge(tabs, 1)
                sp.dma_start(inv_tab.rearrange("(h p c) o -> p h (c o)", h=2, p=P), inv_w).then_inc(tab_st, 16)
                sp.wait_ge(tabs, 2)
                sp.dma_start(slot_tab.rearrange("(h p c) o -> p h (c o)", h=2, p=P), slot_w).then_inc(tab_st, 16)
                sp.wait_ge(tab_st, 32)

            @block.vector
            def _(dve):
                def body(i):
                    for k in range(2):
                        free(dve, hist, i)
                        one_hots(dve, i, k, hot)

                pairs(dve, EG, body, last=True)
                dve.wait_ge(hist, 2 * EG)
                for k in range(2):
                    for h in range(2):
                        nc.vector.tensor_copy(count[:, k, h, :], PS[2 * k + h][:, 0:LO])
                        last = nc.vector.tensor_tensor_scan(cumul[:, k, h, :], mask[:, 0:LO], PS[2 * k + h][:, 0:LO], 0.0, MUL, ADD)
                last.then_inc(cum, 1)
                dve.wait_ge(cum, 1)
                for k in range(2):
                    nc.vector.tensor_copy(rowtot[:, 2 * k:2 * k + 2], cumul[:, k, :, LO - 1])
                    nc.vector.tensor_copy(lowtot[:, 2 * k + 1:2 * k + 2], cumul[:, k, 0, LO - 1:LO])
                    last = nc.vector.memset(lowtot[:, 2 * k:2 * k + 1], 0.0)
                last.then_inc(tot, 1)
                dve.wait_ge(off, 1)
                nc.vector.tensor_copy(offset, B[0][:, 0:4]).then_inc(offs, 1)
                dve.wait_ge(offs, 1)
                for k in range(2):
                    for h in range(2):
                        last = nc.vector.scalar_tensor_tensor(R[:, k, h, :], cumul[:, k, h, :], offset[:, 2 * k + h:2 * k + h + 1],
                                                              count[:, k, h, :], ADD, SUB)
                last.then_inc(start_, 1)
                nc.vector.tensor_scalar(has_w, count[:, 1, :, :], 0.0, None, ALU.is_gt).then_inc(slot1, 1)
                dve.wait_ge(start_, 1)
                nc.vector.tensor_scalar(slot_w, R[:, 1, :, :], -1.0, -1.0, MUL, ADD).then_inc(slot1, 1)
                dve.wait_ge(slot1, 2)
                nc.vector.tensor_tensor(slot_w, slot_w, has_w, MUL).then_inc(slot2, 1)
                dve.wait_ge(slot2, 1)
                dve.wait_ge(tabs, 1)
                nc.vector.tensor_scalar(slot_w, slot_w, float(EP), None, ADD).then_inc(tabs, 1)

            @block.gpsimd
            def _(pool):
                pool.wait_ge(cum, 1)
                nc.gpsimd.tensor_scalar(inv_w, count[:, 0, :, :], 1.0, None, ADD).then_inc(inv1, 1)
                pool.wait_ge(inv1, 1)
                nc.gpsimd.tensor_tensor(inv_w, inv_w, mhalf[:, :].rearrange("p (h c) -> p h c", h=2), ALU.pow).then_inc(tabs, 1)

            @block.tensor
            def _(pe):
                def body(i):
                    for k in range(2):
                        pe.wait_ge(hot, 2 * i + k + 1)
                        for j in range(J):
                            for h in range(2):
                                last = nc.tensor.matmul(PS[2 * k + h][:, 0:LO], one_hi[k][:, j, h * P:(h + 1) * P], one_lo[k][:, j, :],
                                                        start=(first(i) and j == 0),
                                                        stop=(isinstance(i, int) and i == EG - 1 and j == J - 1))
                        last.then_inc(hist, 1)

                pairs(pe, EG, body, last=True)
                pe.wait_ge(tot, 1)
                nc.tensor.matmul(B[0][:, 0:4], before[:, :], rowtot, start=True, stop=False)
                nc.tensor.matmul(B[0][:, 0:4], ones[:, :], lowtot, start=False, stop=True).then_inc(off, 1)

        ph = Phase()
        hot, hotT, looked, counted, based, eqd, radd, ranked, base_w = ph.sems(9)
        stored = sca_a
        rows_in = ph.sems(2)
        hi_bc = [krow[k][:, 0:GR] for k in range(2)]
        key_bc = [xT[k] for k in range(2)]
        hotTs = [hid[k] for k in range(2)]
        base = [f3[:, 16 + 4 * k:20 + 4 * k] for k in range(2)]
        within = [f3[:, 24 + 4 * k:28 + 4 * k] for k in range(2)]
        rankf = [f3[:, 32 + 4 * k:36 + 4 * k] for k in range(2)]
        mslot = [st6[k][:, :, 0:4] for k in range(2)]
        junk_eq = [big[:, 10 + 3 * k:13 + 3 * k, :].rearrange("p a b -> p (a b)") for k in range(2)]
        junk_lo = [[flat(t[j // 2])[:, (j % 2) * LO:(j % 2 + 1) * LO] for j in range(J)] for t in (yN, zN)]
        with nc.Block() as block:

            @block.sync
            def _(sp):
                ph.clear_other(sp)

                def body(i):
                    for k in range(2):
                        free(sp, eqd, i)
                        free(sp, hotT, i)
                        sp.dma_start(hi_bc[k], raw_rows[k, bass.ds(i * GR, GR)].partition_broadcast(P)).then_inc(rows_in[k], 16)
                        sp.dma_start(key_bc[k][:, :], raw_rows[2 + k, bass.ds(i * GR, GR)].partition_broadcast(P)).then_inc(rows_in[k], 16)

                pairs(sp, EG, body)

            @block.vector
            def _(dve):
                def body(i):
                    for k in range(2):
                        free(dve, counted, i)
                        one_hots(dve, i, k, hot)
                    for k in range(2):
                        dve.wait_ge(rows_in[k], 32 * i + 32)
                        free(dve, looked, i)
                        for h in range(2):
                            last = nc.vector.tensor_scalar(hotTs[k][:, h, :], hi_bc[k], pidx[:, h:h + 1], None, EQ)
                        last.then_inc(hotT, 1)
                    for k in range(2):
                        for j in range(J):
                            w = (j + 1) * P
                            last = nc.vector.scalar_tensor_tensor(junk_eq[k][:, j * w // 2:j * w // 2 + w], key_bc[k][:, 0:w], ef[:, k, bass.ds(J * i + j, 1)],
                                                                  mask[:, (3 - j) * P:(3 - j) * P + w], EQ, MUL,
                                                                  accum_out=within[k][:, j:j + 1])
                        last.then_inc(eqd, 1)
                    for k in range(2):
                        dve.wait_ge(looked, 2 * i + k + 1)
                        free(dve, ranked, i)
                        for j in range(J):
                            last = nc.vector.scalar_tensor_tensor(junk_lo[k][j], PS[2 * k + j // 2][:, (j % 2) * LO:(j % 2 + 1) * LO], 1.0,
                                                                  one_lo[k][:, j, :], MUL, MUL, accum_out=base[k][:, j:j + 1])
                        last.then_inc(based, 1)
                        dve.wait_ge(counted, 2 * i + k + 1)
                        nc.vector.tensor_tensor(R[:, k, :, :], R[:, k, :, :], PS[4 + k][:, :].rearrange("p (h c) -> p h c", h=2), ADD).then_inc(radd, 1)
                    for k in range(2):
                        dve.wait_ge(based, 2 * i + k + 1)
                        dve.wait_ge(eqd, 2 * i + k + 1)
                        nc.vector.tensor_tensor(rankf[k], base[k], within[k], ADD).then_inc(base_w, 1)
                    for k in range(2):
                        dve.wait_ge(base_w, 2 * i + k + 1)
                        free(dve, stored[k], i, k=16 * J)
                        nc.vector.tensor_scalar(islot[k][:, 0, :], rankf[k], -1.0, float(EP - 1), MUL, ADD)
                        nc.vector.tensor_copy(mslot[k], me[:, bass.ds(J * i, J), :]).then_inc(ranked, 1)

                pairs(dve, EG, body)

            @block.tensor
            def _(pe):
                def body(i):
                    for k in range(2):
                        pe.wait_ge(hotT, 2 * i + k + 1)
                        pe.wait_ge(hot, 2 * i + k + 1)
                        free(pe, radd, i)
                        for j in range(J):
                            for h in range(2):
                                last = nc.tensor.matmul(PS[2 * k + j // 2][:, (j % 2) * LO:(j % 2 + 1) * LO],
                                                        hotTs[k][:, h, j * P:(j + 1) * P], R[:, k, h, :], start=(h == 0), stop=(h == 1))
                        last.then_inc(looked, 1)
                        for h in range(2):
                            for j in range(J):
                                last = nc.tensor.matmul(PS[4 + k][:, h * LO:(h + 1) * LO], one_hi[k][:, j, h * P:(h + 1) * P],
                                                        one_lo[k][:, j, :], start=(j == 0), stop=(j == J - 1))
                        last.then_inc(counted, 1)

                pairs(pe, EG, body)

            @block.gpsimd
            def _(pool):
                def body(i):
                    for k in range(2):
                        pool.wait_ge(ranked, 2 * i + k + 1)
                        pool.sem_inc(gate, 1)
                        for j in range(J):
                            nc.gpsimd.indirect_dma_start(meta[k], bass.IndirectOffsetOnAxis(ap=islot[k][:, 0, j:j + 1], axis=0),
                                                         mslot[k][:, j, :], None).then_inc(stored[k].sem, 16)

                pairs(pool, EG, body)
                for k in range(2):
                    landed(pool, stored[k], EG * J * 16)

        for s in stored:
            s.end(16 * J * EG)

        ph = Phase()
        (m_in, row_c, row_st, lin_in, same_d, cnt_d, cnt_st, nxt_in, cnt_in, edge_d, inv_d, fix, tpd, tpc, idx_a, idx_b,
         row_st2, pads, zrow, ends) = ph.sems(20)
        meta_r = [big[0:ET, 0, :], big[0:ET, 1, :]]
        fields = lambda k, f: meta_r[k].rearrange("t (p f) -> t f p", f=4)[:, f, :]
        keyc = big[0:ET, 2, :].rearrange("t (k p) -> t k p", p=P)
        aux = big[0:ET, 3, :].rearrange("t (k p) -> t k p", p=P)
        scat = big[0:ET, 4, :].rearrange("t (k p) -> t k p", p=P)
        other = big[0:ET, 5, :].rearrange("t (k p) -> t k p", p=P)
        HALF = EP // 2
        half_ctx = nc.sbuf_tensor("line_buf", [1, 2 * HALF + 8], F32)
        line_buf = half_ctx.__enter__()
        line = line_buf[0:1, 0:HALF + 1]
        sameline = line_buf[0:1, HALF + 4:2 * HALF + 4]
        cntline = line_buf[0:1, 0:HALF]
        KD, KS = 1, 0
        with nc.Block() as block:

            @block.sync
            def _(sp):
                ph.clear_other(sp)
                for k in range(2):
                    sp.dma_start(meta_r[k], meta[k].rearrange("(t p) f -> t (p f)", p=P)).then_inc(m_in, 16)
                sp.wait_ge(row_c, 1)
                for k, f in ((KD, 0), (KS, 1)):
                    sp.dma_start(key_row[k][0, FRONT:FRONT + EP].rearrange("(t p) -> t p", p=P), keyc[:, f, :]).then_inc(row_st, 16)
                sp.dma_start(type_row[0, :].rearrange("(t p) -> t p", p=P), keyc[:, 2, :]).then_inc(row_st, 16)
                sp.wait_ge(pads, 1)
                for k in range(2):
                    sp.dma_start(key_row[k][0:1, 0:FRONT], padv[0:1, 0:FRONT]).then_inc(row_st, 16)
                    sp.dma_start(key_row[k][0:1, FRONT + EP:ROWLEN], padv[0:1, 0:FRONT]).then_inc(row_st, 16)
                sp.dma_start(d1_tab[EP:EP + 1, :], padv[0:1, FRONT:FRONT + D]).then_inc(row_st, 16)
                sp.wait_ge(row_st, 16 * 8)
                for n, k in enumerate((KD, KS)):
                    sp.dma_start(aux[:, n, :], key_row[k][0, FRONT + 1:FRONT + 1 + EP].rearrange("(t p) -> t p", p=P)).then_inc(nxt_in, 16)
                for n, k in enumerate((KD, KS)):
                    for c in range(2):
                        if n or c:
                            sp.wait_ge(cnt_st, 16 * (2 * n + c))
                            sp.wait_ge(zrow, 2 * n + c + 1)
                        at = FRONT - 1 + c * HALF
                        sp.dma_start(line, key_row[k][0:1, at:at + HALF + 1]).then_inc(lin_in, 16)
                        sp.wait_ge(cnt_d, 2 * n + c + 1)
                        sp.dma_start(cnt_row[k][0:1, c * HALF:(c + 1) * HALF], cntline).then_inc(cnt_st, 16)
                sp.wait_ge(cnt_st, 64)
                sp.dma_start(aux[:, 3, :], cnt_row[KD][0, :].rearrange("(t p) -> t p", p=P)).then_inc(cnt_in, 16)
                sp.dma_start(scat[:, 2, :], cnt_row[KS][0, :].rearrange("(t p) -> t p", p=P)).then_inc(cnt_in, 16)
                sp.wait_ge(inv_d, 1)
                sp.dma_start(inv_row[0, :].rearrange("(t p) -> t p", p=P), aux[:, 3, :]).then_inc(row_st2, 16)
                sp.wait_ge(edge_d, 1)
                sp.dma_start(last_row[0, :].rearrange("(t p) -> t p", p=P), keyc[:, 3, :]).then_inc(row_st2, 16)
                sp.wait_ge(row_st2, 32)

            @block.vector
            def _(dve):
                nc.vector.memset(padv[:, 0:FRONT], -1.0)
                nc.vector.memset(padv[:, FRONT:], 0.0).then_inc(pads, 1)
                dve.wait_ge(m_in, 32)
                nc.vector.tensor_copy(keyc[:, 0, :], fields(KD, 1))
                nc.vector.tensor_copy(keyc[:, 1, :], fields(KS, 0))
                nc.vector.tensor_copy(keyc[:, 2, :], fields(KD, 2)).then_inc(row_c, 1)
                nc.vector.tensor_copy(scat[:, 3, :], fields(KD, 3))
                nc.vector.tensor_copy(other[:, 0, :], fields(KD, 0))
                nc.vector.tensor_copy(other[:, 1, :], fields(KS, 1)).then_inc(fix, 1)
                dve.wait_ge(nxt_in, 32)
                dve.wait_ge(row_c, 1)
                nc.vector.tensor_tensor(aux[:, 0, :], keyc[:, 0, :], aux[:, 0, :], ALU.not_equal).then_inc(ends, 1)
                dve.wait_ge(ends, 1)
                nc.vector.scalar_tensor_tensor(keyc[:, 3, :], keyc[:, 0, :], float(N), aux[:, 0, :], ALU.is_lt, MUL)
                nc.vector.tensor_tensor(aux[:, 2, :], keyc[:, 1, :], aux[:, 1, :], ALU.not_equal).then_inc(edge_d, 1)
                dve.wait_ge(edge_d, 1)
                nc.vector.tensor_scalar(scat[:, 0, :], keyc[:, 3, :], -float(SKIP), float(SKIP), MUL, ADD)
                nc.vector.tensor_scalar(scat[:, 1, :], aux[:, 2, :], -float(SKIP), float(SKIP), MUL, ADD).then_inc(idx_a, 1)
                dve.wait_ge(idx_a, 1)
                nc.vector.tensor_tensor(scat[:, 0, :], scat[:, 0, :], keyc[:, 0, :], ADD)
                nc.vector.tensor_tensor(scat[:, 1, :], scat[:, 1, :], keyc[:, 1, :], ADD).then_inc(idx_a, 1)
                dve.wait_ge(idx_a, 2)
                dve.sem_inc(fix, 1)
                nc.vector.memset(carry[:, :], 0.0).then_inc(zrow, 1)
                for n in range(4):
                    dve.wait_ge(lin_in, 16 * (n + 1))
                    nc.vector.tensor_tensor(sameline, line_buf[0:1, 1:HALF + 1], line_buf[0:1, 0:HALF], EQ).then_inc(same_d, 1)
                    dve.wait_ge(same_d, n + 1)
                    dve.wait_ge(zrow, n + 1)
                    nc.vector.tensor_tensor_scan(cntline, sameline, ones[0:1, 0:1].broadcast_to([1, HALF]), carry[0:1, 0:1], MUL, ADD).then_inc(cnt_d, 1)
                    dve.wait_ge(cnt_d, n + 1)
                    nc.vector.tensor_copy(carry[0:1, 0:1], cntline[:, HALF - 1:HALF]).then_inc(zrow, 1)
                dve.wait_ge(cnt_in, 32)
                nc.vector.reciprocal(aux[:, 3, :], aux[:, 3, :]).then_inc(inv_d, 1)
                dve.sem_inc(fix, 1)
                for n, (dst_ix, bound) in enumerate(((IX_SRC, N - 1), (IX_DST, N - 1), (IX_EDGE, E - 1), (IX_DSTW, None),
                                                     (IX_SDST, N - 1), (IX_SSRC, N - 1), (IX_SSRCW, None))):
                    dve.wait_ge(tpd, n + 1)
                    if bound is None:
                        last = nc.vector.tensor_copy(ix[:, dst_ix, :], PS[n % 2][:, 0:ET])
                    else:
                        last = nc.vector.tensor_scalar(ix[:, dst_ix, :], PS[n % 2][:, 0:ET], float(bound), None, MIN)
                    last.then_inc(tpc, 1)
                dve.wait_ge(tpd, 8)
                nc.vector.tensor_scalar(inv_e[:, :], PS[1][:, 0:ET], 1.0, None, ADD).then_inc(tpc, 1)

            @block.gpsimd
            def _(pool):
                pool.wait_ge(tpc, 8)
                nc.gpsimd.tensor_tensor(inv_e[:, :], inv_e[:, :], mhalf[:, 0:ET], ALU.pow).then_inc(idx_b, 1)
                pool.wait_ge(idx_b, 1)

            @block.tensor
            def _(pe):
                pe.wait_ge(fix, 2)
                srcs = (other[:, 0, :], keyc[:, 0, :], scat[:, 3, :], scat[:, 0, :], other[:, 1, :], keyc[:, 1, :], scat[:, 1, :], scat[:, 2, :])
                for n, src in enumerate(srcs):
                    if n >= 2:
                        pe.wait_ge(tpc, n - 1)
                    if n == 7:
                        pe.wait_ge(cnt_in, 32)
                    nc.tensor.transpose(PS[n % 2][:, 0:ET], src, ident[0:ET, 0:ET]).then_inc(tpd, 1)

        half_ctx.__exit__(None, None, None)
        def elu_steps(dve, i, src, bias, acts, t, tdone, done):
            for u in range(2):
                dve.wait_ge(acts, ready(i, u))
                nc.vector.tensor_scalar(t[u], t[u], 1.0, -1.0, MIN, ADD).then_inc(tdone, 1)
            for u in range(2):
                dve.wait_ge(tdone, ready(i, u))
                for h in range(2):
                    last = nc.vector.scalar_tensor_tensor(t[u][:, h, :], src[u][h][:, :], bias[h], t[u][:, h, :], ADD, MAX)
                last.then_inc(done, 1)

        ph = Phase()
        ixd, tpd, cpd, hidd, expd, tmin, elud, samed, scand, scaled = ph.sems(10)
        gx, ge = gat_a, gat_b
        kin, iin, aout = (ph.sems(2) for _ in range(3))
        eaT = [flat(zN[u]) for u in range(2)]
        inv_bc = [flat(rN[u]) for u in range(2)]
        same = [flat(xb[u]) for u in range(2)]
        mean = [big[:, 2 * u:2 * u + 2, :] for u in range(2)]
        hid3 = [hid[u][:, :, :] for u in range(2)]
        with nc.Block() as block:

            @block.sync
            def _(sp):
                ph.clear_other(sp)

                def body(i):
                    for u in range(2):
                        free(sp, samed, i)
                        free(sp, scaled, i)
                        g = 2 * i + u
                        sp.dma_start(krow[u][:, 0:GR + 1], row_bc(key_row[1], g * GR + FRONT - 1, GR + 1)).then_inc(kin[u], 16)
                        sp.dma_start(inv_bc[u], row_bc(inv_row, g * GR, GR)).then_inc(iin[u], 16)
                    for u in range(2):
                        sp.wait_ge(scaled, ready(i, u))
                        sp.dma_start(plane(agg0, 2 * i + u), mean[u].rearrange("p h c -> p (h c)")).then_inc(aout[u], 16)

                pairs(sp, EPAIR, body)
                for u in range(2):
                    sp.wait_ge(aout[u], 16 * EPAIR)

            @block.gpsimd
            def _(pool):
                def body(i):
                    for u in range(2):
                        free(pool, gx[u], i, k=16 * J)
                        free(pool, ge[u], i, k=16 * J)
                        free(pool, tpd, i)
                        pool.sem_inc(gate, 1)
                        for n, which in enumerate((IX_SRC, IX_EDGE)):
                            last = nc.gpsimd.tensor_copy(islot[u][:, n, :], ix[:, which, bass.ds((2 * i + u) * J, J)])
                        last.then_inc(ixd, 1)
                        pool.wait_ge(ixd, ready(i, u))
                        pool.sem_inc(gate, 1)
                        for j in range(J):
                            nc.gpsimd.indirect_dma_start(xN[u][:, j, :], None, a["x"],
                                                         bass.IndirectOffsetOnAxis(ap=islot[u][:, 0, j:j + 1], axis=0)).then_inc(gx[u].sem, 16)
                            nc.gpsimd.indirect_dma_start(yN[u][:, j, :], None, a["edge_attr"],
                                                         bass.IndirectOffsetOnAxis(ap=islot[u][:, 1, j:j + 1], axis=0)).then_inc(ge[u].sem, 16)

                pairs(pool, EPAIR, body)

            @block.tensor
            def _(pe):
                def body(i):
                    for u in range(2):
                        landed(pe, gx[u], 16 * J * i + 16 * J)
                        landed(pe, ge[u], 16 * J * i + 16 * J)
                        free(pe, cpd, i)
                        for j in range(J):
                            nc.tensor.transpose(A[u][:, j * P:(j + 1) * P], xN[u][:, j, :], ident[:, :])
                            last = nc.tensor.transpose(B[u][:, j * P:(j + 1) * P], yN[u][:, j, :], ident[:, :])
                        last.then_inc(tpd, 1)
                    for u in range(2):
                        pe.wait_ge(cpd, ready(i, u))
                        free(pe, elud, i)
                        for h in range(2):
                            nc.tensor.matmul(H[u][h][:, :], W1a[:, 0, h * P:(h + 1) * P], xT[u][:, :], start=True, stop=False)
                            last = nc.tensor.matmul(H[u][h][:, :], W1a[:, 1, h * P:(h + 1) * P], eaT[u], start=False, stop=True)
                        last.then_inc(hidd, 1)

                pairs(pe, EPAIR, body)

            @block.scalar
            def _(act):
                def body(i):
                    for u in range(2):
                        act.wait_ge(tpd, ready(i, u))
                        free(act, hidd, i)
                        nc.scalar.activation(xT[u][:, :], A[u][:, :], ACT.Copy)
                        nc.scalar.activation(eaT[u], B[u][:, :], ACT.Copy).then_inc(cpd, 1)
                    for u in range(2):
                        act.wait_ge(hidd, ready(i, u))
                        free(act, scand, i, 1)
                        for h in range(2):
                            last = nc.scalar.activation(hid[u][:, h, :], H[u][h][:, :], ACT.Exp, bias=b0[:, h:h + 1])
                        last.then_inc(expd, 1)

                pairs(act, EPAIR, body)

            @block.vector
            def _(dve):
                nc.vector.memset(agg[1][:, :, :], 0.0).then_inc(scand, 1)

                def body(i):
                    for u in range(2):
                        dve.wait_ge(kin[u], 16 * i + 16)
                        nc.vector.tensor_tensor(same[u], krow[u][:, 1:GR + 1], krow[u][:, 0:GR], EQ).then_inc(samed, 1)
                    elu_steps(dve, i, H, [b0[:, h:h + 1] for h in range(2)], expd, hid3, tmin, elud)
                    for u in range(2):
                        dve.wait_ge(samed, ready(i, u))
                        dve.wait_ge(elud, ready(i, u))
                        dve.wait_ge(scand, ready(i, u))
                        for h in range(2):
                            last = nc.vector.tensor_tensor_scan(agg[u][:, h, :], same[u], hid[u][:, h, :],
                                                                agg[1 - u][:, h, GR - 1:GR], MUL, ADD)
                        last.then_inc(scand, 1)
                    for u in range(2):
                        dve.wait_ge(scand, ready(i, u, 1))
                        dve.wait_ge(iin[u], 16 * i + 16)
                        free(dve, aout[u], i, k=16)
                        for h in range(2):
                            last = nc.vector.tensor_tensor(mean[u][:, h, :], agg[u][:, h, :], inv_bc[u], MUL)
                        last.then_inc(scaled, 1)

                pairs(dve, EPAIR, body)

        for s in (*gx, *ge):
            s.end(16 * J * EPAIR)

        class Norm:

            def __init__(self, ph, r, y):
                self.r, self.y = r, y
                self.stats, self.moments, self.eps, self.rstd, self.done = ph.sems(5)

            def moments_steps(self, dve, i, rdone):
                for u in range(2):
                    dve.wait_ge(rdone, ready(i, u))
                    for j in range(J):
                        last = nc.vector.bn_stats(st6[u][:, j, :], self.r[u][:, j, :])
                    last.then_inc(self.stats, 1)
                for u in range(2):
                    dve.wait_ge(self.stats, ready(i, u))
                    free(dve, self.done, i)
                    dve.sem_inc(dve_gate, 1)
                    for j in range(J):
                        last = nc.vector.bn_aggr(mv[u][:, j, :], st6[u][:, j, :])
                    last.then_inc(self.moments, 1)

            def rstd_steps(self, pool, i):
                for u in range(2):
                    pool.wait_ge(self.moments, ready(i, u))
                    pool.sem_inc(gate, 1)
                    nc.gpsimd.tensor_scalar(ve[u][:, :], mv[u][:, :, 1], EPS, None, ADD).then_inc(self.eps, 1)
                for u in range(2):
                    pool.wait_ge(self.eps, ready(i, u))
                    nc.gpsimd.tensor_tensor(rs[u][:, :], ve[u][:, :], mhalf[:, 0:J], ALU.pow).then_inc(self.rstd, 1)

            def scale_steps(self, dve, i, out_free=None):
                for u in range(2):
                    dve.wait_ge(self.rstd, ready(i, u))
                    if out_free:
                        out_free(dve, i, u)
                    for j in range(J):
                        last = nc.vector.tensor_scalar(self.y[u][:, j, :], self.r[u][:, j, :], mv[u][:, j, 0:1], rs[u][:, j:j + 1], SUB, MUL)
                    last.then_inc(self.done, 1)

        def rows_gather(pool, u, dst, table, slot, done):
            for j in range(J):
                nc.gpsimd.indirect_dma_start(dst[u][:, j, :], None, table, bass.IndirectOffsetOnAxis(ap=islot[u][:, slot, j:j + 1], axis=0)).then_inc(done[u].sem, 16)

        def rows_scatter(pool, u, src, table, slot, done):
            for j in range(J):
                nc.gpsimd.indirect_dma_start(table, bass.IndirectOffsetOnAxis(ap=islot[u][:, slot, j:j + 1], axis=0), src[u][:, j, :], None,
                                             bounds_check=N - 1, oob_is_err=False).then_inc(done[u].sem, 16)

        def indices(pool, i, u, done, *lists):
            for n, which in enumerate(lists):
                last = nc.gpsimd.tensor_copy(islot[u][:, n, :], ix[:, which, bass.ds((2 * i + u) * J, J)])
            last.then_inc(done, 1)
            pool.wait_ge(done, ready(i, u))
            pool.sem_inc(gate, 1)

        def transposes(dst, src, u):
            for j in range(J):
                last = nc.tensor.transpose(dst[u][:, j * P:(j + 1) * P], src[u][:, j, :], ident[:, :])
            return last

        def back_product(dst, lhs, rhs, u):
            for j in range(J):
                for c in range(len(lhs)):
                    last = nc.tensor.matmul(dst[u][:, j * P:(j + 1) * P], lhs[c][:, j * P:(j + 1) * P], rhs[c],
                                            start=(c == 0), stop=(c == len(lhs) - 1))
            return last

        for edge in (False, True):
            n_pairs = EPAIR if edge else NPAIR
            ph = Phase()
            tpd, cpd, hidd, expd, tmin, elud, xbd, y1d, r1d, tp1d, cp1d, y2d, r2d, ixd = ph.sems(14)
            ain = ph.sems(2)
            xin, o1, o2 = (gat_a, sca_a, sca_b) if edge else (ph.sems(2) for _ in range(3))
            norm1, norm2 = Norm(ph, rN, yN), Norm(ph, rN, zN)
            bias = [b0[:, 4 + 2 * edge + h:5 + 2 * edge + h] for h in range(2)]
            per = 16 * J if edge else 16
            x1T = [agg[u][:, 1, :] for u in range(2)] if not edge else [big[:, u, :] for u in range(2)]
            with nc.Block() as block:

                @block.sync
                def _(sp):
                    ph.clear_other(sp)

                    def body(i):
                        for u in range(2):
                            g = 2 * i + u
                            if edge:
                                free(sp, hidd, i)
                                sp.dma_start(agg[u][:, :, :].rearrange("p h c -> p (h c)"), plane(agg0, g)).then_inc(ain[u], 16)
                                continue
                            free(sp, xbd, i)
                            free(sp, tpd, i)
                            if isinstance(i, int) and g == NG - 1:
                                sp.dma_start(flat(xN[u])[0:TAILP, :], tail(a["x"])).then_inc(xin[u], 16)
                            else:
                                sp.dma_start(flat(xN[u]), group(a["x"], g)).then_inc(xin[u], 16)
                        for norm, y, tab, o in ((norm1, yN, x1_tab, o1), (norm2, zN, x2_tab, o2)):
                            for u in range(2):
                                if not edge:
                                    sp.wait_ge(norm.done, ready(i, u))
                                    sp.dma_start(group(tab, 2 * i + u), flat(y[u])).then_inc(o[u], 16)

                    pairs(sp, n_pairs, body, last=not edge)
                    for u in range(2):
                        if not edge:
                            sp.wait_ge(o1[u], 16 * NPAIR)
                            sp.wait_ge(o2[u], 16 * NPAIR)

                @block.gpsimd
                def _(pool):
                    def body(i):
                        if edge:
                            for u in range(2):
                                free(pool, xin[u], i, k=per)
                                free(pool, o1[u], i, k=per)
                                free(pool, o2[u], i, k=per)
                                free(pool, tpd, i)
                                free(pool, xbd, i)
                                pool.sem_inc(gate, 1)
                                indices(pool, i, u, ixd, IX_DST, IX_DSTW)
                                rows_gather(pool, u, xN, a["x"], 0, xin)
                        for u in range(2):
                            landed(pool, xin[u], per * i + per)
                            free(pool, r1d, i)
                            nc.gpsimd.tensor_tensor(flat(xb[u]), flat(xN[u]), flat(b2b_bc), ADD).then_inc(xbd, 1)
                        norm1.rstd_steps(pool, i)
                        if edge:
                            for u in range(2):
                                pool.wait_ge(norm1.done, ready(i, u))
                                pool.sem_inc(gate, 1)
                                rows_scatter(pool, u, yN, x1_tab, 1, o1)
                        norm2.rstd_steps(pool, i)
                        if edge:
                            for u in range(2):
                                pool.wait_ge(norm2.done, ready(i, u))
                                pool.sem_inc(gate, 1)
                                rows_scatter(pool, u, zN, x2_tab, 1, o2)

                    pairs(pool, n_pairs, body)
                    if edge:
                        for u in range(2):
                            landed(pool, o1[u], per * EPAIR)
                            landed(pool, o2[u], per * EPAIR)

                @block.tensor
                def _(pe):
                    def body(i):
                        for u in range(2):
                            landed(pe, xin[u], per * i + per)
                            free(pe, r2d, i)
                            transposes(A, xN, u).then_inc(tpd, 1)
                        for u in range(2):
                            pe.wait_ge(cpd, ready(i, u))
                            free(pe, elud, i)
                            if edge:
                                pe.wait_ge(ain[u], 16 * i + 16)
                            for h in range(2):
                                cols = slice(h * P, (h + 1) * P)
                                last = nc.tensor.matmul(H[u][h][:, :], W2a[:, 0, cols], xT[u][:, :], start=True, stop=not edge)
                                if edge:
                                    for c in range(2):
                                        last = nc.tensor.matmul(H[u][h][:, :], Wf[:, c, cols], agg[u][:, c, :], start=False, stop=(c == 1))
                            last.then_inc(hidd, 1)
                        for u in range(2):
                            pe.wait_ge(elud, ready(i, u))
                            back_product(A, [hid[u][:, c, :] for c in range(2)], [W2b[:, c, :] for c in range(2)], u).then_inc(y1d, 1)
                        for u in range(2):
                            pe.wait_ge(norm1.done, ready(i, u))
                            transposes(A, yN, u).then_inc(tp1d, 1)
                        for u in range(2):
                            pe.wait_ge(cp1d, ready(i, u))
                            back_product(A, [x1T[u]], [WL1[:, :]], u).then_inc(y2d, 1)

                    pairs(pe, n_pairs, body)

                @block.scalar
                def _(act):
                    def body(i):
                        for u in range(2):
                            act.wait_ge(tpd, ready(i, u))
                            free(act, hidd, i)
                            nc.scalar.activation(xT[u][:, :], A[u][:, :], ACT.Copy).then_inc(cpd, 1)
                        for u in range(2):
                            act.wait_ge(hidd, ready(i, u))
                            free(act, y1d, i)
                            for h in range(2):
                                last = nc.scalar.activation(hid[u][:, h, :], H[u][h][:, :], ACT.Exp, bias=bias[h])
                            last.then_inc(expd, 1)
                        for u in range(2):
                            act.wait_ge(tp1d, ready(i, u))
                            free(act, y2d, i)
                            nc.scalar.activation(x1T[u], A[u][:, :], ACT.Copy).then_inc(cp1d, 1)

                    pairs(act, n_pairs, body)

                @block.vector
                def _(dve):
                    def free1(dve, i, u):
                        free(dve, o1[u], i, k=per)

                    def free2(dve, i, u):
                        free(dve, o2[u], i, k=per)

                    def body(i):
                        elu_steps(dve, i, H, bias, expd, hid3, tmin, elud)
                        for u in range(2):
                            dve.wait_ge(y1d, ready(i, u))
                            dve.wait_ge(xbd, ready(i, u))
                            free(dve, norm2.done, i)
                            nc.vector.tensor_tensor(flat(rN[u]), A[u][:, :], flat(xb[u]), ADD).then_inc(r1d, 1)
                        norm1.moments_steps(dve, i, r1d)
                        norm1.scale_steps(dve, i, free1)
                        for u in range(2):
                            dve.wait_ge(y2d, ready(i, u))
                            dve.wait_ge(norm1.done, ready(i, u))
                            nc.vector.tensor_tensor(flat(rN[u]), A[u][:, :], flat(yN[u]), ADD).then_inc(r2d, 1)
                        norm2.moments_steps(dve, i, r2d)
                        norm2.scale_steps(dve, i, free2)

                    pairs(dve, n_pairs, body)
            if edge:
                for s in (*xin, *o1, *o2):
                    s.end(per * EPAIR)

        ph = Phase()
        ixd, scd, tpd, samed, scand = ph.sems(5)
        kin, aout = ph.sems(2), ph.sems(2)
        gx, gi = gat_a, gat_b
        same = [flat(xb[u]) for u in range(2)]
        total = [agg[u][:, 0, :] for u in range(2)]
        with nc.Block() as block:

            @block.sync
            def _(sp):
                ph.clear_other(sp)

                def body(i):
                    for u in range(2):
                        free(sp, samed, i)
                        sp.dma_start(krow[u][:, 0:GR + 1], row_bc(key_row[0], (2 * i + u) * GR + FRONT - 1, GR + 1)).then_inc(kin[u], 16)
                    for u in range(2):
                        sp.wait_ge(scand, ready(i, u, 1))
                        sp.dma_start(plane(agg1, 2 * i + u), total[u]).then_inc(aout[u], 16)

                pairs(sp, EPAIR, body)
                for u in range(2):
                    sp.wait_ge(aout[u], 16 * EPAIR)

            @block.gpsimd
            def _(pool):
                def body(i):
                    for u in range(2):
                        free(pool, gx[u], i, k=16 * J)
                        free(pool, gi[u], i, k=16 * J)
                        free(pool, scd, i)
                        pool.sem_inc(gate, 1)
                        indices(pool, i, u, ixd, IX_SDST)
                        rows_gather(pool, u, xN, x1_tab, 0, gx)
                        rows_gather(pool, u, ginv, inv_tab, 0, gi)

                pairs(pool, EPAIR, body)

            @block.tensor
            def _(pe):
                def body(i):
                    for u in range(2):
                        pe.wait_ge(scd, ready(i, u))
                        free(pe, scand, i, 1)
                        transposes(A, yN, u).then_inc(tpd, 1)

                pairs(pe, EPAIR, body)

            @block.vector
            def _(dve):
                nc.vector.memset(agg[1][:, :, :], 0.0).then_inc(scand, 1)

                def body(i):
                    for u in range(2):
                        dve.wait_ge(kin[u], 16 * i + 16)
                        nc.vector.tensor_tensor(same[u], krow[u][:, 1:GR + 1], krow[u][:, 0:GR], EQ).then_inc(samed, 1)
                    for u in range(2):
                        landed(dve, gx[u], 16 * J * i + 16 * J)
                        landed(dve, gi[u], 16 * J * i + 16 * J)
                        free(dve, tpd, i)
                        for j in range(J):
                            last = nc.vector.tensor_scalar(yN[u][:, j, :], xN[u][:, j, :], ginv[u][:, j, :], None, MUL)
                        last.then_inc(scd, 1)
                    for u in range(2):
                        dve.wait_ge(samed, ready(i, u))
                        dve.wait_ge(tpd, ready(i, u))
                        free(dve, aout[u], i, k=16)
                        dve.wait_ge(scand, ready(i, u))
                        nc.vector.tensor_tensor_scan(total[u], same[u], A[u][:, :], total[1 - u][:, GR - 1:GR], MUL, ADD).then_inc(scand, 1)

                pairs(dve, EPAIR, body)

        for s in (*gx, *gi):
            s.end(16 * J * EPAIR)

        ph = Phase()
        ixd, scd, tpd, sumd, y2d, r2d = ph.sems(6)
        ain = ph.sems(2)
        gx, o2 = gat_a, sca_a
        norm = Norm(ph, rN, zN)
        with nc.Block() as block:

            @block.sync
            def _(sp):
                ph.clear_other(sp)

                def body(i):
                    for u in range(2):
                        free(sp, sumd, i)
                        sp.dma_start(total[u], plane(agg1, 2 * i + u)).then_inc(ain[u], 16)

                pairs(sp, EPAIR, body)

            @block.gpsimd
            def _(pool):
                def body(i):
                    for u in range(2):
                        free(pool, gx[u], i, k=16 * J)
                        free(pool, o2[u], i, k=16 * J)
                        free(pool, r2d, i)
                        free(pool, scd, i)
                        pool.sem_inc(gate, 1)
                        indices(pool, i, u, ixd, IX_SSRC, IX_SSRCW)
                        rows_gather(pool, u, xN, x1_tab, 0, gx)
                    norm.rstd_steps(pool, i)
                    for u in range(2):
                        pool.wait_ge(norm.done, ready(i, u))
                        pool.sem_inc(gate, 1)
                        rows_scatter(pool, u, zN, x2_tab, 1, o2)

                pairs(pool, EPAIR, body)
                for u in range(2):
                    landed(pool, o2[u], 16 * J * EPAIR)

            @block.tensor
            def _(pe):
                def body(i):
                    for u in range(2):
                        pe.wait_ge(scd, ready(i, u))
                        free(pe, r2d, i)
                        transposes(A, yN, u).then_inc(tpd, 1)
                    for u in range(2):
                        pe.wait_ge(sumd, ready(i, u))
                        back_product(A, [xT[u][:, :]], [WL1[:, :]], u).then_inc(y2d, 1)

                pairs(pe, EPAIR, body)

            @block.vector
            def _(dve):
                def body(i):
                    for u in range(2):
                        landed(dve, gx[u], 16 * J * i + 16 * J)
                        free(dve, tpd, i)
                        for j in range(J):
                            last = nc.vector.tensor_scalar(yN[u][:, j, :], xN[u][:, j, :], inv_e[:, bass.ds((2 * i + u) * J + j, 1)], None, MUL)
                        last.then_inc(scd, 1)
                    for u in range(2):
                        dve.wait_ge(tpd, ready(i, u))
                        dve.wait_ge(ain[u], 16 * i + 16)
                        free(dve, y2d, i)
                        nc.vector.tensor_tensor(xT[u][:, :], A[u][:, :], total[u], ADD).then_inc(sumd, 1)
                    for u in range(2):
                        dve.wait_ge(y2d, ready(i, u))
                        free(dve, norm.done, i)
                        for j in range(J):
                            last = nc.vector.scalar_tensor_tensor(rN[u][:, j, :], A[u][:, j * P:(j + 1) * P], inv_e[:, bass.ds((2 * i + u) * J + j, 1)],
                                                                  xN[u][:, j, :], MUL, ADD)
                        last.then_inc(r2d, 1)
                    norm.moments_steps(dve, i, r2d)
                    norm.scale_steps(dve, i, lambda dve, i, u: free(dve, o2[u], i, k=16 * J))

                pairs(dve, EPAIR, body)

        for s in (*gx, *o2):
            s.end(16 * J * EPAIR)

        def typed_messages(l, table, out_tab):
            ph = Phase()
            ixd, tpd, cpd, projd, hd, maskd, msgd, samed, scand = ph.sems(9)
            kin, tin, aout = (ph.sems(2) for _ in range(3))
            gx = gat_a
            same = [flat(xb[u]) for u in range(2)]
            types = [flat(rN[u]) for u in range(2)]
            hT = [flat(zN[u]) for u in range(2)]
            masked = [big[:, 8 * u:8 * u + 8, :] for u in range(2)]
            total = [agg[u][:, 0, :] for u in range(2)]
            with nc.Block() as block:

                @block.sync
                def _(sp):
                    ph.clear_other(sp)

                    def body(i):
                        for u in range(2):
                            free(sp, samed, i)
                            sp.dma_start(krow[u][:, 0:GR + 1], row_bc(key_row[1], (2 * i + u) * GR + FRONT - 1, GR + 1)).then_inc(kin[u], 16)
                            free(sp, maskd, i)
                            sp.sem_inc(sp_gate, 1)
                            sp.dma_start(types[u], row_bc(type_row, (2 * i + u) * GR, GR)).then_inc(tin[u], 16)
                        for u in range(2):
                            sp.wait_ge(scand, ready(i, u, 1))
                            sp.dma_start(plane(out_tab, 2 * i + u), total[u]).then_inc(aout[u], 16)

                    pairs(sp, EPAIR, body)
                    for u in range(2):
                        sp.wait_ge(aout[u], 16 * EPAIR)

                @block.gpsimd
                def _(pool):
                    def body(i):
                        for u in range(2):
                            free(pool, gx[u], i, k=16 * J)
                            free(pool, tpd, i)
                            pool.sem_inc(gate, 1)
                            indices(pool, i, u, ixd, IX_SRC)
                            rows_gather(pool, u, xN, table, 0, gx)

                    pairs(pool, EPAIR, body)

                @block.tensor
                def _(pe):
                    def body(i):
                        for u in range(2):
                            landed(pe, gx[u], 16 * J * i + 16 * J)
                            free(pe, cpd if l == 0 else hd, i)
                            transposes(A, xN, u).then_inc(tpd, 1)
                        if l == 0:
                            for u in range(2):
                                pe.wait_ge(cpd, ready(i, u))
                                free(pe, hd, i)
                                nc.tensor.matmul(B[u][:, :], Wp[:, :], xT[u][:, :], start=True, stop=True).then_inc(projd, 1)
                        for u in range(2):
                            pe.wait_ge(maskd, ready(i, u))
                            free(pe, scand, i, 1)
                            for t in range(NTYPE):
                                last = nc.tensor.matmul(H[u][0][:, :], We[:, l * NTYPE + t, :], masked[u][:, t, :], start=(t == 0), stop=(t == NTYPE - 1))
                            last.then_inc(msgd, 1)

                    pairs(pe, EPAIR, body)

                @block.scalar
                def _(act):
                    def body(i):
                        if l == 0:
                            for u in range(2):
                                act.wait_ge(tpd, ready(i, u))
                                free(act, projd, i)
                                nc.scalar.activation(xT[u][:, :], A[u][:, :], ACT.Copy).then_inc(cpd, 1)
                        for u in range(2):
                            act.wait_ge(projd if l == 0 else tpd, ready(i, u))
                            free(act, maskd, i)
                            if l == 0:
                                nc.scalar.activation(hT[u], B[u][:, :], ACT.Relu, bias=bp[:, :]).then_inc(hd, 1)
                            else:
                                nc.scalar.activation(hT[u], A[u][:, :], ACT.Copy).then_inc(hd, 1)

                    pairs(act, EPAIR, body)

                @block.vector
                def _(dve):
                    nc.vector.memset(agg[1][:, :, :], 0.0).then_inc(scand, 1)

                    def body(i):
                        for u in range(2):
                            dve.wait_ge(kin[u], 16 * i + 16)
                            nc.vector.tensor_tensor(same[u], krow[u][:, 1:GR + 1], krow[u][:, 0:GR], EQ).then_inc(samed, 1)
                        for u in range(2):
                            dve.wait_ge(hd, ready(i, u))
                            dve.wait_ge(tin[u], 16 * i + 16)
                            free(dve, msgd, i)
                            for t in range(NTYPE):
                                last = nc.vector.scalar_tensor_tensor(masked[u][:, t, :], types[u], float(t), hT[u], EQ, MUL)
                            last.then_inc(maskd, 1)
                        for u in range(2):
                            dve.wait_ge(samed, ready(i, u))
                            dve.wait_ge(msgd, ready(i, u))
                            free(dve, aout[u], i, k=16)
                            dve.wait_ge(scand, ready(i, u))
                            nc.vector.tensor_tensor_scan(total[u], same[u], H[u][0][:, :], total[1 - u][:, GR - 1:GR], MUL, ADD).then_inc(scand, 1)

                    pairs(dve, EPAIR, body)

            for s in gx:
                s.end(16 * J * EPAIR)

        work = [big[:, 8 * u:8 * u + 8, :] for u in range(2)]

        class Gru:

            def __init__(self, ph, l, hin, hout, messages):
                self.l, self.hin, self.hout, self.messages = l, hin, hout, messages
                self.gates, self.rz, self.q, self.q2, self.n, self.d, self.dz, self.s, self.done = ph.sems(9)

            def pe(self, pe, i, h_ready, msg_in, a_free):
                l = self.l
                for u in range(2):
                    h = work[u][:, self.hin, :]
                    pe.wait_ge(h_ready[u] if isinstance(h_ready, list) else h_ready, 16 * i + 16 if isinstance(h_ready, list) else ready(i, u))
                    a_free(pe, i, u)
                    free(pe, self.q2, i)
                    if self.messages:
                        pe.wait_ge(msg_in[u], 16 * i + 16)
                    for bank, c in ((H[u][0], 0), (H[u][1], 1), (A[u], 2)):
                        both = self.messages and c < 2
                        last = nc.tensor.matmul(bank[:, :], Whh[:, l, c * D:(c + 1) * D], h, start=True, stop=not both)
                        if both:
                            last = nc.tensor.matmul(bank[:, :], Wih[:, l, c * D:(c + 1) * D], self.messages[u], start=False, stop=True)
                    if self.messages:
                        last = nc.tensor.matmul(B[u][:, :], Wih[:, l, 2 * D:3 * D], self.messages[u], start=True, stop=True)
                    last.then_inc(self.gates, 1)

            def act_gates(self, act, i):
                for u in range(2):
                    act.wait_ge(self.gates, ready(i, u))
                    free(act, self.dz, i)
                    nc.scalar.activation(hid[u][:, 0, :], H[u][0][:, :], ACT.Sigmoid, bias=brz[:, self.l, 0:1])
                    nc.scalar.activation(hid[u][:, 1, :], H[u][1][:, :], ACT.Sigmoid, bias=brz[:, self.l, 1:2]).then_inc(self.rz, 1)

            def act_new(self, act, i):
                for u in range(2):
                    act.wait_ge(self.q2, ready(i, u))
                    free(act, self.s, i)
                    nc.scalar.activation(work[u][:, 1, :], work[u][:, 0, :], ACT.Tanh, bias=bih[:, self.l, 2:3]).then_inc(self.n, 1)

            def act_relu(self, act, i, out_free):
                for u in range(2):
                    act.wait_ge(self.s, ready(i, u))
                    out_free(act, i, u)
                    nc.scalar.activation(work[u][:, self.hout, :], work[u][:, 2, :], ACT.Relu).then_inc(self.done, 1)

            def dve_q(self, dve, i):
                for u in range(2):
                    dve.wait_ge(self.rz, ready(i, u))
                    free(dve, self.n, i)
                    nc.vector.scalar_tensor_tensor(work[u][:, 0, :], A[u][:, :], bhh[:, self.l, 2:3], hid[u][:, 0, :], ADD, MUL)\
                        .then_inc(self.q if self.messages else self.q2, 1)
                if self.messages:
                    for u in range(2):
                        dve.wait_ge(self.q, ready(i, u))
                        nc.vector.tensor_tensor(work[u][:, 0, :], work[u][:, 0, :], B[u][:, :], ADD).then_inc(self.q2, 1)

            def dve_dz(self, dve, i):
                for u in range(2):
                    dve.wait_ge(self.d, ready(i, u))
                    nc.vector.tensor_tensor(work[u][:, 2, :], work[u][:, 2, :], hid[u][:, 1, :], MUL).then_inc(self.dz, 1)

            def pool_d(self, pool, i):
                for u in range(2):
                    pool.wait_ge(self.n, ready(i, u))
                    free(pool, self.done, i)
                    nc.gpsimd.tensor_tensor(work[u][:, 2, :], work[u][:, self.hin, :], work[u][:, 1, :], SUB).then_inc(self.d, 1)

            def pool_s(self, pool, i):
                for u in range(2):
                    pool.wait_ge(self.dz, ready(i, u))
                    nc.gpsimd.tensor_tensor(work[u][:, 2, :], work[u][:, 2, :], work[u][:, 1, :], ADD).then_inc(self.s, 1)

        def recurrent(mode):
            dense, one, two = mode == "dense", mode == "first", mode == "second"
            n_pairs = NPAIR if dense else EPAIR
            ph = Phase()
            tpd, cpd, projd, hd, xbd, tp1d, cp1d, yd, rd, ixd = ph.sems(10)
            min_, hin, xout, hout, cout = (ph.sems(2) for _ in range(5))
            if one:
                xin, rout = gat_a, sca_a
            elif two:
                xin, rout, r3out = ph.sems(2), None, sca_a
            else:
                xin, rout, r3out = ph.sems(2), ph.sems(2), ph.sems(2)
            per_x = 16 * J if one else 16
            per_o = 16 if dense else 16 * J
            messages = None if dense else [agg[u][:, 0, :] for u in range(2)]
            gru1 = Gru(ph, 0, 3, 4, messages) if not two else None
            gru2 = Gru(ph, 1, 4, 5, messages) if not one else None
            norm = Norm(ph, rN, zN) if not one else None
            with nc.Block() as block:

                @block.sync
                def _(sp):
                    ph.clear_other(sp)

                    def body(i):
                        for u in range(2):
                            g = 2 * i + u
                            if not one:
                                free(sp, xbd, i)
                                if dense:
                                    free(sp, tpd, i)
                                    sp.dma_start(flat(xN[u]), group(x2_tab, g)).then_inc(xin[u], 16)
                                else:
                                    sp.dma_start(flat(xN[u]), plane(x2_c, g)).then_inc(xin[u], 16)
                                    free(sp, gru2.d, i)
                                    free(sp, gru2.gates, i)
                                    sp.dma_start(work[u][:, 4, :], plane(h1_c, g)).then_inc(hin[u], 16)
                            if not dense:
                                free(sp, (gru1 or gru2).gates, i)
                                sp.dma_start(messages[u], plane(agg2 if one else agg3, g)).then_inc(min_[u], 16)
                        for u in range(2):
                            g = 2 * i + u
                            if one:
                                landed(sp, xin[u], per_x * i + per_x)
                                sp.dma_start(plane(x2_c, g), flat(xN[u])).then_inc(xout[u], 16)
                                sp.wait_ge(gru1.done, ready(i, u))
                                sp.dma_start(plane(h1_c, g), work[u][:, 4, :]).then_inc(hout[u], 16)
                            if dense:
                                sp.wait_ge(cp1d, ready(i, u))
                                sp.dma_start(group(h1_tab, g), flat(yN[u])).then_inc(rout[u], 16)
                        if not one:
                            for u in range(2):
                                sp.wait_ge(norm.done, ready(i, u))
                                sp.dma_start(group(x3_tab, 2 * i + u) if dense else plane(x3_c, 2 * i + u), flat(zN[u])).then_inc(cout[u], 16)

                    pairs(sp, n_pairs, body)
                    for u in range(2):
                        for s, used in ((xout[u], one), (hout[u], one), (rout[u] if dense else None, dense), (cout[u], not one)):
                            if used:
                                sp.wait_ge(s, 16 * n_pairs)

                @block.gpsimd
                def _(pool):
                    def body(i):
                        if not dense:
                            for u in range(2):
                                if one:
                                    free(pool, xin[u], i, k=per_x)
                                    free(pool, rout[u], i, k=per_o)
                                    free(pool, tpd, i)
                                    free(pool, xout[u], i, k=16)
                                    pool.sem_inc(gate, 1)
                                    indices(pool, i, u, ixd, IX_DST, IX_DSTW)
                                    rows_gather(pool, u, xN, x2_tab, 0, xin)
                                else:
                                    free(pool, r3out[u], i, k=per_o)
                                    pool.sem_inc(gate, 1)
                                    indices(pool, i, u, ixd, IX_DSTW)
                        if not one:
                            for u in range(2):
                                pool.wait_ge(xin[u], 16 * i + 16)
                                free(pool, rd, i)
                                nc.gpsimd.tensor_tensor(flat(xb[u]), flat(xN[u]), flat(bo_bc), ADD).then_inc(xbd, 1)
                        if gru1:
                            gru1.pool_d(pool, i)
                            gru1.pool_s(pool, i)
                        if one:
                            for u in range(2):
                                pool.wait_ge(cp1d, ready(i, u))
                                pool.sem_inc(gate, 1)
                                rows_scatter(pool, u, yN, h1_tab, 1, rout)
                        if gru2:
                            gru2.pool_d(pool, i)
                            gru2.pool_s(pool, i)
                            norm.rstd_steps(pool, i)
                        if two:
                            for u in range(2):
                                pool.wait_ge(norm.done, ready(i, u))
                                pool.sem_inc(gate, 1)
                                rows_scatter(pool, u, zN, x3_tab, 0, r3out)

                    pairs(pool, n_pairs, body)
                    for u in range(2):
                        if one:
                            landed(pool, rout[u], per_o * EPAIR)
                        if two:
                            landed(pool, r3out[u], per_o * EPAIR)

                @block.tensor
                def _(pe):
                    def body(i):
                        if not two:
                            for u in range(2):
                                landed(pe, xin[u], per_x * i + per_x)
                                free(pe, rd if dense else gru1.q2, i)
                                transposes(A, xN, u).then_inc(tpd, 1)
                            for u in range(2):
                                pe.wait_ge(cpd, ready(i, u))
                                free(pe, cp1d, i)
                                nc.tensor.matmul(B[u][:, :], Wp[:, :], xT[u][:, :], start=True, stop=True).then_inc(projd, 1)
                            gru1.pe(pe, i, hd, min_, lambda pe, i, u: pe.wait_ge(cpd, ready(i, u)))
                            for u in range(2):
                                pe.wait_ge(gru1.done, ready(i, u))
                                for j in range(J):
                                    last = nc.tensor.transpose(B[u][:, j * P:(j + 1) * P], work[u][:, 4, j * P:(j + 1) * P], ident[:, :])
                                last.then_inc(tp1d, 1)
                        if not one:
                            gru2.pe(pe, i, hin if two else gru1.done, min_,
                                    (lambda pe, i, u: free(pe, rd, i)) if two else (lambda pe, i, u: pe.wait_ge(gru1.q2, ready(i, u))))
                            for u in range(2):
                                pe.wait_ge(gru2.done, ready(i, u))
                                back_product(A, [work[u][:, 5, :]], [Wo[:, :]], u).then_inc(yd, 1)

                    pairs(pe, n_pairs, body)

                @block.scalar
                def _(act):
                    def h1_free(act, i, u):
                        if one:
                            free(act, hout[u], i, k=16)
                            free(act, tp1d, i)
                        else:
                            free(act, gru2.d, i)
                            free(act, gru2.gates, i)
                            free(act, tp1d, i)

                    def body(i):
                        if gru1:
                            for u in range(2):
                                act.wait_ge(tpd, ready(i, u))
                                free(act, projd, i)
                                nc.scalar.activation(xT[u][:, :], A[u][:, :], ACT.Copy).then_inc(cpd, 1)
                            for u in range(2):
                                act.wait_ge(projd, ready(i, u))
                                free(act, gru1.d, i)
                                nc.scalar.activation(work[u][:, 3, :], B[u][:, :], ACT.Relu, bias=bp[:, :]).then_inc(hd, 1)
                            gru1.act_gates(act, i)
                            gru1.act_new(act, i)
                            gru1.act_relu(act, i, h1_free)
                            for u in range(2):
                                act.wait_ge(tp1d, ready(i, u))
                                free(act, rout[u], i, k=per_o)
                                nc.scalar.activation(flat(yN[u]), B[u][:, :], ACT.Copy).then_inc(cp1d, 1)
                        if gru2:
                            gru2.act_gates(act, i)
                            gru2.act_new(act, i)
                            gru2.act_relu(act, i, lambda act, i, u: free(act, yd, i))

                    pairs(act, n_pairs, body)

                @block.vector
                def _(dve):
                    def out_free(dve, i, u):
                        free(dve, cout[u], i, k=16)
                        if two:
                            free(dve, r3out[u], i, k=per_o)

                    def body(i):
                        if gru1:
                            gru1.dve_q(dve, i)
                            gru1.dve_dz(dve, i)
                        if gru2:
                            gru2.dve_q(dve, i)
                            gru2.dve_dz(dve, i)
                            for u in range(2):
                                dve.wait_ge(yd, ready(i, u))
                                dve.wait_ge(xbd, ready(i, u))
                                free(dve, norm.done, i)
                                nc.vector.tensor_tensor(flat(rN[u]), A[u][:, :], flat(xb[u]), ADD).then_inc(rd, 1)
                            norm.moments_steps(dve, i, rd)
                            norm.scale_steps(dve, i, out_free)

                    pairs(dve, n_pairs, body)

            if one:
                for s in (*xin, *rout):
                    s.end(per_o * EPAIR)
            if two:
                for s in r3out:
                    s.end(per_o * EPAIR)

        recurrent("dense")
        typed_messages(0, x2_tab, agg2)
        recurrent("first")
        typed_messages(1, h1_tab, agg3)
        recurrent("second")

        col_names = ("blankp0", "blankp1", "nblank0", "c0", "c1", "mx", "vx", "nmx", "sd", "sdd", "sxd", "md", "cov", "vd", "t0", "t1",
                     "var", "inv", "s0", "mu", "A1", "B1", "alpha", "s1", "C", "Dv", "F1", "as0", "bshift", "t2", "cw0", "cw1")
        cols = {n: f3[:, k:k + 1] for k, n in enumerate(col_names)}
        G_, BE, BLANK, BB, A_, CB, CW = 1, 2, 3, 0, 4, 5, 6

        def val(l, c):
            return v3[:, l, c:c + 1]

        ph = Phase()
        tpd, bnd, linked, tot, powd, eps_d = ph.sems(6)
        xin = ph.sems(2)
        with nc.Block() as block:

            @block.sync
            def _(sp):
                ph.clear_other(sp)

                def body(i):
                    for u in range(2):
                        free(sp, tpd, i)
                        g = 2 * i + u
                        if isinstance(i, int) and g == NG - 1:
                            sp.dma_start(flat(xN[u])[0:TAILP, :], tail(x3_tab)).then_inc(xin[u], 16)
                        else:
                            sp.dma_start(flat(xN[u]), group(x3_tab, g)).then_inc(xin[u], 16)

                pairs(sp, NPAIR, body, last=True)

            @block.tensor
            def _(pe):
                for l in range(2):
                    last = nc.tensor.matmul(B[0][:, l:l + 1], W3[:, l, :], val(l, BLANK), start=True, stop=True)
                last.then_inc(tot, 1)

                def body(i):
                    for u in range(2):
                        pe.wait_ge(xin[u], 16 * i + 16)
                        free(pe, bnd, i)
                        transposes(A, xN, u).then_inc(tpd, 1)

                pairs(pe, NPAIR, body)

            @block.vector
            def _(dve):
                n = [0]

                def link(ins):
                    n[0] += 1
                    ins.then_inc(linked, 1)
                    dve.wait_ge(linked, n[0])

                dve.wait_ge(tot, 1)
                for l in range(2):
                    link(nc.vector.tensor_tensor(cols[f"blankp{l}"], B[0][:, l:l + 1], val(l, BB), ADD))
                    link(nc.vector.reduce_sum(cols["t0"], v3[:, l, CW:CW + 4], axis=mybir.AxisListType.X))
                    link(nc.vector.scalar_tensor_tensor(cols[f"c{l}"], cols[f"blankp{l}"], cols["t0"], val(l, CB), MUL, ADD))
                link(nc.vector.tensor_scalar(cols["nblank0"], cols["blankp0"], -1.0, None, MUL))

                def body(i):
                    for u in range(2):
                        dve.wait_ge(tpd, ready(i, u))
                        dve.sem_inc(dve_gate, 1)
                        g = 2 * i + u
                        src = A[u][:, :]
                        if isinstance(i, int) and g == NG - 1:
                            src = A[u][:, :].rearrange("p (j q) -> p j q", j=J)[:, :, 0:TAILP]
                        nc.vector.bn_stats(stat3[:, bass.ds(g * 6, 6)], src).then_inc(bnd, 1)

                pairs(dve, NPAIR, body, last=True)
                dve.wait_ge(bnd, NG)
                link(nc.vector.bn_aggr(f3[:, 5:7], stat3[:, :]))
                link(nc.vector.tensor_scalar(cols["nmx"], cols["mx"], -1.0, None, MUL))

        def sorted_pool(l):
            ph = Phase()
            ixd, tpd, cpd, carried, net, tp1d, cp1d, tpx, cpx, smd, smc, convd = ph.sems(12)
            kin, lin, xin, din, o1, o2, o3, o4 = (ph.sems(2) for _ in range(8))
            gx, gs = gat_a, gat_b
            win = [winb[u][:, :] for u in range(2)]
            xsT = [xT[u][:, :] for u in range(2)]
            x3T = [agg[u][:, 0, :] for u in range(2)]
            d1T = [agg[u][:, 1, :] for u in range(2)]
            last_bc = [flat(rN[u]) for u in range(2)]
            dT = [flat(zN[u]) for u in range(2)]
            STEPS = 21 + l

            with nc.Block() as block:

                @block.sync
                def _(sp):
                    ph.clear_other(sp)

                    def body(i):
                        for u in range(2):
                            g = 2 * i + u
                            free(sp, smd, i)
                            sp.dma_start(krow[u][:, 0:GR + 3], row_bc(key_row[1], g * GR + FRONT - 3, GR + 3)).then_inc(kin[u], 16)
                            sp.dma_start(last_bc[u], row_bc(last_row, g * GR, GR)).then_inc(lin[u], 16)
                            if l == 0:
                                free(sp, tpx, i)
                                sp.dma_start(flat(xb[u]), plane(x3_c, g)).then_inc(xin[u], 16)
                            else:
                                free(sp, cpd, i)
                                sp.dma_start(hid[u][:, 0, :], plane(x3src_t, g)).then_inc(din[u], 16)
                                sp.dma_start(d1T[u], plane(d1_t, g)).then_inc(din[u], 16)
                                sp.dma_start(x3T[u], plane(agg1, g)).then_inc(xin[u], 16)
                        for u in range(2):
                            g = 2 * i + u
                            if l == 0:
                                sp.wait_ge(cpd, ready(i, u))
                                sp.dma_start(plane(x3src_t, g), xsT[u]).then_inc(o1[u], 16)
                                sp.wait_ge(cpx, ready(i, u))
                                sp.dma_start(plane(agg1, g), x3T[u]).then_inc(o2[u], 16)
                            sp.wait_ge(net, 2 * STEPS * i + 2 * STEPS)
                            sp.dma_start(plane(d1_t if l == 0 else d2_t, g), dT[u]).then_inc(o3[u], 16)
                            if l == 0:
                                sp.wait_ge(cp1d, ready(i, u))
                                sp.dma_start(d1_tab[bass.ds(g * GR, GR), :].rearrange("(j p) d -> p j d", p=P), yN[u][:, :, :]).then_inc(o4[u], 16)

                    pairs(sp, EPAIR, body)
                    for u in range(2):
                        for s in (o1, o2, o3, o4) if l == 0 else (o3,):
                            sp.wait_ge(s[u], 16 * EPAIR)

                @block.gpsimd
                def _(pool):
                    def body(i):
                        for u in range(2):
                            free(pool, gx[u], i, k=16 * J)
                            free(pool, tpd, i)
                            if l == 0:
                                free(pool, convd, i)
                            pool.sem_inc(gate, 1)
                            indices(pool, i, u, ixd, IX_SRC if l == 0 else IX_SLOT)
                            rows_gather(pool, u, xN, x3_tab if l == 0 else d1_tab, 0, gx)
                            if l == 0:
                                rows_gather(pool, u, ginv, slot_tab, 0, gs)

                    pairs(pool, EPAIR, body)

                @block.tensor
                def _(pe):
                    def body(i):
                        for u in range(2):
                            landed(pe, gx[u], 16 * J * i + 16 * J)
                            free(pe, carried, i, 1)
                            transposes(A, xN, u).then_inc(tpd, 1)
                            if l == 0:
                                pe.wait_ge(xin[u], 16 * i + 16)
                                free(pe, cpx, i)
                                transposes(B, xb, u).then_inc(tpx, 1)
                        if l == 0:
                            for u in range(2):
                                pe.wait_ge(net, 2 * STEPS * i + 2 * STEPS)
                                free(pe, cp1d, i)
                                for j in range(J):
                                    last = nc.tensor.transpose(H[u][0][:, j * P:(j + 1) * P], dT[u][:, j * P:(j + 1) * P], ident[:, :])
                                last.then_inc(tp1d, 1)

                    pairs(pe, EPAIR, body)

                @block.scalar
                def _(act):
                    def body(i):
                        for u in range(2):
                            act.wait_ge(tpd, ready(i, u))
                            if l == 0:
                                free(act, o1[u], i, k=16)
                                nc.scalar.activation(xsT[u], A[u][:, :], ACT.Copy).then_inc(cpd, 1)
                                act.wait_ge(tpx, ready(i, u))
                                free(act, smd, i)
                                free(act, o2[u], i, k=16)
                                nc.scalar.activation(x3T[u], B[u][:, :], ACT.Identity, bias=cols["nmx"]).then_inc(cpx, 1)
                            else:
                                act.wait_ge(din[u], 32 * i + 32)
                                free(act, carried, i, 1)
                                nc.scalar.activation(xsT[u], hid[u][:, 0, :], ACT.Identity, scale=cols["A1"], bias=cols["bshift"]).then_inc(cpd, 1)
                        if l == 0:
                            for u in range(2):
                                act.wait_ge(tp1d, ready(i, u))
                                free(act, o4[u], i, k=16)
                                nc.scalar.activation(flat(yN[u]), H[u][0][:, :], ACT.Copy).then_inc(cp1d, 1)

                    pairs(act, EPAIR, body)

                @block.vector
                def _(dve):
                    nc.vector.memset(win[0][:, :], 0.0)
                    nc.vector.memset(win[1][:, :], 0.0).then_inc(carried, 1)

                    def body(i):
                        for u in range(2):
                            dve.wait_ge(cpd, ready(i, u))
                            dve.wait_ge(tpd, ready(i, u))
                            dve.wait_ge(carried, ready(i, u))
                            free(dve, net, i, k=2 * STEPS)
                            nc.vector.tensor_copy(win[u][:, 0:3], win[1 - u][:, GR:GR + 3])
                            if l == 0:
                                nc.vector.tensor_scalar(win[u][:, 3:3 + GR], A[u][:, :], cols["nblank0"], None, ADD).then_inc(carried, 1)
                            else:
                                nc.vector.scalar_tensor_tensor(win[u][:, 3:3 + GR], A[u][:, :], cols["s0"], xsT[u], MUL, ADD).then_inc(carried, 1)
                        count = [0]

                        def step(make, after=()):
                            for u in range(2):
                                if count[0]:
                                    dve.wait_ge(net, 2 * STEPS * i + (2 * count[0] + u - 1))
                                for f in after:
                                    f(u)
                                make(u).then_inc(net, 1)
                            count[0] += 1

                        w = work
                        for k in (1, 2, 3):
                            step(lambda u: nc.vector.tensor_tensor(w[u][:, 3 + k, :], krow[u][:, 3:3 + GR], krow[u][:, 3 - k:3 - k + GR], EQ),
                                 after=(lambda u: dve.wait_ge(kin[u], 16 * i + 16),))
                        for k in (1, 2, 3):
                            step(lambda u: nc.vector.tensor_tensor(w[u][:, k, :], win[u][:, 3 - k:3 - k + GR], w[u][:, 3 + k, :], MUL),
                                 after=(lambda u: dve.wait_ge(carried, ready(i, u, 1)),))
                        v = lambda u, k: win[u][:, 3:3 + GR] if k == 8 else w[u][:, k, :]
                        for o, a_, b_, op in ((4, 8, 1, MIN), (5, 8, 1, MAX), (6, 2, 3, MIN), (7, 2, 3, MAX), (0, 4, 6, MIN), (1, 4, 6, MAX),
                                              (2, 5, 7, MIN), (3, 5, 7, MAX), (4, 1, 2, MIN), (5, 1, 2, MAX)):
                            step(lambda u: nc.vector.tensor_tensor(v(u, o), v(u, a_), v(u, b_), op))
                        step(lambda u: nc.vector.tensor_scalar(w[u][:, 6, :], w[u][:, 0, :], val(l, CW), None, MUL))
                        step(lambda u: nc.vector.scalar_tensor_tensor(w[u][:, 7, :], w[u][:, 4, :], val(l, CW + 1), w[u][:, 6, :], MUL, ADD))
                        step(lambda u: nc.vector.scalar_tensor_tensor(w[u][:, 6, :], w[u][:, 5, :], val(l, CW + 2), w[u][:, 7, :], MUL, ADD))
                        step(lambda u: nc.vector.scalar_tensor_tensor(dT[u], w[u][:, 3, :], val(l, CW + 3), w[u][:, 6, :], MUL, ADD),
                             after=(lambda u: free(dve, o3[u], i, k=16),) + ((lambda u: free(dve, tp1d, i),) if l == 0 else ()))
                        e = dT
                        if l == 1:
                            step(lambda u: nc.vector.scalar_tensor_tensor(w[u][:, 5, :], d1T[u], cols["as0"], dT[u], MUL, ADD),
                                 after=(lambda u: dve.wait_ge(din[u], 32 * i + 32),))
                            e = [w[u][:, 5, :] for u in range(2)]
                        step(lambda u: nc.vector.scalar_tensor_tensor(w[u][:, 7, :], e[u], 1.0, last_bc[u], MUL, MUL, accum_out=sum3[u][:, 0:1]),
                             after=(lambda u: dve.wait_ge(lin[u], 16 * i + 16), lambda u: free(dve, smc, i)))
                        for u in range(2):
                            dve.wait_ge(net, 2 * STEPS * i + 2 * STEPS)
                            nc.vector.scalar_tensor_tensor(w[u][:, 1, :], w[u][:, 7, :], 1.0, w[u][:, 7, :], MUL, MUL, accum_out=sum3[u][:, 1:2])
                            if l == 0:
                                dve.wait_ge(cpx, ready(i, u))
                            else:
                                dve.wait_ge(xin[u], 16 * i + 16)
                            nc.vector.scalar_tensor_tensor(w[u][:, 2, :], w[u][:, 7, :], 1.0, x3T[u], MUL, MUL, accum_out=sum3[u][:, 2:3]).then_inc(smd, 1)
                        for u in range(2):
                            dve.wait_ge(smd, ready(i, u))
                            nc.vector.tensor_copy(sums[:, bass.ds(2 * i + u, 1), :].rearrange("p o c -> p (o c)"), sum3[u][:, :]).then_inc(smc, 1)
                            if l == 0:
                                landed(dve, gs[u], 16 * J * i + 16 * J)
                                nc.vector.tensor_copy(ix[:, IX_SLOT, bass.ds((2 * i + u) * J, J)], ginv[u][:, :, 0]).then_inc(convd, 1)

                    pairs(dve, EPAIR, body)

            for s in gx:
                s.end(16 * J * EPAIR)
            if l == 0:
                for s in gs:
                    s.end(16 * J * EPAIR)

        def coefficients(l):
            ph = Phase()
            linked, var_d, inv_d, eps_d, rep, mm = ph.sems(6)
            c = cols
            with nc.Block() as block:

                @block.sync
                def _(sp):
                    ph.clear_other(sp)

                @block.gpsimd
                def _(pool):
                    pool.wait_ge(var_d, 1)
                    nc.gpsimd.tensor_scalar(c["t2"], c["var"], EPS, None, ADD).then_inc(eps_d, 1)
                    pool.wait_ge(eps_d, 1)
                    nc.gpsimd.tensor_tensor(c["inv"], c["t2"], mhalf[:, 0:1], ALU.pow).then_inc(inv_d, 1)

                @block.tensor
                def _(pe):
                    if l == 1:
                        pe.wait_ge(rep, 1)
                        nc.tensor.matmul(A[0][:, 0:D], hid[0][:, 0, 0:P], ident[:, :], start=True, stop=True)
                        nc.tensor.matmul(A[1][:, 0:D], hid[0][:, 1, 0:P], ident[:, :], start=True, stop=True).then_inc(mm, 1)

                @block.vector
                def _(dve):
                    n = [0]

                    def link(ins):
                        n[0] += 1
                        ins.then_inc(linked, 1)
                        dve.wait_ge(linked, n[0])

                    def mul(o, x, y):
                        link(nc.vector.tensor_tensor(o, x, y, MUL))

                    def mad(o, x, y, z):
                        link(nc.vector.scalar_tensor_tensor(o, x, y, z, MUL, ADD))

                    for k, name in enumerate(("sd", "sdd", "sxd")):
                        link(nc.vector.reduce_sum(c[name], sums[:, :, k], axis=mybir.AxisListType.X))
                        link(nc.vector.tensor_scalar(c[("md", "vd", "cov")[k]], c[name], 1.0 / N, None, MUL))
                    slope = val(0, A_)
                    if l == 1:
                        mul(c["alpha"], val(1, A_), c["A1"])
                        slope = c["alpha"]
                    mul(c["t0"], c["md"], c["md"])
                    link(nc.vector.tensor_tensor(c["vd"], c["vd"], c["t0"], SUB))
                    mul(c["t0"], slope, c["vx"])
                    link(nc.vector.scalar_tensor_tensor(c["t1"], c["cov"], 2.0, c["t0"], MUL, ADD))
                    mad(c["var"], c["t1"], slope, c["vd"])
                    dve.sem_inc(var_d, 1)
                    dve.wait_ge(inv_d, 1)
                    s = c[f"s{l}"]
                    mul(s, c["inv"], val(l, G_))
                    mad(c["mu"], slope, c["mx"], c["md"])
                    if l == 0:
                        link(nc.vector.tensor_tensor(c["mu"], c["mu"], c["c0"], ADD))
                        link(nc.vector.tensor_tensor(c["t0"], c["c0"], c["mu"], SUB))
                        mad(c["B1"], c["t0"], s, val(0, BE))
                        link(nc.vector.tensor_scalar(c["A1"], s, val(0, A_), 1.0, MUL, ADD))
                        link(nc.vector.tensor_tensor(c["bshift"], c["B1"], c["blankp1"], SUB))
                        mul(c["as0"], val(1, A_), s)
                        return
                    mad(c["t1"], c["B1"], val(1, A_), c["c1"])
                    link(nc.vector.tensor_tensor(c["mu"], c["mu"], c["t1"], ADD))
                    link(nc.vector.tensor_tensor(c["t0"], c["t1"], c["mu"], SUB))
                    mad(c["Dv"], c["t0"], s, val(1, BE))
                    link(nc.vector.tensor_tensor(c["Dv"], c["Dv"], c["B1"], ADD))
                    mad(c["C"], c["alpha"], s, c["A1"])
                    link(nc.vector.tensor_scalar(c["C"], c["C"], 1.0, None, ADD))
                    mad(c["F1"], c["as0"], s, c["s0"])
                    link(nc.vector.tensor_scalar(hid[0][:, 0, 0:P], ones[:, :], c["C"], None, MUL))
                    nc.vector.tensor_scalar(hid[0][:, 1, 0:P], ones[:, :], c["Dv"], None, MUL).then_inc(rep, 1)
                    dve.wait_ge(mm, 1)
                    for j in range(J):
                        nc.vector.tensor_copy(C_bc[:, j, :], A[0][:, 0:D])
                        last = nc.vector.tensor_copy(D_bc[:, j, :], A[1][:, 0:D])
                    link(last)

        def finish(edge):
            n_pairs = EPAIR if edge else NPAIR
            ph = Phase()
            cd, dd, rd, fd, fd2, tpd, ixd = ph.sems(7)
            xin, din = ph.sems(2), ph.sems(2)
            oo = sca_a if edge else ph.sems(2)
            per = 16 * J if edge else 16
            norm = Norm(ph, rN, zN)
            d1T = [agg[u][:, 0, :] for u in range(2)]
            d2T = [agg[u][:, 1, :] for u in range(2)]
            with nc.Block() as block:

                @block.sync
                def _(sp):
                    ph.clear_other(sp)

                    def body(i):
                        for u in range(2):
                            g = 2 * i + u
                            free(sp, cd, i)
                            if edge:
                                free(sp, fd2, i)
                                sp.dma_start(flat(xN[u]), plane(x3_c, g)).then_inc(xin[u], 16)
                                sp.dma_start(d1T[u], plane(d1_t, g)).then_inc(din[u], 16)
                                sp.dma_start(d2T[u], plane(d2_t, g)).then_inc(din[u], 16)
                            else:
                                sp.dma_start(flat(xN[u]), group(x3_tab, g)).then_inc(xin[u], 16)
                        if not edge:
                            for u in range(2):
                                g = 2 * i + u
                                sp.wait_ge(norm.done, ready(i, u))
                                if isinstance(i, int) and g == NG - 1:
                                    sp.dma_start(tail(out), flat(zN[u])[0:TAILP, :]).then_inc(oo[u], 16)
                                else:
                                    sp.dma_start(group(out, g), flat(zN[u])).then_inc(oo[u], 16)

                    pairs(sp, n_pairs, body, last=not edge)
                    if not edge:
                        for u in range(2):
                            sp.wait_ge(oo[u], 16 * NPAIR)

                @block.gpsimd
                def _(pool):
                    def body(i):
                        if edge:
                            for u in range(2):
                                free(pool, oo[u], i, k=per)
                                pool.sem_inc(gate, 1)
                                indices(pool, i, u, ixd, IX_DSTW)
                        for u in range(2):
                            pool.wait_ge(cd, ready(i, u))
                            free(pool, rd if edge else norm.done, i)
                            nc.gpsimd.tensor_tensor(flat(xb[u]), flat(yN[u]), flat(D_bc), ADD).then_inc(dd, 1)
                        norm.rstd_steps(pool, i)
                        if edge:
                            for u in range(2):
                                pool.wait_ge(norm.done, ready(i, u))
                                pool.sem_inc(gate, 1)
                                rows_scatter(pool, u, zN, out, 0, oo)

                    pairs(pool, n_pairs, body)
                    if edge:
                        for u in range(2):
                            landed(pool, oo[u], per * EPAIR)

                @block.tensor
                def _(pe):
                    if edge:
                        def body(i):
                            for u in range(2):
                                pe.wait_ge(fd2, ready(i, u))
                                free(pe, rd, i)
                                for j in range(J):
                                    last = nc.tensor.transpose(A[u][:, j * P:(j + 1) * P], xT[u][:, j * P:(j + 1) * P], ident[:, :])
                                last.then_inc(tpd, 1)

                        pairs(pe, n_pairs, body)

                @block.vector
                def _(dve):
                    def body(i):
                        if edge:
                            for u in range(2):
                                dve.wait_ge(din[u], 32 * i + 32)
                                free(dve, tpd, i)
                                nc.vector.tensor_scalar(xT[u][:, :], d1T[u], cols["F1"], None, MUL).then_inc(fd, 1)
                            for u in range(2):
                                dve.wait_ge(fd, ready(i, u))
                                nc.vector.scalar_tensor_tensor(xT[u][:, :], d2T[u], cols["s1"], xT[u][:, :], MUL, ADD).then_inc(fd2, 1)
                        for u in range(2):
                            dve.wait_ge(xin[u], 16 * i + 16)
                            free(dve, dd, i)
                            nc.vector.tensor_tensor(flat(yN[u]), flat(xN[u]), flat(C_bc), MUL).then_inc(cd, 1)
                        r = xb
                        if edge:
                            r = rN
                            for u in range(2):
                                dve.wait_ge(dd, ready(i, u))
                                dve.wait_ge(tpd, ready(i, u))
                                free(dve, norm.done, i)
                                nc.vector.tensor_tensor(flat(rN[u]), A[u][:, :], flat(xb[u]), ADD).then_inc(rd, 1)
                        norm.r = r
                        norm.moments_steps(dve, i, rd if edge else dd)
                        norm.scale_steps(dve, i, lambda dve, i, u: free(dve, oo[u], i, k=per))

                    pairs(dve, n_pairs, body)

            if edge:
                for s in oo:
                    s.end(per * EPAIR)

        sorted_pool(0)
        coefficients(0)
        sorted_pool(1)
        coefficients(1)
        finish(False)
        finish(True)


_LAYOUT = (
    ("x", "x", None), ("src", "src", None), ("dst", "dst", None), ("edge_attr", "edge_attr_128", None),
    ("edge_type_8", "edge_type_8", None), ("W1a", "L0_gnn_W1a", None), ("b1a", "L0_gnn_b1a", None),
    ("W1bT", "L0_gnn_W1b", (1, 0)), ("b1b", "L0_gnn_b1b", None), ("W2a", "L0_gnn_W2a", None), ("b2a", "L0_gnn_b2a", None),
    ("W2b", "L0_gnn_W2b", None), ("b2b", "L0_gnn_b2b", None), ("WL1", "L1_gnn_W", (1, 0)),
    ("Wp", "L2_gnn_node_proj_w", (1, 0)), ("bp", "L2_gnn_node_proj_b", None), ("We", "L2_gnn_edge_W", (0, 1, 3, 2)),
    ("Wih", "L2_gnn_gru_wih", (0, 2, 1)), ("Whh", "L2_gnn_gru_whh", (0, 2, 1)), ("bih", "L2_gnn_gru_bih", None),
    ("bhh", "L2_gnn_gru_bhh", None), ("Wo", "L2_gnn_out_w", (1, 0)), ("bo", "L2_gnn_out_b", None),
    ("W3", ("L3_gnn_W0", "L3_gnn_W1"), (0, 2, 1)),
    *((f"{n}{l}", f"L3_gnn_{n}{l}", None) for l in range(2) for n in ("b", "cw", "cb", "a", "g", "be", "blank")),
)


def kernel(**inputs):
    from concourse import bacc
    from concourse.bass_utils import run_bass_kernel_spmd

    nc = bacc.Bacc("TRN2", target_bir_lowering=False, num_devices=1)
    arrays, args = {}, {}
    for name, source, order in _LAYOUT:
        if isinstance(source, tuple):
            x = np.stack([np.asarray(inputs[s]) for s in source])
        else:
            x = np.asarray(inputs[source])
        if order:
            x = x.transpose(order)
        if name == "We":
            x = x.reshape(NLAYER * NTYPE, D, D)
        x = np.ascontiguousarray(x)
        arrays["in_" + name] = x
        args[name] = nc.dram_tensor("in_" + name, x.shape, mybir.dt.from_np(x.dtype), kind="ExternalInput").ap()
    out = nc.dram_tensor("out", (N, D), F32, kind="ExternalOutput").ap()
    build(nc, args, out)
    return run_bass_kernel_spmd(nc, [arrays], core_ids=[0]).results[0]["out"]
```

```python
from contextlib import ExitStack

import numpy as np
import concourse.bass as bass
from concourse import mybir

F32, BF16, I32 = mybir.dt.float32, mybir.dt.bfloat16, mybir.dt.int32
ALU, ACT = mybir.AluOpType, mybir.ActivationFunctionType
ADD, SUB, MUL, MAX, MIN, EQ = ALU.add, ALU.subtract, ALU.mult, ALU.max, ALU.min, ALU.is_equal

P = 128
N, E, D, HID = 50000, 12500, 128, 256
NTYPE, NLAYER, TOP = 8, 2, 4
J = 4
GR = J * P
NG = -(-N // GR)
NPAD = NG * GR
TAILP = (N - (NG - 1) * GR) // J
EG = -(-E // GR)
EG += EG % 2
EP = EG * GR
ET = EP // P
EFULL = E // P
NPAIR, EPAIR = NG // 2, EG // 2
LO = 256
PADKEY = NPAD - 1
SKIP = 1 << 20
FRONT = 16
ROWLEN = FRONT + EP + FRONT
EPS = 1e-5
NHI = 2 * P * LO
assert N <= NPAD and N % J == 0 and PADKEY >= N and PADKEY < NHI


def pairs(eng, n, body, last=False):
    body(0)
    end = n - 1 if last else n
    if end > 1:
        with eng.Fori(1, end) as i:
            body(i)
    if last:
        body(n - 1)


def pipeline(eng, n, lag, body):
    start = lag + 1 + (lag + 1) % 2
    for i in range(min(start, n + lag)):
        body(i, i % 2)
    loops = (n - 1 - start) // 2
    end = start
    if loops > 0:
        end = start + 2 * loops
        with eng.Fori(start // 2, end // 2) as k:
            body(2 * k, 0)
            body(2 * k + 1, 1)
    for i in range(end, n + lag):
        body(i, i % 2)


def late(i, q, k, n, step):
    if not isinstance(i, int) or 0 <= i - k < n:
        step(i - k, (q + k) % 2)


def other_at(eng, sem, k, u, n):
    if isinstance(k, int):
        if k < 0:
            return
        k = min(k, n - 1)
    eng.wait_ge(sem, ready(k, u))


def ready(i, u, base=0):
    return 2 * i + (base + u + 1)


def first(i):
    return isinstance(i, int) and i == 0


def free(eng, sem, i, base=0, k=2, ago=1):
    if not isinstance(i, int) or i >= ago:
        landed(eng, sem, k * (i - (ago - 1)) + base)


class Swdge:

    def __init__(self, sem):
        self.sem, self.base = sem, 0

    def end(self, total):
        self.base += total


def landed(eng, s, count):
    if isinstance(s, Swdge):
        eng.wait_ge(s.sem, s.base + count)
    else:
        eng.wait_ge(s, count)


def landed_pair(eng, s, i, q, per):
    landed(eng, s, per // 2 * i + (per - per // 2 * q))


def build(nc, a, out):
    ctx = ExitStack()
    with ctx:
        def sb(name, shape, dt=F32):
            return ctx.enter_context(nc.sbuf_tensor(name, shape, dt))

        def sem(name):
            return ctx.enter_context(nc.semaphore(name))

        def dram(name, shape, dt=F32):
            return nc.dram_tensor(name, shape, dt, kind="Internal").ap()

        x1_tab = dram("x1_tab", (NPAD, D))
        x2_tab = dram("x2_tab", (NPAD, D))
        h1_tab = dram("h1_tab", (NPAD, D))
        x3_tab = dram("x3_tab", (NPAD, D))
        raw_rows = dram("raw_rows", (4, EP))
        meta = [dram(f"meta{k}", (EP, 4)) for k in range(2)]
        key_row = [dram(f"key_row{k}", (1, ROWLEN)) for k in range(2)]
        cnt_row = [dram(f"cnt_row{k}", (1, EP)) for k in range(2)]
        inv_row = dram("inv_row", (1, EP))
        type_row = dram("type_row", (1, EP))
        last_row = dram("last_row", (1, EP))
        inv_tab = dram("inv_tab", (NHI, 1))
        slot_tab = dram("slot_tab", (NHI, 1))
        agg0 = dram("agg_t0", (EG, P, 2 * GR))
        agg1 = dram("agg_t1", (EG, P, GR))
        agg2 = dram("agg_t2", (EG, P, GR))
        agg3 = dram("agg_t3", (EG, P, GR))
        x2_c = dram("x2_c", (EG, P, GR))
        h1_c = dram("h1_c", (EG, P, GR))
        x3_c = dram("x3_c", (EG, P, GR))
        x3src_t = dram("x3src_t", (EG, P, GR))
        d1_t = dram("d1_t", (EG, P, GR))
        d2_t = dram("d2_t", (EG, P, GR))
        d1_tab = dram("d1_tab", (EP + 1, D))

        PS = [ctx.enter_context(nc.psum_tensor(f"ps{b}", [P, GR], F32)) for b in range(8)]
        A = [PS[0], PS[1]]
        H = [[PS[2], PS[3]], [PS[4], PS[5]]]
        B = [PS[6], PS[7]]

        ident = sb("ident", [P, P])
        ones = sb("ones", [P, P])
        mhalf = sb("mhalf", [P, GR])
        before = sb("before", [P, P])
        iota_lo = sb("iota_lo", [P, LO])
        pidx = sb("pidx", [P, 2])
        mask = sb("mask", [P, 7 * P])
        scratch_i = sb("scratch_i", [P, 7 * P], I32)
        W1a = sb("W1a", [P, 2, HID])
        W1bT = sb("W1bT", [P, 2, HID])
        W2a = sb("W2a", [P, 3, HID])
        W2b = sb("W2b", [P, 2, D])
        Wf = sb("Wf", [P, 2, HID])
        b0 = sb("b0", [P, 10])
        b2b_bc = sb("b2b_bc", [P, J, D])
        WL1 = sb("WL1", [P, D])
        Wp = sb("Wp", [P, D])
        bp = sb("bp", [P, 1])
        We = sb("We", [P, NLAYER * NTYPE, D])
        Wih = sb("Wih", [P, NLAYER, 3 * D])
        Whh = sb("Whh", [P, NLAYER, 3 * D])
        bih = sb("bih", [P, NLAYER, 3])
        bhh = sb("bhh", [P, NLAYER, 3])
        brz = sb("brz", [P, NLAYER, 3])
        Wo = sb("Wo", [P, D])
        bo_bc = sb("bo_bc", [P, J, D])
        W3 = sb("W3", [P, 2, D])
        v3 = sb("v3", [P, 2, 16])
        f3 = sb("f3", [P, 64])
        C_bc = sb("C_bc", [P, J, D])
        D_bc = sb("D_bc", [P, J, D])

        ef = sb("ef", [P, 7, ET])
        me = sb("me", [P, ET, 4])
        ix = sb("ix", [P, 9, ET], I32)
        inv_e = sb("inv_e", [P, ET])
        IX_SRC, IX_EDGE, IX_DST, IX_DSTW, IX_SDST, IX_SSRC, IX_SSRCW, IX_SLOT = range(8)

        big = sb("big", [P, 16, GR])
        x2N = [[sb(f"xN{q}{u}", [P, J, D]) for u in range(2)] for q in range(2)]
        xN = x2N[0]
        xT = [sb(f"xT{u}", [P, GR]) for u in range(2)]
        rN = [sb(f"rN{u}", [P, J, D]) for u in range(2)]
        yN = [sb(f"yN{u}", [P, J, D]) for u in range(2)]
        zN = [sb(f"zN{u}", [P, J, D]) for u in range(2)]
        xb = [sb(f"xb{u}", [P, J, D]) for u in range(2)]
        hid2 = [[sb(f"hid{q}{u}", [P, 2, GR]) for u in range(2)] for q in range(2)]
        hid = hid2[0]
        agg = [sb(f"agg{u}", [P, 2, GR]) for u in range(2)]
        r2N = [sb(f"r2N{u}", [P, J, D]) for u in range(2)]
        norm_bufs = [[[sb(f"{n}_{k}{u}", [P, J, w]) for u in range(2)] for n, w in
                      (("stats", 6), ("moments", 2), ("vareps", 1), ("rstd", 1), ("shift", 1))] for k in range(2)]
        st6 = [sb(f"st6{u}", [P, J, 6]) for u in range(2)]
        islot = [sb(f"islot{u}", [P, 4, J], I32) for u in range(2)]
        krow = [sb(f"krow{u}", [P, GR + 4]) for u in range(2)]

        padv = sb("padv", [P, FRONT + D])
        carry = sb("carry", [P, 2])
        stat3 = sb("stat3", [P, NG * 6])
        winb = [sb(f"win{u}", [P, GR + 4]) for u in range(2)]
        sum3 = [sb(f"sum3{u}", [P, 3]) for u in range(2)]
        sums = sb("sums", [P, EG, 3])
        ginv = [sb(f"ginv{u}", [P, J, 1]) for u in range(2)]
        gate, dve_gate, sp_gate = sem("gate"), sem("dve_gate"), sem("sp_gate")
        gat_a, gat_b, sca_a, sca_b = ([Swdge(sem(f"{n}{u}")) for u in range(2)] for n in ("gather_a", "gather_b", "scatter_a", "scatter_b"))
        sets = [[sem(f"even{n}") for n in range(60)], [sem(f"odd{n}") for n in range(60)]]
        phase = [0]

        class Phase:

            def __init__(self):
                self.taken = 0
                self.own = sets[phase[0] % 2]
                self.other = sets[(phase[0] + 1) % 2] if phase[0] else []
                phase[0] += 1

            def sem(self):
                self.taken += 1
                return self.own[self.taken - 1]

            def sems(self, n):
                return [self.sem() for _ in range(n)]

            def clear_other(self, sp):
                for s in self.other:
                    sp.sem_clear(s)

        def group(tab, g, n=1):
            return tab[bass.ds(g * GR, GR), :].rearrange("(p j) d -> p (j d)", j=J)

        def tail(tab):
            return tab[(NG - 1) * GR:N, :].rearrange("(p j) d -> p (j d)", j=J)

        def plane(tab, g):
            return tab[bass.ds(g, 1), :, :].rearrange("g p c -> (g p) c")

        def row_bc(row, start, n):
            return row[0, bass.ds(start, n)].partition_broadcast(P)

        def flat(t):
            return t[:, :, :].rearrange("p j d -> p (j d)")

        ph = Phase()
        w_in, keys_in, consts, ints, floats, tp, tpe, raw_st, iot, made, wf_p, wf_c, mset, raw_out = ph.sems(14)
        raw_i = big[:, 0:3, 0:P].bitcast(I32)
        raw_h = big[:, 3:7, 0:P].bitcast(I32)
        raw_f = big[:, 8:15, 0:P]
        with nc.Block() as block:

            @block.sync
            def _(sp):
                sp.wait_ge(mset, 1)
                for f, name in enumerate(("src", "dst", "edge_type_8")):
                    sp.dma_start(raw_i[0:EFULL, f, :], a[name][0:EFULL * P].rearrange("(t p) -> t p", p=P)).then_inc(keys_in, 16)
                    sp.dma_start(raw_i[EFULL:EFULL + 1, f, 0:E - EFULL * P],
                                 a[name][EFULL * P:E].rearrange("(o p) -> o p", o=1)).then_inc(keys_in, 16)
                loads = [
                    (W1a, a["W1a"].rearrange("(c p) h -> p c h", p=P)), (W1bT, a["W1bT"].rearrange("(c p) h -> p c h", p=P)),
                    (W2a, a["W2a"].rearrange("(c p) h -> p c h", p=P)), (W2b, a["W2b"].rearrange("(c p) h -> p c h", p=P)),
                    (WL1, a["WL1"]), (Wp, a["Wp"]), (We, a["We"].rearrange("t h d -> h t d")),
                    (Wih, a["Wih"].rearrange("l h d -> h l d")), (Whh, a["Whh"].rearrange("l h d -> h l d")),
                    (Wo, a["Wo"]), (W3, a["W3"].rearrange("l h d -> h l d"))]
                for t, src in loads:
                    sp.dma_start(t[:], src).then_inc(w_in, 16)
                sp.wait_ge(raw_st, 1)
                for r, f in enumerate((3, 5, 0, 1)):
                    sp.dma_start(raw_rows[r, :].rearrange("(t p) -> t p", p=P), raw_f[0:ET, f, :]).then_inc(raw_out, 16)
                sp.wait_ge(w_in, 16 * len(loads))
                sp.wait_ge(raw_out, 16 * 4)

            @block.scalar
            def _(act):
                n = [0]

                def load(t, src):
                    act.dma_start(t, src, allow_slow_non_contiguous=True).then_inc(keys_in, 16)
                    n[0] += 1

                for o, name in ((0, "b1a"), (2, "b1b"), (4, "b2a")):
                    load(b0[:, o:o + 2], a[name].rearrange("(c p) -> p c", p=P))
                load(bp[:, :], a["bp"].rearrange("(c p) -> p c", p=P))
                load(bih[:, :, :], a["bih"].rearrange("l (g p) -> p l g", p=P))
                load(bhh[:, :, :], a["bhh"].rearrange("l (g p) -> p l g", p=P))
                for j in range(J):
                    load(b2b_bc[:, j, :], a["b2b"].partition_broadcast(P))
                    load(bo_bc[:, j, :], a["bo"].partition_broadcast(P))
                for l in range(2):
                    for c, name in enumerate(("b", "g", "be", "blank")):
                        load(v3[:, l, c:c + 1], a[f"{name}{l}"].rearrange("(c p) -> p c", p=P))
                    load(v3[:, l, 4:5], a[f"a{l}"].partition_broadcast(P))
                    load(v3[:, l, 5:6], a[f"cb{l}"].partition_broadcast(P))
                    load(v3[:, l, 6:10], a[f"cw{l}"].partition_broadcast(P))
                act.wait_ge(keys_in, 16 * (6 + n[0]))
                act.sem_inc(consts, 1)
                act.wait_ge(wf_p, 1)
                nc.scalar.activation(Wf[:, 0, :], H[0][0][:, 0:HID], ACT.Copy)
                nc.scalar.activation(Wf[:, 1, :], H[0][1][:, 0:HID], ACT.Copy).then_inc(wf_c, 1)
                for f in range(7):
                    act.wait_ge(tp, f + 1)
                    nc.scalar.activation(ef[:, f, :], PS[f % 2][:, 0:ET], ACT.Copy).then_inc(tpe, 1)

            @block.gpsimd
            def _(pool):
                nc.gpsimd.iota(scratch_i[:, 0:LO], [[1, LO]], base=0, channel_multiplier=0).then_inc(iot, 1)
                nc.gpsimd.iota(scratch_i[:, LO:LO + 2], [[P, 2]], base=0, channel_multiplier=1).then_inc(iot, 1)
                pool.wait_ge(iot, 2)
                nc.gpsimd.tensor_copy(iota_lo[:, :], scratch_i[:, 0:LO])
                nc.gpsimd.tensor_copy(pidx[:, :], scratch_i[:, LO:LO + 2]).then_inc(iot, 1)
                nc.gpsimd.memset(mhalf[:, :], -0.5)
                nc.gpsimd.memset(ident[:, :], 0.0)
                nc.gpsimd.memset(before[:, :], 1.0)
                nc.gpsimd.memset(mask[:, :], 1.0)
                nc.gpsimd.memset(ones[:, :], 1.0).then_inc(iot, 1)
                pool.wait_ge(iot, 4)
                nc.gpsimd.affine_select(out=ident[:, :], in_=ident[:, :], compare_op=ALU.not_equal, fill=1.0, base=0,
                                        pattern=[[-1, P]], channel_multiplier=1)
                nc.gpsimd.affine_select(out=before[:, :], in_=before[:, :], compare_op=ALU.is_gt, fill=0.0, base=0,
                                        pattern=[[1, P]], channel_multiplier=-1)
                nc.gpsimd.affine_select(out=mask[:, :], in_=mask[:, :], compare_op=ALU.is_gt, fill=0.0, base=3 * P,
                                        pattern=[[-1, 7 * P]], channel_multiplier=1).then_inc(made, 1)
                nc.gpsimd.iota(scratch_i[:, 0:ET], [[P, ET]], base=0, channel_multiplier=1).then_inc(iot, 1)
                pool.wait_ge(iot, 5)
                nc.gpsimd.tensor_copy(me[:, :, 3], scratch_i[:, 0:ET]).then_inc(iot, 1)
                pool.wait_ge(iot, 6)

            @block.vector
            def _(dve):
                nc.vector.memset(raw_i[:, :, :], PADKEY).then_inc(mset, 1)
                dve.wait_ge(keys_in, 16 * 6)
                dve.wait_ge(consts, 1)
                for k in range(2):
                    nc.vector.tensor_scalar(raw_h[:, 2 * k, :], raw_i[:, k, :], 8, None, ALU.arith_shift_right)
                    nc.vector.tensor_scalar(raw_h[:, 2 * k + 1, :], raw_i[:, k, :], LO - 1, None, ALU.bitwise_and).then_inc(ints, 1)
                dve.wait_ge(ints, 2)
                nc.vector.tensor_copy(raw_f[:, 0:3, :], raw_i[:, :, :])
                nc.vector.tensor_copy(raw_f[:, 3:7, :], raw_h[:, :, :]).then_inc(raw_st, 1)
                nc.vector.tensor_tensor(brz[:, :, :], bih[:, :, :], bhh[:, :, :], ADD).then_inc(floats, 1)
                dve.wait_ge(wf_p, 1)
                nc.vector.tensor_tensor(b0[:, 6:8], b0[:, 4:6], B[0][:, 0:2], ADD).then_inc(floats, 1)
                dve.wait_ge(tpe, 3)
                nc.vector.tensor_copy(me[:, :, 0:3].rearrange("p t f -> p f t"), ef[:, 0:3, :]).then_inc(floats, 1)
                dve.wait_ge(floats, 3)

            @block.tensor
            def _(pe):
                pe.wait_ge(made, 1)
                pe.wait_ge(raw_st, 1)
                for f in range(7):
                    if f >= 2:
                        pe.wait_ge(tpe, f - 1)
                    if f == 0:
                        pe.wait_ge(consts, 1)
                        pe.wait_ge(w_in, 16 * 11)
                        for c in range(2):
                            for q in range(2):
                                nc.tensor.matmul(H[0][c][:, 0:HID], W1bT[:, q, c * P:(c + 1) * P], W2a[:, 1 + q, :],
                                                 start=(q == 0), stop=(q == 1))
                        for c in range(2):
                            for q in range(2):
                                last = nc.tensor.matmul(B[0][:, c:c + 1], W2a[:, 1 + q, c * P:(c + 1) * P], b0[:, 2 + q:3 + q],
                                                        start=(q == 0), stop=(q == 1))
                        last.then_inc(wf_p, 1)
                    nc.tensor.transpose(PS[f % 2][:, 0:ET], raw_f[0:ET, f, :], ident[0:ET, 0:ET]).then_inc(tp, 1)

        ph = Phase()
        hot, hist, cum, tot, tots, off, offs, start_, tabs, tab_st, inv1, slot1, slot2, jg = ph.sems(14)
        one_lo = [big[:, 2 * k, :].bitcast(BF16).rearrange("p (j c) -> p j c", j=J) for k in range(2)]
        one_hi = [big[:, 2 * k + 1, :].bitcast(BF16).rearrange("p (j c) -> p j c", j=J) for k in range(2)]
        R = big[:, 4:6, :].rearrange("p k (h c) -> p k h c", h=2)
        cumul = big[:, 6:8, :].rearrange("p k (h c) -> p k h c", h=2)
        count = big[:, 8:10, :].rearrange("p k (h c) -> p k h c", h=2)
        inv_w = big[:, 10, :].rearrange("p (h c) -> p h c", h=2)
        slot_w = big[:, 11, :].rearrange("p (h c) -> p h c", h=2)
        has_w = big[:, 12, :].rearrange("p (h c) -> p h c", h=2)
        rowtot = f3[:, 0:4]
        lowtot = f3[:, 4:8]
        offset = f3[:, 8:12]

        def one_hots(dve, i, k, done):
            for j in range(J):
                nc.vector.tensor_scalar(one_hi[k][:, j, :], iota_lo[:, :], ef[:, 3 + 2 * k, bass.ds(J * i + j, 1)], None, EQ)
                last = nc.vector.tensor_scalar(one_lo[k][:, j, :], iota_lo[:, :], ef[:, 4 + 2 * k, bass.ds(J * i + j, 1)], None, EQ)
            last.then_inc(done, 1)

        with nc.Block() as block:

            @block.sync
            def _(sp):
                ph.clear_other(sp)
                sp.wait_ge(tabs, 1)
                sp.dma_start(inv_tab.rearrange("(h p c) o -> p h (c o)", h=2, p=P), inv_w).then_inc(tab_st, 16)
                sp.wait_ge(tabs, 2)
                sp.dma_start(slot_tab.rearrange("(h p c) o -> p h (c o)", h=2, p=P), slot_w).then_inc(tab_st, 16)
                sp.wait_ge(tab_st, 32)

            @block.vector
            def _(dve):
                def body(i):
                    for k in range(2):
                        free(dve, hist, i)
                        one_hots(dve, i, k, hot)

                pairs(dve, EG, body, last=True)
                dve.wait_ge(hist, 2 * EG)
                for k in range(2):
                    for h in range(2):
                        nc.vector.tensor_copy(count[:, k, h, :], PS[2 * k + h][:, 0:LO])
                        last = nc.vector.tensor_tensor_scan(cumul[:, k, h, :], mask[:, 0:LO], PS[2 * k + h][:, 0:LO], 0.0, MUL, ADD)
                last.then_inc(cum, 1)
                dve.wait_ge(cum, 1)
                for k in range(2):
                    nc.vector.tensor_copy(rowtot[:, 2 * k:2 * k + 2], cumul[:, k, :, LO - 1])
                    nc.vector.tensor_copy(lowtot[:, 2 * k + 1:2 * k + 2], cumul[:, k, 0, LO - 1:LO])
                    last = nc.vector.memset(lowtot[:, 2 * k:2 * k + 1], 0.0)
                last.then_inc(tot, 1)
                dve.wait_ge(off, 1)
                nc.vector.tensor_copy(offset, B[0][:, 0:4]).then_inc(offs, 1)
                dve.wait_ge(offs, 1)
                for k in range(2):
                    for h in range(2):
                        last = nc.vector.scalar_tensor_tensor(R[:, k, h, :], cumul[:, k, h, :], offset[:, 2 * k + h:2 * k + h + 1],
                                                              count[:, k, h, :], ADD, SUB)
                last.then_inc(start_, 1)
                nc.vector.tensor_scalar(has_w, count[:, 1, :, :], 0.0, None, ALU.is_gt).then_inc(slot1, 1)
                dve.wait_ge(start_, 1)
                nc.vector.tensor_scalar(slot_w, R[:, 1, :, :], -1.0, -1.0, MUL, ADD).then_inc(slot1, 1)
                dve.wait_ge(slot1, 2)
                nc.vector.tensor_tensor(slot_w, slot_w, has_w, MUL).then_inc(slot2, 1)
                dve.wait_ge(slot2, 1)
                dve.wait_ge(tabs, 1)
                nc.vector.tensor_scalar(slot_w, slot_w, float(EP), None, ADD).then_inc(tabs, 1)

            @block.gpsimd
            def _(pool):
                pool.wait_ge(cum, 1)
                nc.gpsimd.tensor_scalar(inv_w, count[:, 0, :, :], 1.0, None, ADD).then_inc(inv1, 1)
                pool.wait_ge(inv1, 1)
                nc.gpsimd.tensor_tensor(inv_w, inv_w, mhalf[:, :].rearrange("p (h c) -> p h c", h=2), ALU.pow).then_inc(tabs, 1)

            @block.tensor
            def _(pe):
                def body(i):
                    for k in range(2):
                        pe.wait_ge(hot, 2 * i + k + 1)
                        for j in range(J):
                            for h in range(2):
                                last = nc.tensor.matmul(PS[2 * k + h][:, 0:LO], one_hi[k][:, j, h * P:(h + 1) * P], one_lo[k][:, j, :],
                                                        start=(first(i) and j == 0),
                                                        stop=(isinstance(i, int) and i == EG - 1 and j == J - 1))
                        last.then_inc(hist, 1)

                pairs(pe, EG, body, last=True)
                pe.wait_ge(tot, 1)
                nc.tensor.matmul(B[0][:, 0:4], before[:, :], rowtot, start=True, stop=False)
                nc.tensor.matmul(B[0][:, 0:4], ones[:, :], lowtot, start=False, stop=True).then_inc(off, 1)

        ph = Phase()
        hot, hotT, looked, counted, based, eqd, radd, ranked, base_w = ph.sems(9)
        stored = sca_a
        rows_in = ph.sems(2)
        hi_bc = [krow[k][:, 0:GR] for k in range(2)]
        key_bc = [xT[k] for k in range(2)]
        hotTs = [hid[k] for k in range(2)]
        base = [f3[:, 16 + 4 * k:20 + 4 * k] for k in range(2)]
        within = [f3[:, 24 + 4 * k:28 + 4 * k] for k in range(2)]
        rankf = [f3[:, 32 + 4 * k:36 + 4 * k] for k in range(2)]
        mslot = [st6[k][:, :, 0:4] for k in range(2)]
        junk_eq = [big[:, 10 + 3 * k:13 + 3 * k, :].rearrange("p a b -> p (a b)") for k in range(2)]
        junk_lo = [[flat(t[j // 2])[:, (j % 2) * LO:(j % 2 + 1) * LO] for j in range(J)] for t in (yN, zN)]
        with nc.Block() as block:

            @block.sync
            def _(sp):
                ph.clear_other(sp)

                def body(i):
                    for k in range(2):
                        free(sp, eqd, i)
                        free(sp, hotT, i)
                        sp.dma_start(hi_bc[k], raw_rows[k, bass.ds(i * GR, GR)].partition_broadcast(P)).then_inc(rows_in[k], 16)
                        sp.dma_start(key_bc[k][:, :], raw_rows[2 + k, bass.ds(i * GR, GR)].partition_broadcast(P)).then_inc(rows_in[k], 16)

                pairs(sp, EG, body)

            @block.vector
            def _(dve):
                def body(i):
                    for k in range(2):
                        free(dve, counted, i)
                        one_hots(dve, i, k, hot)
                    for k in range(2):
                        dve.wait_ge(rows_in[k], 32 * i + 32)
                        free(dve, looked, i)
                        for h in range(2):
                            last = nc.vector.tensor_scalar(hotTs[k][:, h, :], hi_bc[k], pidx[:, h:h + 1], None, EQ)
                        last.then_inc(hotT, 1)
                    for k in range(2):
                        for j in range(J):
                            w = (j + 1) * P
                            last = nc.vector.scalar_tensor_tensor(junk_eq[k][:, j * w // 2:j * w // 2 + w], key_bc[k][:, 0:w], ef[:, k, bass.ds(J * i + j, 1)],
                                                                  mask[:, (3 - j) * P:(3 - j) * P + w], EQ, MUL,
                                                                  accum_out=within[k][:, j:j + 1])
                        last.then_inc(eqd, 1)
                    for k in range(2):
                        dve.wait_ge(looked, 2 * i + k + 1)
                        free(dve, ranked, i)
                        for j in range(J):
                            last = nc.vector.scalar_tensor_tensor(junk_lo[k][j], PS[2 * k + j // 2][:, (j % 2) * LO:(j % 2 + 1) * LO], 1.0,
                                                                  one_lo[k][:, j, :], MUL, MUL, accum_out=base[k][:, j:j + 1])
                        last.then_inc(based, 1)
                        dve.wait_ge(counted, 2 * i + k + 1)
                        nc.vector.tensor_tensor(R[:, k, :, :], R[:, k, :, :], PS[4 + k][:, :].rearrange("p (h c) -> p h c", h=2), ADD).then_inc(radd, 1)
                    for k in range(2):
                        dve.wait_ge(based, 2 * i + k + 1)
                        dve.wait_ge(eqd, 2 * i + k + 1)
                        nc.vector.tensor_tensor(rankf[k], base[k], within[k], ADD).then_inc(base_w, 1)
                    for k in range(2):
                        dve.wait_ge(base_w, 2 * i + k + 1)
                        free(dve, stored[k], i, k=16 * J)
                        nc.vector.tensor_scalar(islot[k][:, 0, :], rankf[k], -1.0, float(EP - 1), MUL, ADD)
                        nc.vector.tensor_copy(mslot[k], me[:, bass.ds(J * i, J), :]).then_inc(ranked, 1)

                pairs(dve, EG, body)

            @block.tensor
            def _(pe):
                def body(i):
                    for k in range(2):
                        pe.wait_ge(hotT, 2 * i + k + 1)
                        pe.wait_ge(hot, 2 * i + k + 1)
                        free(pe, radd, i)
                        for j in range(J):
                            for h in range(2):
                                last = nc.tensor.matmul(PS[2 * k + j // 2][:, (j % 2) * LO:(j % 2 + 1) * LO],
                                                        hotTs[k][:, h, j * P:(j + 1) * P], R[:, k, h, :], start=(h == 0), stop=(h == 1))
                        last.then_inc(looked, 1)
                        for h in range(2):
                            for j in range(J):
                                last = nc.tensor.matmul(PS[4 + k][:, h * LO:(h + 1) * LO], one_hi[k][:, j, h * P:(h + 1) * P],
                                                        one_lo[k][:, j, :], start=(j == 0), stop=(j == J - 1))
                        last.then_inc(counted, 1)

                pairs(pe, EG, body)

            @block.gpsimd
            def _(pool):
                def body(i):
                    for k in range(2):
                        pool.wait_ge(ranked, 2 * i + k + 1)
                        pool.sem_inc(gate, 1)
                        for j in range(J):
                            nc.gpsimd.indirect_dma_start(meta[k], bass.IndirectOffsetOnAxis(ap=islot[k][:, 0, j:j + 1], axis=0),
                                                         mslot[k][:, j, :], None).then_inc(stored[k].sem, 16)

                pairs(pool, EG, body)
                for k in range(2):
                    landed(pool, stored[k], EG * J * 16)

        for s in stored:
            s.end(16 * J * EG)

        ph = Phase()
        (m_in, row_c, row_st, lin_in, same_d, cnt_d, cnt_st, nxt_in, cnt_in, edge_d, inv_d, fix, tpd, tpc, idx_a, idx_b,
         row_st2, pads, zrow, ends) = ph.sems(20)
        meta_r = [big[0:ET, 0, :], big[0:ET, 1, :]]
        fields = lambda k, f: meta_r[k].rearrange("t (p f) -> t f p", f=4)[:, f, :]
        keyc = big[0:ET, 2, :].rearrange("t (k p) -> t k p", p=P)
        aux = big[0:ET, 3, :].rearrange("t (k p) -> t k p", p=P)
        scat = big[0:ET, 4, :].rearrange("t (k p) -> t k p", p=P)
        others = big[0:ET, 5, :].rearrange("t (k p) -> t k p", p=P)
        HALF = EP // 2
        half_ctx = nc.sbuf_tensor("line_buf", [1, 2 * HALF + 8], F32)
        line_buf = half_ctx.__enter__()
        line = line_buf[0:1, 0:HALF + 1]
        sameline = line_buf[0:1, HALF + 4:2 * HALF + 4]
        cntline = line_buf[0:1, 0:HALF]
        KD, KS = 1, 0
        with nc.Block() as block:

            @block.sync
            def _(sp):
                ph.clear_other(sp)
                for k in range(2):
                    sp.dma_start(meta_r[k], meta[k].rearrange("(t p) f -> t (p f)", p=P)).then_inc(m_in, 16)
                sp.wait_ge(row_c, 1)
                for k, f in ((KD, 0), (KS, 1)):
                    sp.dma_start(key_row[k][0, FRONT:FRONT + EP].rearrange("(t p) -> t p", p=P), keyc[:, f, :]).then_inc(row_st, 16)
                sp.dma_start(type_row[0, :].rearrange("(t p) -> t p", p=P), keyc[:, 2, :]).then_inc(row_st, 16)
                sp.wait_ge(pads, 1)
                for k in range(2):
                    sp.dma_start(key_row[k][0:1, 0:FRONT], padv[0:1, 0:FRONT]).then_inc(row_st, 16)
                    sp.dma_start(key_row[k][0:1, FRONT + EP:ROWLEN], padv[0:1, 0:FRONT]).then_inc(row_st, 16)
                sp.dma_start(d1_tab[EP:EP + 1, :], padv[0:1, FRONT:FRONT + D]).then_inc(row_st, 16)
                sp.wait_ge(row_st, 16 * 8)
                for n, k in enumerate((KD, KS)):
                    sp.dma_start(aux[:, n, :], key_row[k][0, FRONT + 1:FRONT + 1 + EP].rearrange("(t p) -> t p", p=P)).then_inc(nxt_in, 16)
                for n, k in enumerate((KD, KS)):
                    for c in range(2):
                        if n or c:
                            sp.wait_ge(cnt_st, 16 * (2 * n + c))
                            sp.wait_ge(zrow, 2 * n + c + 1)
                        at = FRONT - 1 + c * HALF
                        sp.dma_start(line, key_row[k][0:1, at:at + HALF + 1]).then_inc(lin_in, 16)
                        sp.wait_ge(cnt_d, 2 * n + c + 1)
                        sp.dma_start(cnt_row[k][0:1, c * HALF:(c + 1) * HALF], cntline).then_inc(cnt_st, 16)
                sp.wait_ge(cnt_st, 64)
                sp.dma_start(aux[:, 3, :], cnt_row[KD][0, :].rearrange("(t p) -> t p", p=P)).then_inc(cnt_in, 16)
                sp.dma_start(scat[:, 2, :], cnt_row[KS][0, :].rearrange("(t p) -> t p", p=P)).then_inc(cnt_in, 16)
                sp.wait_ge(inv_d, 1)
                sp.dma_start(inv_row[0, :].rearrange("(t p) -> t p", p=P), aux[:, 3, :]).then_inc(row_st2, 16)
                sp.wait_ge(edge_d, 1)
                sp.dma_start(last_row[0, :].rearrange("(t p) -> t p", p=P), keyc[:, 3, :]).then_inc(row_st2, 16)
                sp.wait_ge(row_st2, 32)

            @block.vector
            def _(dve):
                nc.vector.memset(padv[:, 0:FRONT], -1.0)
                nc.vector.memset(padv[:, FRONT:], 0.0).then_inc(pads, 1)
                dve.wait_ge(m_in, 32)
                nc.vector.tensor_copy(keyc[:, 0, :], fields(KD, 1))
                nc.vector.tensor_copy(keyc[:, 1, :], fields(KS, 0))
                nc.vector.tensor_copy(keyc[:, 2, :], fields(KD, 2)).then_inc(row_c, 1)
                nc.vector.tensor_copy(scat[:, 3, :], fields(KD, 3))
                nc.vector.tensor_copy(others[:, 0, :], fields(KD, 0))
                nc.vector.tensor_copy(others[:, 1, :], fields(KS, 1)).then_inc(fix, 1)
                dve.wait_ge(nxt_in, 32)
                dve.wait_ge(row_c, 1)
                nc.vector.tensor_tensor(aux[:, 0, :], keyc[:, 0, :], aux[:, 0, :], ALU.not_equal).then_inc(ends, 1)
                dve.wait_ge(ends, 1)
                nc.vector.scalar_tensor_tensor(keyc[:, 3, :], keyc[:, 0, :], float(N), aux[:, 0, :], ALU.is_lt, MUL)
                nc.vector.tensor_tensor(aux[:, 2, :], keyc[:, 1, :], aux[:, 1, :], ALU.not_equal).then_inc(edge_d, 1)
                dve.wait_ge(edge_d, 1)
                nc.vector.tensor_scalar(scat[:, 0, :], keyc[:, 3, :], -float(SKIP), float(SKIP), MUL, ADD)
                nc.vector.tensor_scalar(scat[:, 1, :], aux[:, 2, :], -float(SKIP), float(SKIP), MUL, ADD).then_inc(idx_a, 1)
                dve.wait_ge(idx_a, 1)
                nc.vector.tensor_tensor(scat[:, 0, :], scat[:, 0, :], keyc[:, 0, :], ADD)
                nc.vector.tensor_tensor(scat[:, 1, :], scat[:, 1, :], keyc[:, 1, :], ADD).then_inc(idx_a, 1)
                dve.wait_ge(idx_a, 2)
                dve.sem_inc(fix, 1)
                nc.vector.memset(carry[:, :], 0.0).then_inc(zrow, 1)
                for n in range(4):
                    dve.wait_ge(lin_in, 16 * (n + 1))
                    nc.vector.tensor_tensor(sameline, line_buf[0:1, 1:HALF + 1], line_buf[0:1, 0:HALF], EQ).then_inc(same_d, 1)
                    dve.wait_ge(same_d, n + 1)
                    dve.wait_ge(zrow, n + 1)
                    nc.vector.tensor_tensor_scan(cntline, sameline, ones[0:1, 0:1].broadcast_to([1, HALF]), carry[0:1, 0:1], MUL, ADD).then_inc(cnt_d, 1)
                    dve.wait_ge(cnt_d, n + 1)
                    nc.vector.tensor_copy(carry[0:1, 0:1], cntline[:, HALF - 1:HALF]).then_inc(zrow, 1)
                dve.wait_ge(cnt_in, 32)
                nc.vector.reciprocal(aux[:, 3, :], aux[:, 3, :]).then_inc(inv_d, 1)
                dve.sem_inc(fix, 1)
                for n, (dst_ix, bound) in enumerate(((IX_SRC, N - 1), (IX_DST, N - 1), (IX_EDGE, E - 1), (IX_DSTW, None),
                                                     (IX_SDST, N - 1), (IX_SSRC, N - 1), (IX_SSRCW, None))):
                    dve.wait_ge(tpd, n + 1)
                    if bound is None:
                        last = nc.vector.tensor_copy(ix[:, dst_ix, :], PS[n % 2][:, 0:ET])
                    else:
                        last = nc.vector.tensor_scalar(ix[:, dst_ix, :], PS[n % 2][:, 0:ET], float(bound), None, MIN)
                    last.then_inc(tpc, 1)
                dve.wait_ge(tpd, 8)
                nc.vector.tensor_scalar(inv_e[:, :], PS[1][:, 0:ET], 1.0, None, ADD).then_inc(tpc, 1)

            @block.gpsimd
            def _(pool):
                pool.wait_ge(tpc, 8)
                nc.gpsimd.tensor_tensor(inv_e[:, :], inv_e[:, :], mhalf[:, 0:ET], ALU.pow).then_inc(idx_b, 1)
                pool.wait_ge(idx_b, 1)

            @block.tensor
            def _(pe):
                pe.wait_ge(fix, 2)
                srcs = (others[:, 0, :], keyc[:, 0, :], scat[:, 3, :], scat[:, 0, :], others[:, 1, :], keyc[:, 1, :], scat[:, 1, :], scat[:, 2, :])
                for n, src in enumerate(srcs):
                    if n >= 2:
                        pe.wait_ge(tpc, n - 1)
                    if n == 7:
                        pe.wait_ge(cnt_in, 32)
                    nc.tensor.transpose(PS[n % 2][:, 0:ET], src, ident[0:ET, 0:ET]).then_inc(tpd, 1)

        half_ctx.__exit__(None, None, None)
        def elu_steps(dve, i, src, bias, acts, t, tdone, done):
            for u in range(2):
                dve.wait_ge(acts, ready(i, u))
                nc.vector.tensor_scalar(t[u][:, :, :], t[u][:, :, :], 1.0, -1.0, MIN, ADD).then_inc(tdone, 1)
            for u in range(2):
                dve.wait_ge(tdone, ready(i, u))
                for h in range(2):
                    last = nc.vector.scalar_tensor_tensor(t[u][:, h, :], src[u][h][:, :], bias[h], t[u][:, h, :], ADD, MAX)
                last.then_inc(done, 1)

        ph = Phase()
        ixd, tpd, cpd, hidd, expd, tmin, elud, samed, scand, scaled = ph.sems(10)
        gx, ge = gat_a, gat_b
        kin, iin, aout = (ph.sems(2) for _ in range(3))
        eaT = [flat(zN[u]) for u in range(2)]
        inv_bc = [flat(rN[u]) for u in range(2)]
        same = [flat(xb[u]) for u in range(2)]
        mean = [big[:, 2 * u:2 * u + 2, :] for u in range(2)]
        with nc.Block() as block:

            @block.sync
            def _(sp):
                ph.clear_other(sp)

                def body(i):
                    for u in range(2):
                        free(sp, samed, i)
                        free(sp, scaled, i)
                        g = 2 * i + u
                        sp.dma_start(krow[u][:, 0:GR + 1], row_bc(key_row[1], g * GR + FRONT - 1, GR + 1)).then_inc(kin[u], 16)
                        sp.dma_start(inv_bc[u], row_bc(inv_row, g * GR, GR)).then_inc(iin[u], 16)
                    for u in range(2):
                        sp.wait_ge(scaled, ready(i, u))
                        sp.dma_start(plane(agg0, 2 * i + u), mean[u].rearrange("p h c -> p (h c)")).then_inc(aout[u], 16)

                pairs(sp, EPAIR, body)
                for u in range(2):
                    sp.wait_ge(aout[u], 16 * EPAIR)

            @block.gpsimd
            def _(pool):
                def body(i):
                    for u in range(2):
                        free(pool, gx[u], i, k=16 * J)
                        free(pool, ge[u], i, k=16 * J)
                        free(pool, tpd, i)
                        pool.sem_inc(gate, 1)
                        for n, which in enumerate((IX_SRC, IX_EDGE)):
                            last = nc.gpsimd.tensor_copy(islot[u][:, n, :], ix[:, which, bass.ds((2 * i + u) * J, J)])
                        last.then_inc(ixd, 1)
                        pool.wait_ge(ixd, ready(i, u))
                        pool.sem_inc(gate, 1)
                        for j in range(J):
                            nc.gpsimd.indirect_dma_start(xN[u][:, j, :], None, a["x"],
                                                         bass.IndirectOffsetOnAxis(ap=islot[u][:, 0, j:j + 1], axis=0)).then_inc(gx[u].sem, 16)
                            nc.gpsimd.indirect_dma_start(yN[u][:, j, :], None, a["edge_attr"],
                                                         bass.IndirectOffsetOnAxis(ap=islot[u][:, 1, j:j + 1], axis=0)).then_inc(ge[u].sem, 16)

                pairs(pool, EPAIR, body)

            @block.tensor
            def _(pe):
                def body(i):
                    for u in range(2):
                        landed(pe, gx[u], 16 * J * i + 16 * J)
                        landed(pe, ge[u], 16 * J * i + 16 * J)
                        free(pe, cpd, i)
                        for j in range(J):
                            nc.tensor.transpose(A[u][:, j * P:(j + 1) * P], xN[u][:, j, :], ident[:, :])
                            last = nc.tensor.transpose(B[u][:, j * P:(j + 1) * P], yN[u][:, j, :], ident[:, :])
                        last.then_inc(tpd, 1)
                    for u in range(2):
                        pe.wait_ge(cpd, ready(i, u))
                        free(pe, elud, i)
                        for h in range(2):
                            nc.tensor.matmul(H[u][h][:, :], W1a[:, 0, h * P:(h + 1) * P], xT[u][:, :], start=True, stop=False)
                            last = nc.tensor.matmul(H[u][h][:, :], W1a[:, 1, h * P:(h + 1) * P], eaT[u], start=False, stop=True)
                        last.then_inc(hidd, 1)

                pairs(pe, EPAIR, body)

            @block.scalar
            def _(act):
                def body(i):
                    for u in range(2):
                        act.wait_ge(tpd, ready(i, u))
                        free(act, hidd, i)
                        nc.scalar.activation(xT[u][:, :], A[u][:, :], ACT.Copy)
                        nc.scalar.activation(eaT[u], B[u][:, :], ACT.Copy).then_inc(cpd, 1)
                    for u in range(2):
                        act.wait_ge(hidd, ready(i, u))
                        free(act, scand, i, 1)
                        for h in range(2):
                            last = nc.scalar.activation(hid[u][:, h, :], H[u][h][:, :], ACT.Exp, bias=b0[:, h:h + 1])
                        last.then_inc(expd, 1)

                pairs(act, EPAIR, body)

            @block.vector
            def _(dve):
                nc.vector.memset(agg[1][:, :, :], 0.0).then_inc(scand, 1)

                def body(i):
                    for u in range(2):
                        dve.wait_ge(kin[u], 16 * i + 16)
                        nc.vector.tensor_tensor(same[u], krow[u][:, 1:GR + 1], krow[u][:, 0:GR], EQ).then_inc(samed, 1)
                    elu_steps(dve, i, H, [b0[:, h:h + 1] for h in range(2)], expd, hid, tmin, elud)
                    for u in range(2):
                        dve.wait_ge(samed, ready(i, u))
                        dve.wait_ge(elud, ready(i, u))
                        dve.wait_ge(scand, ready(i, u))
                        for h in range(2):
                            last = nc.vector.tensor_tensor_scan(agg[u][:, h, :], same[u], hid[u][:, h, :],
                                                                agg[1 - u][:, h, GR - 1:GR], MUL, ADD)
                        last.then_inc(scand, 1)
                    for u in range(2):
                        dve.wait_ge(scand, ready(i, u, 1))
                        dve.wait_ge(iin[u], 16 * i + 16)
                        free(dve, aout[u], i, k=16)
                        for h in range(2):
                            last = nc.vector.tensor_tensor(mean[u][:, h, :], agg[u][:, h, :], inv_bc[u], MUL)
                        last.then_inc(scaled, 1)

                pairs(dve, EPAIR, body)

        for s in (*gx, *ge):
            s.end(16 * J * EPAIR)

        class Norm:

            def __init__(self, ph, r, y, bufs=0):
                self.r, self.y = r, y
                self.stats, self.moments, self.eps, self.rstd, self.shift, self.done = ph.sems(6)
                self.st, self.mv, self.ve, self.rs, self.sh = norm_bufs[bufs]

            def moments_steps(self, dve, i, rdone):
                for u in range(2):
                    dve.wait_ge(rdone, ready(i, u))
                    free(dve, self.moments, i)
                    for j in range(J):
                        last = nc.vector.bn_stats(self.st[u][:, j, :], self.r[u][:, j, :])
                    last.then_inc(self.stats, 1)
                for u in range(2):
                    dve.wait_ge(self.stats, ready(i, u))
                    free(dve, self.done, i)
                    dve.sem_inc(dve_gate, 1)
                    for j in range(J):
                        last = nc.vector.bn_aggr(self.mv[u][:, j, :], self.st[u][:, j, :])
                    last.then_inc(self.moments, 1)

            def rstd_steps(self, pool, i, shift=False):
                for u in range(2):
                    pool.wait_ge(self.moments, ready(i, u))
                    pool.sem_inc(gate, 1)
                    last = nc.gpsimd.tensor_scalar(self.ve[u][:, :, 0], self.mv[u][:, :, 1], EPS, None, ADD)
                    if shift:
                        last = nc.gpsimd.tensor_scalar(self.sh[u][:, :, 0], self.mv[u][:, :, 0], -1.0, None, MUL)
                    last.then_inc(self.eps, 1)
                for u in range(2):
                    pool.wait_ge(self.eps, ready(i, u))
                    nc.gpsimd.tensor_tensor(self.rs[u][:, :, 0], self.ve[u][:, :, 0], mhalf[:, 0:J], ALU.pow).then_inc(self.rstd, 1)
                if shift:
                    for u in range(2):
                        pool.wait_ge(self.rstd, ready(i, u))
                        nc.gpsimd.tensor_tensor(self.sh[u][:, :, 0], self.sh[u][:, :, 0], self.rs[u][:, :, 0], MUL).then_inc(self.shift, 1)

            def scale_steps(self, dve, i, out_free=None):
                for u in range(2):
                    dve.wait_ge(self.rstd, ready(i, u))
                    if out_free:
                        out_free(dve, i, u)
                    for j in range(J):
                        last = nc.vector.tensor_scalar(self.y[u][:, j, :], self.r[u][:, j, :], self.mv[u][:, j, 0:1], self.rs[u][:, j, :], SUB, MUL)
                    last.then_inc(self.done, 1)

            def act_scale_steps(self, act, i, out_free=None):
                for u in range(2):
                    act.wait_ge(self.shift, ready(i, u))
                    if out_free:
                        out_free(act, i, u)
                    for j in range(J):
                        last = nc.scalar.activation(self.y[u][:, j, :], self.r[u][:, j, :], ACT.Identity, scale=self.rs[u][:, j, :], bias=self.sh[u][:, j, :])
                    last.then_inc(self.done, 1)

        def rows_gather(pool, u, dst, table, slot, done):
            for j in range(J):
                nc.gpsimd.indirect_dma_start(dst[u][:, j, :], None, table, bass.IndirectOffsetOnAxis(ap=islot[u][:, slot, j:j + 1], axis=0)).then_inc(done[u].sem, 16)

        def rows_scatter(pool, u, src, table, slot, done):
            for j in range(J):
                nc.gpsimd.indirect_dma_start(table, bass.IndirectOffsetOnAxis(ap=islot[u][:, slot, j:j + 1], axis=0), src[u][:, j, :], None,
                                             bounds_check=N - 1, oob_is_err=False).then_inc(done[u].sem, 16)

        def indices(pool, i, u, done, *lists, slot=0):
            for n, which in enumerate(lists):
                last = nc.gpsimd.tensor_copy(islot[u][:, slot + n, :], ix[:, which, bass.ds((2 * i + u) * J, J)])
            last.then_inc(done, 1)
            pool.wait_ge(done, ready(i, u))
            pool.sem_inc(gate, 1)

        def ends(gathers):
            for q in range(2):
                for s in gathers[q]:
                    s.end(16 * J * ((EPAIR + 1 - q) // 2))

        def transposes(dst, src, u):
            for j in range(J):
                last = nc.tensor.transpose(dst[u][:, j * P:(j + 1) * P], src[u][:, j, :], ident[:, :])
            return last

        def back_product(dst, lhs, rhs, u):
            for j in range(J):
                for c in range(len(lhs)):
                    last = nc.tensor.matmul(dst[u][:, j * P:(j + 1) * P], lhs[c][:, j * P:(j + 1) * P], rhs[c],
                                            start=(c == 0), stop=(c == len(lhs) - 1))
            return last

        for edge in (False, True):
            n_pairs = EPAIR if edge else NPAIR
            ph = Phase()
            tpd, cpd, hidd, expd, tmin, elud, xbd, y1d, r1d, tp1d, cp1d, y2d, r2d, ixd, ixd1, ixd2 = ph.sems(16)
            ain = ph.sems(2)
            o1, o2 = (sca_a, sca_b) if edge else (ph.sems(2) for _ in range(2))
            xin = (gat_a, gat_b) if edge else (ph.sems(2), ph.sems(2))
            norm1, norm2 = Norm(ph, rN, yN, 0), Norm(ph, r2N, zN, 1)
            bias = [b0[:, 4 + 2 * edge + h:5 + 2 * edge + h] for h in range(2)]
            per = 16 * J if edge else 16
            x1T = [big[:, u, :] for u in range(2)]
            L0, L1, L2, L3, L4 = range(1, 6)
            with nc.Block() as block:

                @block.sync
                def _(sp):
                    ph.clear_other(sp)

                    def load(i, q):
                        for u in range(2):
                            g = 2 * i + u
                            if edge:
                                free(sp, hidd, i)
                                sp.dma_start(agg[u][:, :, :].rearrange("p h c -> p (h c)"), plane(agg0, g)).then_inc(ain[u], 16)
                                continue
                            free(sp, xbd, i, ago=2)
                            free(sp, tpd, i, ago=2)
                            if isinstance(i, int) and g == NG - 1:
                                sp.dma_start(flat(x2N[q][u])[0:TAILP, :], tail(a["x"])).then_inc(xin[q][u], 16)
                            else:
                                sp.dma_start(flat(x2N[q][u]), group(a["x"], g)).then_inc(xin[q][u], 16)

                    def store(norm, y, tab, o):
                        def step(i, q):
                            for u in range(2):
                                sp.wait_ge(norm.done, ready(i, u))
                                sp.dma_start(group(tab, 2 * i + u), flat(y[u])).then_inc(o[u], 16)
                        return step

                    def body(i, q):
                        late(i, q, 0, n_pairs, load)
                        if not edge:
                            late(i, q, L3, n_pairs, store(norm1, yN, x1_tab, o1))
                            late(i, q, L4, n_pairs, store(norm2, zN, x2_tab, o2))

                    pipeline(sp, n_pairs, L4, body)
                    for u in range(2):
                        if not edge:
                            sp.wait_ge(o1[u], 16 * NPAIR)
                            sp.wait_ge(o2[u], 16 * NPAIR)

                @block.gpsimd
                def _(pool):
                    def gather(i, q):
                        for u in range(2):
                            free(pool, tpd, i, ago=2)
                            free(pool, xbd, i, ago=2)
                            pool.sem_inc(gate, 1)
                            indices(pool, i, u, ixd, IX_DST, slot=q)
                            rows_gather(pool, u, x2N[q], a["x"], q, xin[q])

                    def add_bias(i, q):
                        for u in range(2):
                            landed_pair(pool, xin[q][u], i, q, per)
                            free(pool, r1d, i)
                            nc.gpsimd.tensor_tensor(flat(xb[u]), flat(x2N[q][u]), flat(b2b_bc), ADD).then_inc(xbd, 1)

                    def scatter(norm, y, tab, slot, o):
                        def step(i, q):
                            for u in range(2):
                                pool.wait_ge(norm.done, ready(i, u))
                                free(pool, o[u], i, k=per)
                                pool.sem_inc(gate, 1)
                                nc.gpsimd.tensor_copy(islot[u][:, slot, :], ix[:, IX_DSTW, bass.ds((2 * i + u) * J, J)]).then_inc(sdone[slot], 1)
                                pool.wait_ge(sdone[slot], ready(i, u))
                                pool.sem_inc(gate, 1)
                                rows_scatter(pool, u, y, tab, slot, o)
                        return step

                    sdone = {2: ixd1, 3: ixd2}

                    def body(i, q):
                        late(i, q, L1, n_pairs, add_bias)
                        if edge:
                            late(i, q, 0, n_pairs, gather)
                        late(i, q, L2, n_pairs, lambda i, q: norm1.rstd_steps(pool, i, True))
                        if edge:
                            late(i, q, L3, n_pairs, scatter(norm1, yN, x1_tab, 2, o1))
                            late(i, q, L4, n_pairs, scatter(norm2, zN, x2_tab, 3, o2))
                        late(i, q, L3, n_pairs, lambda i, q: norm2.rstd_steps(pool, i, True))

                    pipeline(pool, n_pairs, L4, body)
                    if edge:
                        for u in range(2):
                            landed(pool, o1[u], per * EPAIR)
                            landed(pool, o2[u], per * EPAIR)

                @block.tensor
                def _(pe):
                    def trans_x(i, q):
                        for u in range(2):
                            landed_pair(pe, xin[q][u], i, q, per)
                            other_at(pe, cp1d, i - (L3 - L0) - 1, u, n_pairs)
                            transposes(A, x2N[q], u).then_inc(tpd, 1)

                    def hidden(i, q):
                        for u in range(2):
                            pe.wait_ge(cpd, ready(i, u))
                            free(pe, elud, i)
                            if edge:
                                pe.wait_ge(ain[u], 16 * i + 16)
                            for h in range(2):
                                cols = slice(h * P, (h + 1) * P)
                                last = nc.tensor.matmul(H[u][h][:, :], W2a[:, 0, cols], xT[u][:, :], start=True, stop=not edge)
                                if edge:
                                    for c in range(2):
                                        last = nc.tensor.matmul(H[u][h][:, :], Wf[:, c, cols], agg[u][:, c, :], start=False, stop=(c == 1))
                            last.then_inc(hidd, 1)

                    def out0(i, q):
                        for u in range(2):
                            pe.wait_ge(elud, ready(i, u))
                            free(pe, r1d, i)
                            other_at(pe, r2d, i - (L3 - L1), u, n_pairs)
                            back_product(B, [hid2[q][u][:, c, :] for c in range(2)], [W2b[:, c, :] for c in range(2)], u).then_inc(y1d, 1)

                    def trans_x1(i, q):
                        for u in range(2):
                            pe.wait_ge(norm1.done, ready(i, u))
                            other_at(pe, cpd, i + (L3 - L0), u, n_pairs)
                            transposes(A, yN, u).then_inc(tp1d, 1)

                    def out1(i, q):
                        for u in range(2):
                            pe.wait_ge(cp1d, ready(i, u))
                            other_at(pe, r1d, i + (L3 - L2), u, n_pairs)
                            back_product(B, [x1T[u]], [WL1[:, :]], u).then_inc(y2d, 1)

                    def body(i, q):
                        late(i, q, L0, n_pairs, trans_x)
                        late(i, q, L3, n_pairs, trans_x1)
                        late(i, q, L0, n_pairs, hidden)
                        late(i, q, L3, n_pairs, out1)
                        late(i, q, L1, n_pairs, out0)

                    pipeline(pe, n_pairs, L4, body)

                @block.scalar
                def _(act):
                    def free1(act, i, u):
                        free(act, o1[u], i, k=per)
                        free(act, r2d, i)
                        free(act, tp1d, i)

                    def copy_x(i, q):
                        for u in range(2):
                            act.wait_ge(tpd, ready(i, u))
                            free(act, hidd, i)
                            nc.scalar.activation(xT[u][:, :], A[u][:, :], ACT.Copy).then_inc(cpd, 1)

                    def exps(i, q):
                        for u in range(2):
                            act.wait_ge(hidd, ready(i, u))
                            free(act, y1d, i, ago=2)
                            for h in range(2):
                                last = nc.scalar.activation(hid2[q][u][:, h, :], H[u][h][:, :], ACT.Exp, bias=bias[h])
                            last.then_inc(expd, 1)

                    def copy_x1(i, q):
                        for u in range(2):
                            act.wait_ge(tp1d, ready(i, u))
                            free(act, y2d, i)
                            nc.scalar.activation(x1T[u], A[u][:, :], ACT.Copy).then_inc(cp1d, 1)

                    def body(i, q):
                        late(i, q, L3, n_pairs, lambda i, q: norm1.act_scale_steps(act, i, free1))
                        late(i, q, L0, n_pairs, copy_x)
                        late(i, q, L3, n_pairs, copy_x1)
                        late(i, q, L4, n_pairs, lambda i, q: norm2.act_scale_steps(act, i, lambda e, i, u: free(e, o2[u], i, k=per)))
                        late(i, q, L0, n_pairs, exps)

                    pipeline(act, n_pairs, L4, body)

                @block.vector
                def _(dve):
                    def residual0(i, q):
                        for u in range(2):
                            dve.wait_ge(y1d, ready(i, u))
                            dve.wait_ge(xbd, ready(i, u))
                            free(dve, norm1.done, i)
                            nc.vector.tensor_tensor(flat(rN[u]), B[u][:, :], flat(xb[u]), ADD).then_inc(r1d, 1)

                    def residual1(i, q):
                        for u in range(2):
                            dve.wait_ge(y2d, ready(i, u))
                            free(dve, norm2.done, i)
                            nc.vector.tensor_tensor(flat(r2N[u]), B[u][:, :], flat(yN[u]), ADD).then_inc(r2d, 1)

                    def body(i, q):
                        late(i, q, L1, n_pairs, lambda i, q: elu_steps(dve, i, H, bias, expd, hid2[q], tmin, elud))
                        late(i, q, L2, n_pairs, residual0)
                        late(i, q, L2, n_pairs, lambda i, q: norm1.moments_steps(dve, i, r1d))
                        late(i, q, L3, n_pairs, residual1)
                        late(i, q, L3, n_pairs, lambda i, q: norm2.moments_steps(dve, i, r2d))

                    pipeline(dve, n_pairs, L4, body)

            if edge:
                for s in (*o1, *o2):
                    s.end(per * EPAIR)
                ends(xin)

        ph = Phase()
        ixd, scd, tpd, samed, scand = ph.sems(5)
        kin, aout = ph.sems(2), ph.sems(2)
        gx, gi = gat_a, gat_b
        same = [flat(xb[u]) for u in range(2)]
        total = [agg[u][:, 0, :] for u in range(2)]
        with nc.Block() as block:

            @block.sync
            def _(sp):
                ph.clear_other(sp)

                def body(i):
                    for u in range(2):
                        free(sp, samed, i)
                        sp.dma_start(krow[u][:, 0:GR + 1], row_bc(key_row[0], (2 * i + u) * GR + FRONT - 1, GR + 1)).then_inc(kin[u], 16)
                    for u in range(2):
                        sp.wait_ge(scand, ready(i, u, 1))
                        sp.dma_start(plane(agg1, 2 * i + u), total[u]).then_inc(aout[u], 16)

                pairs(sp, EPAIR, body)
                for u in range(2):
                    sp.wait_ge(aout[u], 16 * EPAIR)

            @block.gpsimd
            def _(pool):
                def body(i):
                    for u in range(2):
                        free(pool, gx[u], i, k=16 * J)
                        free(pool, gi[u], i, k=16 * J)
                        free(pool, scd, i)
                        pool.sem_inc(gate, 1)
                        indices(pool, i, u, ixd, IX_SDST)
                        rows_gather(pool, u, xN, x1_tab, 0, gx)
                        rows_gather(pool, u, ginv, inv_tab, 0, gi)

                pairs(pool, EPAIR, body)

            @block.tensor
            def _(pe):
                def body(i):
                    for u in range(2):
                        pe.wait_ge(scd, ready(i, u))
                        free(pe, scand, i, 1)
                        transposes(A, yN, u).then_inc(tpd, 1)

                pairs(pe, EPAIR, body)

            @block.vector
            def _(dve):
                nc.vector.memset(agg[1][:, :, :], 0.0).then_inc(scand, 1)

                def body(i):
                    for u in range(2):
                        dve.wait_ge(kin[u], 16 * i + 16)
                        nc.vector.tensor_tensor(same[u], krow[u][:, 1:GR + 1], krow[u][:, 0:GR], EQ).then_inc(samed, 1)
                    for u in range(2):
                        landed(dve, gx[u], 16 * J * i + 16 * J)
                        landed(dve, gi[u], 16 * J * i + 16 * J)
                        free(dve, tpd, i)
                        for j in range(J):
                            last = nc.vector.tensor_scalar(yN[u][:, j, :], xN[u][:, j, :], ginv[u][:, j, :], None, MUL)
                        last.then_inc(scd, 1)
                    for u in range(2):
                        dve.wait_ge(samed, ready(i, u))
                        dve.wait_ge(tpd, ready(i, u))
                        free(dve, aout[u], i, k=16)
                        dve.wait_ge(scand, ready(i, u))
                        nc.vector.tensor_tensor_scan(total[u], same[u], A[u][:, :], total[1 - u][:, GR - 1:GR], MUL, ADD).then_inc(scand, 1)

                pairs(dve, EPAIR, body)

        for s in (*gx, *gi):
            s.end(16 * J * EPAIR)

        ph = Phase()
        ixd, scd, tpd, sumd, y2d, r2d = ph.sems(6)
        ain = ph.sems(2)
        gx, o2 = gat_a, sca_a
        norm = Norm(ph, rN, zN)
        with nc.Block() as block:

            @block.sync
            def _(sp):
                ph.clear_other(sp)

                def body(i):
                    for u in range(2):
                        free(sp, sumd, i)
                        sp.dma_start(total[u], plane(agg1, 2 * i + u)).then_inc(ain[u], 16)

                pairs(sp, EPAIR, body)

            @block.gpsimd
            def _(pool):
                def body(i):
                    for u in range(2):
                        free(pool, gx[u], i, k=16 * J)
                        free(pool, o2[u], i, k=16 * J)
                        free(pool, r2d, i)
                        free(pool, scd, i)
                        pool.sem_inc(gate, 1)
                        indices(pool, i, u, ixd, IX_SSRC, IX_SSRCW)
                        rows_gather(pool, u, xN, x1_tab, 0, gx)
                    norm.rstd_steps(pool, i)
                    for u in range(2):
                        pool.wait_ge(norm.done, ready(i, u))
                        pool.sem_inc(gate, 1)
                        rows_scatter(pool, u, zN, x2_tab, 1, o2)

                pairs(pool, EPAIR, body)
                for u in range(2):
                    landed(pool, o2[u], 16 * J * EPAIR)

            @block.tensor
            def _(pe):
                def body(i):
                    for u in range(2):
                        pe.wait_ge(scd, ready(i, u))
                        free(pe, r2d, i)
                        transposes(A, yN, u).then_inc(tpd, 1)
                    for u in range(2):
                        pe.wait_ge(sumd, ready(i, u))
                        back_product(A, [xT[u][:, :]], [WL1[:, :]], u).then_inc(y2d, 1)

                pairs(pe, EPAIR, body)

            @block.vector
            def _(dve):
                def body(i):
                    for u in range(2):
                        landed(dve, gx[u], 16 * J * i + 16 * J)
                        free(dve, tpd, i)
                        for j in range(J):
                            last = nc.vector.tensor_scalar(yN[u][:, j, :], xN[u][:, j, :], inv_e[:, bass.ds((2 * i + u) * J + j, 1)], None, MUL)
                        last.then_inc(scd, 1)
                    for u in range(2):
                        dve.wait_ge(tpd, ready(i, u))
                        dve.wait_ge(ain[u], 16 * i + 16)
                        free(dve, y2d, i)
                        nc.vector.tensor_tensor(xT[u][:, :], A[u][:, :], total[u], ADD).then_inc(sumd, 1)
                    for u in range(2):
                        dve.wait_ge(y2d, ready(i, u))
                        free(dve, norm.done, i)
                        for j in range(J):
                            last = nc.vector.scalar_tensor_tensor(rN[u][:, j, :], A[u][:, j * P:(j + 1) * P], inv_e[:, bass.ds((2 * i + u) * J + j, 1)],
                                                                  xN[u][:, j, :], MUL, ADD)
                        last.then_inc(r2d, 1)
                    norm.moments_steps(dve, i, r2d)
                    norm.scale_steps(dve, i, lambda dve, i, u: free(dve, o2[u], i, k=16 * J))

                pairs(dve, EPAIR, body)

        for s in (*gx, *o2):
            s.end(16 * J * EPAIR)

        def typed_messages(l, table, out_tab):
            ph = Phase()
            ixd, tpd, cpd, projd, hd, maskd, msgd, samed, scand = ph.sems(9)
            kin, tin, aout = (ph.sems(2) for _ in range(3))
            gx = (gat_a, gat_b)
            same = [flat(xb[u]) for u in range(2)]
            types = [flat(rN[u]) for u in range(2)]
            hT = [flat(zN[u]) for u in range(2)]
            masked = [big[:, 8 * u:8 * u + 8, :] for u in range(2)]
            total = [agg[u][:, 0, :] for u in range(2)]
            L1, L2, L3 = 1, 2, 3
            n_pairs = EPAIR
            with nc.Block() as block:

                @block.sync
                def _(sp):
                    ph.clear_other(sp)

                    def load(i, q):
                        for u in range(2):
                            free(sp, samed, i)
                            sp.dma_start(krow[u][:, 0:GR + 1], row_bc(key_row[1], (2 * i + u) * GR + FRONT - 1, GR + 1)).then_inc(kin[u], 16)
                            free(sp, maskd, i)
                            sp.sem_inc(sp_gate, 1)
                            sp.dma_start(types[u], row_bc(type_row, (2 * i + u) * GR, GR)).then_inc(tin[u], 16)

                    def store(i, q):
                        for u in range(2):
                            sp.wait_ge(scand, ready(i, u, 1))
                            sp.dma_start(plane(out_tab, 2 * i + u), total[u]).then_inc(aout[u], 16)

                    def body(i, q):
                        late(i, q, L1, n_pairs, load)
                        late(i, q, L3, n_pairs, store)

                    pipeline(sp, n_pairs, L3, body)
                    for u in range(2):
                        sp.wait_ge(aout[u], 16 * EPAIR)

                @block.gpsimd
                def _(pool):
                    def gather(i, q):
                        for u in range(2):
                            free(pool, tpd, i, ago=2)
                            pool.sem_inc(gate, 1)
                            indices(pool, i, u, ixd, IX_SRC, slot=q)
                            rows_gather(pool, u, x2N[q], table, q, gx[q])

                    pipeline(pool, n_pairs, L3, lambda i, q: late(i, q, 0, n_pairs, gather))

                @block.tensor
                def _(pe):
                    def trans(i, q):
                        for u in range(2):
                            landed_pair(pe, gx[q][u], i, q, 16 * J)
                            free(pe, cpd if l == 0 else hd, i)
                            transposes(A, x2N[q], u).then_inc(tpd, 1)

                    def project(i, q):
                        for u in range(2):
                            pe.wait_ge(cpd, ready(i, u))
                            free(pe, hd, i)
                            nc.tensor.matmul(B[u][:, :], Wp[:, :], xT[u][:, :], start=True, stop=True).then_inc(projd, 1)

                    def messages(u):
                        def step(i, q):
                            pe.wait_ge(maskd, ready(i, u))
                            free(pe, scand, i, 1)
                            for t in range(NTYPE):
                                last = nc.tensor.matmul(H[u][0][:, :], We[:, l * NTYPE + t, :], masked[u][:, t, :], start=(t == 0), stop=(t == NTYPE - 1))
                            last.then_inc(msgd, 1)
                        return step

                    def body(i, q):
                        late(i, q, L1, n_pairs, trans)
                        late(i, q, L2, n_pairs, messages(0))
                        if l == 0:
                            late(i, q, L1, n_pairs, project)
                        late(i, q, L2, n_pairs, messages(1))

                    pipeline(pe, n_pairs, L3, body)

                @block.scalar
                def _(act):
                    def copy_x(i, q):
                        for u in range(2):
                            act.wait_ge(tpd, ready(i, u))
                            free(act, projd, i)
                            nc.scalar.activation(xT[u][:, :], A[u][:, :], ACT.Copy).then_inc(cpd, 1)

                    def h(i, q):
                        for u in range(2):
                            act.wait_ge(projd if l == 0 else tpd, ready(i, u))
                            free(act, maskd, i)
                            if l == 0:
                                nc.scalar.activation(hT[u], B[u][:, :], ACT.Relu, bias=bp[:, :]).then_inc(hd, 1)
                            else:
                                nc.scalar.activation(hT[u], A[u][:, :], ACT.Copy).then_inc(hd, 1)

                    def body(i, q):
                        if l == 0:
                            late(i, q, L1, n_pairs, copy_x)
                        late(i, q, L1, n_pairs, h)

                    pipeline(act, n_pairs, L3, body)

                @block.vector
                def _(dve):
                    nc.vector.memset(agg[1][:, :, :], 0.0).then_inc(scand, 1)

                    def compare(i, q):
                        for u in range(2):
                            dve.wait_ge(kin[u], 16 * i + 16)
                            free(dve, scand, i, 1)
                            nc.vector.tensor_tensor(same[u], krow[u][:, 1:GR + 1], krow[u][:, 0:GR], EQ).then_inc(samed, 1)

                    def mask(u):
                        def step(i, q):
                            dve.wait_ge(hd, ready(i, u))
                            dve.wait_ge(tin[u], 16 * i + 16)
                            free(dve, msgd, i)
                            for t in range(NTYPE):
                                last = nc.vector.scalar_tensor_tensor(masked[u][:, t, :], types[u], float(t), hT[u], EQ, MUL)
                            last.then_inc(maskd, 1)
                        return step

                    def sums(u):
                        def step(i, q):
                            dve.wait_ge(samed, ready(i, u))
                            dve.wait_ge(msgd, ready(i, u))
                            free(dve, aout[u], i, k=16)
                            dve.wait_ge(scand, ready(i, u))
                            nc.vector.tensor_tensor_scan(total[u], same[u], H[u][0][:, :], total[1 - u][:, GR - 1:GR], MUL, ADD).then_inc(scand, 1)
                        return step

                    def body(i, q):
                        for u in range(2):
                            late(i, q, L3, n_pairs, sums(u))
                            late(i, q, L2, n_pairs, mask(u))
                        late(i, q, L2, n_pairs, compare)

                    pipeline(dve, n_pairs, L3, body)

            ends(gx)

        class Cell:

            def __init__(self, ph, l, rz, n, d, messages=None):
                self.l, self.rz, self.n, self.d, self.messages = l, rz, n, d, messages
                self.gated, self.rzd, self.qd, self.q2d, self.nd, self.dd, self.dzd, self.sd, self.hd = ph.sems(9)

            def gates(self, pe, u, h):
                l = self.l
                for bank, c in ((H[u][0], 0), (H[u][1], 1), (A[u], 2)):
                    both = self.messages and c < 2
                    last = nc.tensor.matmul(bank[:, :], Whh[:, l, c * D:(c + 1) * D], h, start=True, stop=not both)
                    if both:
                        last = nc.tensor.matmul(bank[:, :], Wih[:, l, c * D:(c + 1) * D], self.messages[u], start=False, stop=True)
                if self.messages:
                    last = nc.tensor.matmul(B[u][:, :], Wih[:, l, 2 * D:3 * D], self.messages[u], start=True, stop=True)
                last.then_inc(self.gated, 1)

            def sigmoids(self, act, i, u):
                act.wait_ge(self.gated, ready(i, u))
                free(act, self.dzd, i)
                nc.scalar.activation(self.rz[u][:, 0, :], H[u][0][:, :], ACT.Sigmoid, bias=brz[:, self.l, 0:1])
                nc.scalar.activation(self.rz[u][:, 1, :], H[u][1][:, :], ACT.Sigmoid, bias=brz[:, self.l, 1:2]).then_inc(self.rzd, 1)

            def q_steps(self, dve, i, us=(0, 1)):
                first = self.qd if self.messages else self.q2d
                for u in us:
                    dve.wait_ge(self.rzd, ready(i, u))
                    free(dve, self.sd, i)
                    nc.vector.scalar_tensor_tensor(self.n[u], A[u][:, :], bhh[:, self.l, 2:3], self.rz[u][:, 0, :], ADD, MUL).then_inc(first, 1)
                if self.messages:
                    for u in us:
                        dve.wait_ge(self.qd, ready(i, u))
                        nc.vector.tensor_tensor(self.n[u], self.n[u], B[u][:, :], ADD).then_inc(self.q2d, 1)

            def tanh_steps(self, act, i):
                for u in range(2):
                    act.wait_ge(self.q2d, ready(i, u))
                    nc.scalar.activation(self.n[u], self.n[u], ACT.Tanh, bias=bih[:, self.l, 2:3]).then_inc(self.nd, 1)

            def d_steps(self, pool, i, h):
                for u in range(2):
                    pool.wait_ge(self.nd, ready(i, u))
                    free(pool, self.hd, i)
                    nc.gpsimd.tensor_tensor(self.d[u], h[u], self.n[u], SUB).then_inc(self.dd, 1)

            def dz_steps(self, dve, i):
                for u in range(2):
                    dve.wait_ge(self.dd, ready(i, u))
                    nc.vector.tensor_tensor(self.d[u], self.d[u], self.rz[u][:, 1, :], MUL).then_inc(self.dzd, 1)

            def s_steps(self, eng, tensor_tensor, i):
                for u in range(2):
                    eng.wait_ge(self.dzd, ready(i, u))
                    tensor_tensor(self.d[u], self.d[u], self.n[u], ADD).then_inc(self.sd, 1)

            def relu_steps(self, act, i, h, h_free):
                for u in range(2):
                    act.wait_ge(self.sd, ready(i, u))
                    h_free(i, u)
                    nc.scalar.activation(h[u], self.d[u], ACT.Relu).then_inc(self.hd, 1)

        def dense_recurrent():
            ph = Phase()
            tpd, cpd, projd, h0d, xbd, tp1d, cp1d, yd, rd = ph.sems(9)
            xin, xagain, h1out, x3out = (ph.sems(2), ph.sems(2)), ph.sems(2), ph.sems(2), ph.sems(2)
            plane_ = lambda k: [big[:, 8 * u + k, :] for u in range(2)]
            cell1 = Cell(ph, 0, hid2[0], plane_(0), plane_(1))
            cell2 = Cell(ph, 1, hid2[1], plane_(2), plane_(3))
            h0, h1 = [plane_(4), plane_(5)], [plane_(6), plane_(7)]
            h2 = [agg[u][:, 0, :] for u in range(2)]
            xR = [agg[u][:, 1, :] for u in range(2)]
            norm = Norm(ph, rN, zN)
            L1, L2, L3, L4, L5, L6 = range(1, 7)
            n_pairs = NPAIR

            def start(k):
                return isinstance(k, int)

            with nc.Block() as block:

                @block.sync
                def _(sp):
                    ph.clear_other(sp)

                    def load(i, q):
                        for u in range(2):
                            free(sp, tpd, i, ago=2)
                            sp.dma_start(flat(x2N[q][u]), group(x2_tab, 2 * i + u)).then_inc(xin[q][u], 16)

                    def load_again(i, q):
                        for u in range(2):
                            free(sp, xbd, i)
                            sp.dma_start(xR[u], group(x2_tab, 2 * i + u)).then_inc(xagain[u], 16)

                    def store_h1(i, q):
                        for u in range(2):
                            sp.wait_ge(cp1d, ready(i, u))
                            sp.dma_start(group(h1_tab, 2 * i + u), flat(yN[u])).then_inc(h1out[u], 16)

                    def store_x3(i, q):
                        for u in range(2):
                            sp.wait_ge(norm.done, ready(i, u))
                            sp.dma_start(group(x3_tab, 2 * i + u), flat(zN[u])).then_inc(x3out[u], 16)

                    def body(i, q):
                        late(i, q, 0, n_pairs, load)
                        late(i, q, L4, n_pairs, load_again)
                        late(i, q, L6, n_pairs, store_x3)
                        late(i, q, L4, n_pairs, store_h1)

                    pipeline(sp, n_pairs, L6, body)
                    for u in range(2):
                        sp.wait_ge(h1out[u], 16 * n_pairs)
                        sp.wait_ge(x3out[u], 16 * n_pairs)

                @block.gpsimd
                def _(pool):
                    def add_bias(i, q):
                        for u in range(2):
                            pool.wait_ge(xagain[u], 16 * i + 16)
                            free(pool, rd, i)
                            nc.gpsimd.tensor_tensor(flat(xb[u]), xR[u], flat(bo_bc), ADD).then_inc(xbd, 1)

                    def body(i, q):
                        late(i, q, L3, n_pairs, lambda i, q: cell1.s_steps(pool, nc.gpsimd.tensor_tensor, i))
                        late(i, q, L5, n_pairs, lambda i, q: cell2.d_steps(pool, i, h1[q]))
                        late(i, q, L5, n_pairs, add_bias)
                        late(i, q, L6, n_pairs, lambda i, q: norm.rstd_steps(pool, i))
                        late(i, q, L2, n_pairs, lambda i, q: cell1.d_steps(pool, i, h0[q]))

                    pipeline(pool, n_pairs, L6, body)

                @block.tensor
                def _(pe):
                    def trans_x(i, q):
                        for u in range(2):
                            landed_pair(pe, xin[q][u], i, q, 16)
                            other_at(pe, rd, i + (L1 - L6), u, n_pairs)
                            if start(i):
                                free(pe, h0d, i)
                                other_at(pe, cp1d, i + (L1 - L4 - 1), u, n_pairs)
                            transposes(B, x2N[q], u).then_inc(tpd, 1)

                    def project(i, q):
                        for u in range(2):
                            pe.wait_ge(cpd, ready(i, u))
                            nc.tensor.matmul(B[u][:, :], Wp[:, :], xT[u][:, :], start=True, stop=True).then_inc(projd, 1)

                    def trans_h1(i, q):
                        for u in range(2):
                            pe.wait_ge(cell1.hd, ready(i, u))
                            other_at(pe, h0d, i + (L4 - L1), u, n_pairs)
                            if start(i):
                                free(pe, cp1d, i)
                                other_at(pe, rd, i + (L4 - L6), u, n_pairs)
                            for j in range(J):
                                last = nc.tensor.transpose(B[u][:, j * P:(j + 1) * P], h1[q][u][:, j * P:(j + 1) * P], ident[:, :])
                            last.then_inc(tp1d, 1)

                    def output(i, q):
                        for u in range(2):
                            pe.wait_ge(cell2.hd, ready(i, u))
                            other_at(pe, cp1d, i + (L6 - L4 - 1), u, n_pairs)
                            if start(i):
                                free(pe, rd, i)
                            back_product(B, [h2[u]], [Wo[:, :]], u).then_inc(yd, 1)

                    def gates1(u):
                        def step(i, q):
                            pe.wait_ge(h0d, ready(i, u))
                            other_at(pe, cell2.q2d, i + (L2 - L4 - 1), u, n_pairs)
                            if start(i):
                                free(pe, cell1.q2d, i)
                            cell1.gates(pe, u, h0[q][u])
                        return step

                    def gates2(u):
                        def step(i, q):
                            pe.wait_ge(cell1.hd, ready(i, u))
                            other_at(pe, cell1.q2d, i + (L4 - L2), u, n_pairs)
                            if start(i):
                                free(pe, cell2.q2d, i)
                            cell2.gates(pe, u, h1[q][u])
                        return step

                    def body(i, q):
                        late(i, q, L6, n_pairs, output)
                        late(i, q, L2, n_pairs, gates1(0))
                        late(i, q, L1, n_pairs, trans_x)
                        late(i, q, L2, n_pairs, gates1(1))
                        late(i, q, L1, n_pairs, project)
                        late(i, q, L4, n_pairs, gates2(0))
                        late(i, q, L4, n_pairs, trans_h1)
                        late(i, q, L4, n_pairs, gates2(1))

                    pipeline(pe, n_pairs, L6, body)

                @block.scalar
                def _(act):
                    def copy_x(i, q):
                        for u in range(2):
                            act.wait_ge(tpd, ready(i, u))
                            free(act, projd, i)
                            nc.scalar.activation(xT[u][:, :], B[u][:, :], ACT.Copy).then_inc(cpd, 1)

                    def relu_h0(i, q):
                        for u in range(2):
                            act.wait_ge(projd, ready(i, u))
                            free(act, cell1.dd, i, ago=2)
                            free(act, cell1.gated, i, ago=2)
                            nc.scalar.activation(h0[q][u], B[u][:, :], ACT.Relu, bias=bp[:, :]).then_inc(h0d, 1)

                    def h1_free(i, u):
                        free(act, cell2.dd, i, ago=2)
                        free(act, cell2.gated, i, ago=2)
                        free(act, tp1d, i, ago=2)

                    def copy_h1(i, q):
                        for u in range(2):
                            act.wait_ge(tp1d, ready(i, u))
                            free(act, h1out[u], i, k=16)
                            nc.scalar.activation(flat(yN[u]), B[u][:, :], ACT.Copy).then_inc(cp1d, 1)

                    def body(i, q):
                        late(i, q, L5, n_pairs, lambda i, q: cell2.tanh_steps(act, i))
                        late(i, q, L2, n_pairs, lambda i, q: cell1.sigmoids(act, i, 0))
                        late(i, q, L1, n_pairs, copy_x)
                        late(i, q, L2, n_pairs, lambda i, q: cell1.sigmoids(act, i, 1))
                        late(i, q, L1, n_pairs, relu_h0)
                        late(i, q, L3, n_pairs, lambda i, q: cell1.relu_steps(act, i, h1[q], h1_free))
                        late(i, q, L2, n_pairs, lambda i, q: cell1.tanh_steps(act, i))
                        late(i, q, L5, n_pairs, lambda i, q: cell2.relu_steps(act, i, h2, lambda i, u: free(act, yd, i)))
                        late(i, q, L4, n_pairs, lambda i, q: cell2.sigmoids(act, i, 0))
                        late(i, q, L4, n_pairs, copy_h1)
                        late(i, q, L4, n_pairs, lambda i, q: cell2.sigmoids(act, i, 1))

                    pipeline(act, n_pairs, L6, body)

                @block.vector
                def _(dve):
                    def residual(i, q):
                        for u in range(2):
                            dve.wait_ge(yd, ready(i, u))
                            dve.wait_ge(xbd, ready(i, u))
                            free(dve, norm.done, i)
                            nc.vector.tensor_tensor(flat(rN[u]), B[u][:, :], flat(xb[u]), ADD).then_inc(rd, 1)

                    def body(i, q):
                        late(i, q, L3, n_pairs, lambda i, q: cell1.dz_steps(dve, i))
                        late(i, q, L6, n_pairs, residual)
                        late(i, q, L2, n_pairs, lambda i, q: cell1.q_steps(dve, i, (0,)))
                        late(i, q, L6, n_pairs, lambda i, q: norm.moments_steps(dve, i, rd))
                        late(i, q, L2, n_pairs, lambda i, q: cell1.q_steps(dve, i, (1,)))
                        late(i, q, L5, n_pairs, lambda i, q: cell2.dz_steps(dve, i))
                        late(i, q, L5, n_pairs, lambda i, q: cell2.s_steps(dve, nc.vector.tensor_tensor, i))
                        late(i, q, L6, n_pairs, lambda i, q: norm.scale_steps(dve, i, lambda e, i, u: free(e, x3out[u], i, k=16)))
                        late(i, q, L4, n_pairs, lambda i, q: cell2.q_steps(dve, i))

                    pipeline(dve, n_pairs, L6, body)

        def edge_recurrent(l):
            ph = Phase()
            tpd, cpd, projd, h0d, xbd, lastd, readd, ixd, ixd2 = ph.sems(9)
            min_, hin = (ph.sems(2), ph.sems(2)), (ph.sems(2), ph.sems(2))
            xout = (ph.sems(2), ph.sems(2))
            xagain, hout, cout = (ph.sems(2) for _ in range(3))
            xin, scattered = (gat_a, gat_b), sca_a
            per = 16 * J
            plane_ = lambda k: [big[:, 8 * u + k, :] for u in range(2)]
            messages = [[agg[u][:, q, :] for u in range(2)] for q in range(2)]
            cell = Cell(ph, l, hid2[0], plane_(0), plane_(1))
            h = [plane_(4), plane_(5)]
            hnew = plane_(6)
            norm = Norm(ph, rN, zN) if l == 1 else None
            src, table = (yN, h1_tab) if l == 0 else (zN, x3_tab)
            L1, L2, L3, L4, L5 = range(1, 6)
            n_pairs = EPAIR
            with nc.Block() as block:

                @block.sync
                def _(sp):
                    ph.clear_other(sp)

                    def load(i, q):
                        for u in range(2):
                            g = 2 * i + u
                            free(sp, cell.gated, i, ago=2)
                            sp.dma_start(messages[q][u], plane(agg2 if l == 0 else agg3, g)).then_inc(min_[q][u], 16)
                            if l == 1:
                                free(sp, cell.dd, i, ago=2)
                                sp.dma_start(h[q][u], plane(h1_c, g)).then_inc(hin[q][u], 16)

                    def keep_x(i, q):
                        for u in range(2):
                            landed_pair(sp, xin[q][u], i, q, per)
                            sp.dma_start(plane(x2_c, 2 * i + u), flat(x2N[q][u])).then_inc(xout[q][u], 16)

                    def load_again(i, q):
                        for u in range(2):
                            free(sp, xbd, i)
                            sp.dma_start(flat(yN[u]), plane(x2_c, 2 * i + u)).then_inc(xagain[u], 16)

                    def store_h(i, q):
                        for u in range(2):
                            sp.wait_ge(cell.hd, ready(i, u))
                            sp.dma_start(plane(h1_c, 2 * i + u), hnew[u]).then_inc(hout[u], 16)

                    def store_x3(i, q):
                        for u in range(2):
                            sp.wait_ge(norm.done, ready(i, u))
                            sp.dma_start(plane(x3_c, 2 * i + u), flat(zN[u])).then_inc(cout[u], 16)

                    def body(i, q):
                        late(i, q, L1, n_pairs, load)
                        if l == 0:
                            late(i, q, L1, n_pairs, keep_x)
                            late(i, q, L3, n_pairs, store_h)
                        else:
                            late(i, q, L2, n_pairs, load_again)
                            late(i, q, L5, n_pairs, store_x3)

                    pipeline(sp, n_pairs, L5, body)
                    for u in range(2):
                        if l == 0:
                            sp.wait_ge(hout[u], 16 * n_pairs)
                            for q in range(2):
                                sp.wait_ge(xout[q][u], 16 * ((n_pairs + 1 - q) // 2))
                        else:
                            sp.wait_ge(cout[u], 16 * n_pairs)

                @block.gpsimd
                def _(pool):
                    def gather(i, q):
                        for u in range(2):
                            free(pool, tpd, i, ago=2)
                            if not isinstance(i, int) or i >= 2:
                                landed_pair(pool, xout[q][u], i - 2, q, 16)
                            pool.sem_inc(gate, 1)
                            indices(pool, i, u, ixd, IX_DST, slot=q)
                            rows_gather(pool, u, x2N[q], x2_tab, q, xin[q])

                    def add_bias(i, q):
                        for u in range(2):
                            pool.wait_ge(xagain[u], 16 * i + 16)
                            free(pool, readd, i)
                            nc.gpsimd.tensor_tensor(flat(xb[u]), flat(yN[u]), flat(bo_bc), ADD).then_inc(xbd, 1)

                    def scatter(i, q):
                        for u in range(2):
                            free(pool, scattered[u], i, k=per)
                            pool.wait_ge(readd if l == 0 else norm.done, ready(i, u))
                            pool.sem_inc(gate, 1)
                            indices(pool, i, u, ixd2, IX_DSTW, slot=2)
                            rows_scatter(pool, u, src, table, 2, scattered)

                    def body(i, q):
                        if l == 0:
                            late(i, q, 0, n_pairs, gather)
                            late(i, q, L4, n_pairs, scatter)
                        else:
                            late(i, q, L5, n_pairs, scatter)
                            late(i, q, L3, n_pairs, add_bias)
                            late(i, q, L4, n_pairs, lambda i, q: norm.rstd_steps(pool, i))

                    pipeline(pool, n_pairs, L5, body)
                    for u in range(2):
                        landed(pool, scattered[u], per * EPAIR)

                @block.tensor
                def _(pe):
                    def trans_x(i, q):
                        for u in range(2):
                            landed_pair(pe, xin[q][u], i, q, per)
                            free(pe, cell.rzd, i)
                            free(pe, h0d, i)
                            transposes([H[0][0], H[1][0]], x2N[q], u).then_inc(tpd, 1)

                    def project(i, q):
                        for u in range(2):
                            pe.wait_ge(cpd, ready(i, u))
                            nc.tensor.matmul(H[u][0][:, :], Wp[:, :], xT[u][:, :], start=True, stop=True).then_inc(projd, 1)

                    def gates(i, q):
                        for u in range(2):
                            if l == 0:
                                pe.wait_ge(h0d, ready(i, u))
                            else:
                                landed_pair(pe, hin[q][u], i, q, 16)
                            landed_pair(pe, min_[q][u], i, q, 16)
                            free(pe, cell.q2d, i)
                            other_at(pe, readd, i - 2, u, n_pairs)
                            cell.messages = messages[q]
                            cell.gates(pe, u, h[q][u])

                    def last_product(i, q):
                        for u in range(2):
                            pe.wait_ge(cell.hd, ready(i, u))
                            other_at(pe, cell.rzd, i + 1, u, n_pairs)
                            free(pe, readd, i)
                            if l == 0:
                                for j in range(J):
                                    cols_j = slice(j * P, (j + 1) * P)
                                    last = nc.tensor.transpose(H[u][1][:, cols_j], hnew[u][:, cols_j], ident[:, :])
                            else:
                                last = back_product([H[0][1], H[1][1]], [hnew[u]], [Wo[:, :]], u)
                            last.then_inc(lastd, 1)

                    def body(i, q):
                        late(i, q, L4, n_pairs, last_product)
                        late(i, q, L2, n_pairs, gates)
                        if l == 0:
                            late(i, q, L1, n_pairs, trans_x)
                            late(i, q, L1, n_pairs, project)

                    pipeline(pe, n_pairs, L5, body)

                @block.scalar
                def _(act):
                    def copy_x(i, q):
                        for u in range(2):
                            act.wait_ge(tpd, ready(i, u))
                            free(act, projd, i)
                            nc.scalar.activation(xT[u][:, :], H[u][0][:, :], ACT.Copy).then_inc(cpd, 1)

                    def relu_h0(i, q):
                        for u in range(2):
                            act.wait_ge(projd, ready(i, u))
                            free(act, cell.dd, i, ago=2)
                            free(act, cell.gated, i, ago=2)
                            nc.scalar.activation(h[q][u], H[u][0][:, :], ACT.Relu, bias=bp[:, :]).then_inc(h0d, 1)

                    def h_free(i, u):
                        free(act, lastd, i)
                        if l == 0:
                            free(act, hout[u], i, k=16)

                    def copy_h1(i, q):
                        for u in range(2):
                            act.wait_ge(lastd, ready(i, u))
                            free(act, scattered[u], i, k=per)
                            nc.scalar.activation(flat(yN[u]), H[u][1][:, :], ACT.Copy).then_inc(readd, 1)

                    def body(i, q):
                        if l == 0:
                            late(i, q, L4, n_pairs, copy_h1)
                        late(i, q, L2, n_pairs, lambda i, q: cell.sigmoids(act, i, 0))
                        late(i, q, L2, n_pairs, lambda i, q: cell.sigmoids(act, i, 1))
                        late(i, q, L3, n_pairs, lambda i, q: cell.relu_steps(act, i, hnew, h_free))
                        if l == 0:
                            late(i, q, L1, n_pairs, copy_x)
                            late(i, q, L1, n_pairs, relu_h0)
                        late(i, q, L2, n_pairs, lambda i, q: cell.tanh_steps(act, i))

                    pipeline(act, n_pairs, L5, body)

                @block.vector
                def _(dve):
                    cell.messages = messages[0]

                    def residual(i, q):
                        for u in range(2):
                            dve.wait_ge(lastd, ready(i, u))
                            dve.wait_ge(xbd, ready(i, u))
                            free(dve, norm.done, i)
                            nc.vector.tensor_tensor(flat(rN[u]), H[u][1][:, :], flat(xb[u]), ADD).then_inc(readd, 1)

                    def z_free(dve, i, u):
                        free(dve, cout[u], i, k=16)
                        free(dve, scattered[u], i, k=per)

                    def new_h(i, q):
                        for u in range(2):
                            dve.wait_ge(cell.nd, ready(i, u))
                            free(dve, cell.hd, i)
                            nc.vector.tensor_tensor(cell.d[u], h[q][u], cell.n[u], SUB).then_inc(cell.dd, 1)
                        cell.dz_steps(dve, i)
                        cell.s_steps(dve, nc.vector.tensor_tensor, i)

                    def body(i, q):
                        if l == 1:
                            late(i, q, L5, n_pairs, lambda i, q: norm.scale_steps(dve, i, z_free))
                            late(i, q, L4, n_pairs, residual)
                        late(i, q, L3, n_pairs, new_h)
                        late(i, q, L2, n_pairs, lambda i, q: cell.q_steps(dve, i))
                        if l == 1:
                            late(i, q, L4, n_pairs, lambda i, q: norm.moments_steps(dve, i, readd))

                    pipeline(dve, n_pairs, L5, body)

            if l == 0:
                ends(xin)
            for s in scattered:
                s.end(per * EPAIR)

        dense_recurrent()
        typed_messages(0, x2_tab, agg2)
        edge_recurrent(0)
        typed_messages(1, h1_tab, agg3)
        edge_recurrent(1)

        col_names = ("blankp0", "blankp1", "nblank0", "c0", "c1", "mx", "vx", "nmx", "sd", "sdd", "sxd", "md", "cov", "vd", "t0", "t1",
                     "var", "inv", "s0", "mu", "A1", "B1", "alpha", "s1", "C", "Dv", "F1", "as0", "bshift", "t2", "cw0", "cw1")
        cols = {n: f3[:, k:k + 1] for k, n in enumerate(col_names)}
        G_, BE, BLANK, BB, A_, CB, CW = 1, 2, 3, 0, 4, 5, 6

        def val(l, c):
            return v3[:, l, c:c + 1]

        ph = Phase()
        tpd, bnd, linked, tot, powd, eps_d = ph.sems(6)
        xin = ph.sems(2)
        with nc.Block() as block:

            @block.sync
            def _(sp):
                ph.clear_other(sp)

                def body(i):
                    for u in range(2):
                        free(sp, tpd, i)
                        g = 2 * i + u
                        if isinstance(i, int) and g == NG - 1:
                            sp.dma_start(flat(xN[u])[0:TAILP, :], tail(x3_tab)).then_inc(xin[u], 16)
                        else:
                            sp.dma_start(flat(xN[u]), group(x3_tab, g)).then_inc(xin[u], 16)

                pairs(sp, NPAIR, body, last=True)

            @block.tensor
            def _(pe):
                for l in range(2):
                    last = nc.tensor.matmul(B[0][:, l:l + 1], W3[:, l, :], val(l, BLANK), start=True, stop=True)
                last.then_inc(tot, 1)

                def body(i):
                    for u in range(2):
                        pe.wait_ge(xin[u], 16 * i + 16)
                        free(pe, bnd, i)
                        transposes(A, xN, u).then_inc(tpd, 1)

                pairs(pe, NPAIR, body)

            @block.vector
            def _(dve):
                n = [0]

                def link(ins):
                    n[0] += 1
                    ins.then_inc(linked, 1)
                    dve.wait_ge(linked, n[0])

                dve.wait_ge(tot, 1)
                for l in range(2):
                    link(nc.vector.tensor_tensor(cols[f"blankp{l}"], B[0][:, l:l + 1], val(l, BB), ADD))
                    link(nc.vector.reduce_sum(cols["t0"], v3[:, l, CW:CW + 4], axis=mybir.AxisListType.X))
                    link(nc.vector.scalar_tensor_tensor(cols[f"c{l}"], cols[f"blankp{l}"], cols["t0"], val(l, CB), MUL, ADD))
                link(nc.vector.tensor_scalar(cols["nblank0"], cols["blankp0"], -1.0, None, MUL))

                def body(i):
                    for u in range(2):
                        dve.wait_ge(tpd, ready(i, u))
                        dve.sem_inc(dve_gate, 1)
                        g = 2 * i + u
                        src = A[u][:, :]
                        if isinstance(i, int) and g == NG - 1:
                            src = A[u][:, :].rearrange("p (j q) -> p j q", j=J)[:, :, 0:TAILP]
                        nc.vector.bn_stats(stat3[:, bass.ds(g * 6, 6)], src).then_inc(bnd, 1)

                pairs(dve, NPAIR, body, last=True)
                dve.wait_ge(bnd, NG)
                link(nc.vector.bn_aggr(f3[:, 5:7], stat3[:, :]))
                link(nc.vector.tensor_scalar(cols["nmx"], cols["mx"], -1.0, None, MUL))

        work = [big[:, 8 * u:8 * u + 8, :] for u in range(2)]

        def sorted_pool(l):
            ph = Phase()
            ixd, tpd, cpd, carried, net, tp1d, cp1d, tpx, cpx, smd, smc, convd = ph.sems(12)
            kin, lin, xin, din, o1, o2, o3, o4 = (ph.sems(2) for _ in range(8))
            gx, gs = gat_a, gat_b
            win = [winb[u][:, :] for u in range(2)]
            xsT = [xT[u][:, :] for u in range(2)]
            x3T = [agg[u][:, 0, :] for u in range(2)]
            d1T = [agg[u][:, 1, :] for u in range(2)]
            last_bc = [flat(rN[u]) for u in range(2)]
            dT = [flat(zN[u]) for u in range(2)]
            STEPS = 21 + l

            with nc.Block() as block:

                @block.sync
                def _(sp):
                    ph.clear_other(sp)

                    def body(i):
                        for u in range(2):
                            g = 2 * i + u
                            free(sp, smd, i)
                            sp.dma_start(krow[u][:, 0:GR + 3], row_bc(key_row[1], g * GR + FRONT - 3, GR + 3)).then_inc(kin[u], 16)
                            sp.dma_start(last_bc[u], row_bc(last_row, g * GR, GR)).then_inc(lin[u], 16)
                            if l == 0:
                                free(sp, tpx, i)
                                sp.dma_start(flat(xb[u]), plane(x3_c, g)).then_inc(xin[u], 16)
                            else:
                                free(sp, cpd, i)
                                sp.dma_start(hid[u][:, 0, :], plane(x3src_t, g)).then_inc(din[u], 16)
                                sp.dma_start(d1T[u], plane(d1_t, g)).then_inc(din[u], 16)
                                sp.dma_start(x3T[u], plane(agg1, g)).then_inc(xin[u], 16)
                        for u in range(2):
                            g = 2 * i + u
                            if l == 0:
                                sp.wait_ge(cpd, ready(i, u))
                                sp.dma_start(plane(x3src_t, g), xsT[u]).then_inc(o1[u], 16)
                                sp.wait_ge(cpx, ready(i, u))
                                sp.dma_start(plane(agg1, g), x3T[u]).then_inc(o2[u], 16)
                            sp.wait_ge(net, 2 * STEPS * i + 2 * STEPS)
                            sp.dma_start(plane(d1_t if l == 0 else d2_t, g), dT[u]).then_inc(o3[u], 16)
                            if l == 0:
                                sp.wait_ge(cp1d, ready(i, u))
                                sp.dma_start(d1_tab[bass.ds(g * GR, GR), :].rearrange("(j p) d -> p j d", p=P), yN[u][:, :, :]).then_inc(o4[u], 16)

                    pairs(sp, EPAIR, body)
                    for u in range(2):
                        for s in (o1, o2, o3, o4) if l == 0 else (o3,):
                            sp.wait_ge(s[u], 16 * EPAIR)

                @block.gpsimd
                def _(pool):
                    def body(i):
                        for u in range(2):
                            free(pool, gx[u], i, k=16 * J)
                            free(pool, tpd, i)
                            if l == 0:
                                free(pool, convd, i)
                            pool.sem_inc(gate, 1)
                            indices(pool, i, u, ixd, IX_SRC if l == 0 else IX_SLOT)
                            rows_gather(pool, u, xN, x3_tab if l == 0 else d1_tab, 0, gx)
                            if l == 0:
                                rows_gather(pool, u, ginv, slot_tab, 0, gs)

                    pairs(pool, EPAIR, body)

                @block.tensor
                def _(pe):
                    def body(i):
                        for u in range(2):
                            landed(pe, gx[u], 16 * J * i + 16 * J)
                            free(pe, carried, i, 1)
                            transposes(A, xN, u).then_inc(tpd, 1)
                            if l == 0:
                                pe.wait_ge(xin[u], 16 * i + 16)
                                free(pe, cpx, i)
                                transposes(B, xb, u).then_inc(tpx, 1)
                        if l == 0:
                            for u in range(2):
                                pe.wait_ge(net, 2 * STEPS * i + 2 * STEPS)
                                free(pe, cp1d, i)
                                for j in range(J):
                                    last = nc.tensor.transpose(H[u][0][:, j * P:(j + 1) * P], dT[u][:, j * P:(j + 1) * P], ident[:, :])
                                last.then_inc(tp1d, 1)

                    pairs(pe, EPAIR, body)

                @block.scalar
                def _(act):
                    def body(i):
                        for u in range(2):
                            act.wait_ge(tpd, ready(i, u))
                            if l == 0:
                                free(act, o1[u], i, k=16)
                                nc.scalar.activation(xsT[u], A[u][:, :], ACT.Copy).then_inc(cpd, 1)
                                act.wait_ge(tpx, ready(i, u))
                                free(act, smd, i)
                                free(act, o2[u], i, k=16)
                                nc.scalar.activation(x3T[u], B[u][:, :], ACT.Identity, bias=cols["nmx"]).then_inc(cpx, 1)
                            else:
                                act.wait_ge(din[u], 32 * i + 32)
                                free(act, carried, i, 1)
                                nc.scalar.activation(xsT[u], hid[u][:, 0, :], ACT.Identity, scale=cols["A1"], bias=cols["bshift"]).then_inc(cpd, 1)
                        if l == 0:
                            for u in range(2):
                                act.wait_ge(tp1d, ready(i, u))
                                free(act, o4[u], i, k=16)
                                nc.scalar.activation(flat(yN[u]), H[u][0][:, :], ACT.Copy).then_inc(cp1d, 1)

                    pairs(act, EPAIR, body)

                @block.vector
                def _(dve):
                    nc.vector.memset(win[0][:, :], 0.0)
                    nc.vector.memset(win[1][:, :], 0.0).then_inc(carried, 1)

                    def body(i):
                        for u in range(2):
                            dve.wait_ge(cpd, ready(i, u))
                            dve.wait_ge(tpd, ready(i, u))
                            dve.wait_ge(carried, ready(i, u))
                            free(dve, net, i, k=2 * STEPS)
                            nc.vector.tensor_copy(win[u][:, 0:3], win[1 - u][:, GR:GR + 3])
                            if l == 0:
                                nc.vector.tensor_scalar(win[u][:, 3:3 + GR], A[u][:, :], cols["nblank0"], None, ADD).then_inc(carried, 1)
                            else:
                                nc.vector.scalar_tensor_tensor(win[u][:, 3:3 + GR], A[u][:, :], cols["s0"], xsT[u], MUL, ADD).then_inc(carried, 1)
                        count = [0]

                        def step(make, after=()):
                            for u in range(2):
                                if count[0]:
                                    dve.wait_ge(net, 2 * STEPS * i + (2 * count[0] + u - 1))
                                for f in after:
                                    f(u)
                                make(u).then_inc(net, 1)
                            count[0] += 1

                        w = work
                        for k in (1, 2, 3):
                            step(lambda u: nc.vector.tensor_tensor(w[u][:, 3 + k, :], krow[u][:, 3:3 + GR], krow[u][:, 3 - k:3 - k + GR], EQ),
                                 after=(lambda u: dve.wait_ge(kin[u], 16 * i + 16),))
                        for k in (1, 2, 3):
                            step(lambda u: nc.vector.tensor_tensor(w[u][:, k, :], win[u][:, 3 - k:3 - k + GR], w[u][:, 3 + k, :], MUL),
                                 after=(lambda u: dve.wait_ge(carried, ready(i, u, 1)),))
                        v = lambda u, k: win[u][:, 3:3 + GR] if k == 8 else w[u][:, k, :]
                        for o, a_, b_, op in ((4, 8, 1, MIN), (5, 8, 1, MAX), (6, 2, 3, MIN), (7, 2, 3, MAX), (0, 4, 6, MIN), (1, 4, 6, MAX),
                                              (2, 5, 7, MIN), (3, 5, 7, MAX), (4, 1, 2, MIN), (5, 1, 2, MAX)):
                            step(lambda u: nc.vector.tensor_tensor(v(u, o), v(u, a_), v(u, b_), op))
                        step(lambda u: nc.vector.tensor_scalar(w[u][:, 6, :], w[u][:, 0, :], val(l, CW), None, MUL))
                        step(lambda u: nc.vector.scalar_tensor_tensor(w[u][:, 7, :], w[u][:, 4, :], val(l, CW + 1), w[u][:, 6, :], MUL, ADD))
                        step(lambda u: nc.vector.scalar_tensor_tensor(w[u][:, 6, :], w[u][:, 5, :], val(l, CW + 2), w[u][:, 7, :], MUL, ADD))
                        step(lambda u: nc.vector.scalar_tensor_tensor(dT[u], w[u][:, 3, :], val(l, CW + 3), w[u][:, 6, :], MUL, ADD),
                             after=(lambda u: free(dve, o3[u], i, k=16),) + ((lambda u: free(dve, tp1d, i),) if l == 0 else ()))
                        e = dT
                        if l == 1:
                            step(lambda u: nc.vector.scalar_tensor_tensor(w[u][:, 5, :], d1T[u], cols["as0"], dT[u], MUL, ADD),
                                 after=(lambda u: dve.wait_ge(din[u], 32 * i + 32),))
                            e = [w[u][:, 5, :] for u in range(2)]
                        step(lambda u: nc.vector.scalar_tensor_tensor(w[u][:, 7, :], e[u], 1.0, last_bc[u], MUL, MUL, accum_out=sum3[u][:, 0:1]),
                             after=(lambda u: dve.wait_ge(lin[u], 16 * i + 16), lambda u: free(dve, smc, i)))
                        for u in range(2):
                            dve.wait_ge(net, 2 * STEPS * i + 2 * STEPS)
                            nc.vector.scalar_tensor_tensor(w[u][:, 1, :], w[u][:, 7, :], 1.0, w[u][:, 7, :], MUL, MUL, accum_out=sum3[u][:, 1:2])
                            if l == 0:
                                dve.wait_ge(cpx, ready(i, u))
                            else:
                                dve.wait_ge(xin[u], 16 * i + 16)
                            nc.vector.scalar_tensor_tensor(w[u][:, 2, :], w[u][:, 7, :], 1.0, x3T[u], MUL, MUL, accum_out=sum3[u][:, 2:3]).then_inc(smd, 1)
                        for u in range(2):
                            dve.wait_ge(smd, ready(i, u))
                            nc.vector.tensor_copy(sums[:, bass.ds(2 * i + u, 1), :].rearrange("p o c -> p (o c)"), sum3[u][:, :]).then_inc(smc, 1)
                            if l == 0:
                                landed(dve, gs[u], 16 * J * i + 16 * J)
                                nc.vector.tensor_copy(ix[:, IX_SLOT, bass.ds((2 * i + u) * J, J)], ginv[u][:, :, 0]).then_inc(convd, 1)

                    pairs(dve, EPAIR, body)

            for s in gx:
                s.end(16 * J * EPAIR)
            if l == 0:
                for s in gs:
                    s.end(16 * J * EPAIR)

        def coefficients(l):
            ph = Phase()
            linked, var_d, inv_d, eps_d, rep, mm = ph.sems(6)
            c = cols
            with nc.Block() as block:

                @block.sync
                def _(sp):
                    ph.clear_other(sp)

                @block.gpsimd
                def _(pool):
                    pool.wait_ge(var_d, 1)
                    nc.gpsimd.tensor_scalar(c["t2"], c["var"], EPS, None, ADD).then_inc(eps_d, 1)
                    pool.wait_ge(eps_d, 1)
                    nc.gpsimd.tensor_tensor(c["inv"], c["t2"], mhalf[:, 0:1], ALU.pow).then_inc(inv_d, 1)

                @block.tensor
                def _(pe):
                    if l == 1:
                        pe.wait_ge(rep, 1)
                        nc.tensor.matmul(A[0][:, 0:D], hid[0][:, 0, 0:P], ident[:, :], start=True, stop=True)
                        nc.tensor.matmul(A[1][:, 0:D], hid[0][:, 1, 0:P], ident[:, :], start=True, stop=True).then_inc(mm, 1)

                @block.vector
                def _(dve):
                    n = [0]

                    def link(ins):
                        n[0] += 1
                        ins.then_inc(linked, 1)
                        dve.wait_ge(linked, n[0])

                    def mul(o, x, y):
                        link(nc.vector.tensor_tensor(o, x, y, MUL))

                    def mad(o, x, y, z):
                        link(nc.vector.scalar_tensor_tensor(o, x, y, z, MUL, ADD))

                    for k, name in enumerate(("sd", "sdd", "sxd")):
                        link(nc.vector.reduce_sum(c[name], sums[:, :, k], axis=mybir.AxisListType.X))
                        link(nc.vector.tensor_scalar(c[("md", "vd", "cov")[k]], c[name], 1.0 / N, None, MUL))
                    slope = val(0, A_)
                    if l == 1:
                        mul(c["alpha"], val(1, A_), c["A1"])
                        slope = c["alpha"]
                    mul(c["t0"], c["md"], c["md"])
                    link(nc.vector.tensor_tensor(c["vd"], c["vd"], c["t0"], SUB))
                    mul(c["t0"], slope, c["vx"])
                    link(nc.vector.scalar_tensor_tensor(c["t1"], c["cov"], 2.0, c["t0"], MUL, ADD))
                    mad(c["var"], c["t1"], slope, c["vd"])
                    dve.sem_inc(var_d, 1)
                    dve.wait_ge(inv_d, 1)
                    s = c[f"s{l}"]
                    mul(s, c["inv"], val(l, G_))
                    mad(c["mu"], slope, c["mx"], c["md"])
                    if l == 0:
                        link(nc.vector.tensor_tensor(c["mu"], c["mu"], c["c0"], ADD))
                        link(nc.vector.tensor_tensor(c["t0"], c["c0"], c["mu"], SUB))
                        mad(c["B1"], c["t0"], s, val(0, BE))
                        link(nc.vector.tensor_scalar(c["A1"], s, val(0, A_), 1.0, MUL, ADD))
                        link(nc.vector.tensor_tensor(c["bshift"], c["B1"], c["blankp1"], SUB))
                        mul(c["as0"], val(1, A_), s)
                        return
                    mad(c["t1"], c["B1"], val(1, A_), c["c1"])
                    link(nc.vector.tensor_tensor(c["mu"], c["mu"], c["t1"], ADD))
                    link(nc.vector.tensor_tensor(c["t0"], c["t1"], c["mu"], SUB))
                    mad(c["Dv"], c["t0"], s, val(1, BE))
                    link(nc.vector.tensor_tensor(c["Dv"], c["Dv"], c["B1"], ADD))
                    mad(c["C"], c["alpha"], s, c["A1"])
                    link(nc.vector.tensor_scalar(c["C"], c["C"], 1.0, None, ADD))
                    mad(c["F1"], c["as0"], s, c["s0"])
                    link(nc.vector.tensor_scalar(hid[0][:, 0, 0:P], ones[:, :], c["C"], None, MUL))
                    nc.vector.tensor_scalar(hid[0][:, 1, 0:P], ones[:, :], c["Dv"], None, MUL).then_inc(rep, 1)
                    dve.wait_ge(mm, 1)
                    for j in range(J):
                        nc.vector.tensor_copy(C_bc[:, j, :], A[0][:, 0:D])
                        last = nc.vector.tensor_copy(D_bc[:, j, :], A[1][:, 0:D])
                    link(last)

        def finish(edge):
            n_pairs = EPAIR if edge else NPAIR
            ph = Phase()
            cd, dd, rd, fd, fd2, tpd, ixd = ph.sems(7)
            xin, din = (ph.sems(2), ph.sems(2)), (ph.sems(2), ph.sems(2))
            oo = sca_a if edge else ph.sems(2)
            per = 16 * J if edge else 16
            norm = Norm(ph, rN, zN)
            r_done = rd if edge else dd
            sumN = [xb, xb] if edge else [xb, rN]

            def norm_of(q):
                norm.r = rN if edge else sumN[q]
                return norm

            d12 = [[hid2[q][u][:, :, :] for u in range(2)] for q in range(2)]
            L1, L2, L3 = 1, 2, 3
            with nc.Block() as block:

                @block.sync
                def _(sp):
                    ph.clear_other(sp)

                    def load(i, q):
                        for u in range(2):
                            g = 2 * i + u
                            free(sp, cd, i, ago=2)
                            if edge:
                                free(sp, fd2, i, ago=2)
                                sp.dma_start(flat(x2N[q][u]), plane(x3_c, g)).then_inc(xin[q][u], 16)
                                sp.dma_start(d12[q][u][:, 0, :], plane(d1_t, g)).then_inc(din[q][u], 16)
                                sp.dma_start(d12[q][u][:, 1, :], plane(d2_t, g)).then_inc(din[q][u], 16)
                            else:
                                sp.dma_start(flat(x2N[q][u]), group(x3_tab, g)).then_inc(xin[q][u], 16)

                    def store(i, q):
                        for u in range(2):
                            g = 2 * i + u
                            sp.wait_ge(norm.done, ready(i, u))
                            if isinstance(i, int) and g == NG - 1:
                                sp.dma_start(tail(out), flat(zN[u])[0:TAILP, :]).then_inc(oo[u], 16)
                            else:
                                sp.dma_start(group(out, g), flat(zN[u])).then_inc(oo[u], 16)

                    def body(i, q):
                        late(i, q, 0, n_pairs, load)
                        if not edge:
                            late(i, q, L3, n_pairs, store)

                    pipeline(sp, n_pairs, L3, body)
                    if not edge:
                        for u in range(2):
                            sp.wait_ge(oo[u], 16 * NPAIR)

                @block.gpsimd
                def _(pool):
                    def add_d(i, q):
                        for u in range(2):
                            pool.wait_ge(cd, ready(i, u))
                            free(pool, rd if edge else norm.done, i, ago=1 if edge else 2)
                            nc.gpsimd.tensor_tensor(flat(sumN[q][u]), flat(yN[u]), flat(D_bc), ADD).then_inc(dd, 1)

                    def scatter(i, q):
                        for u in range(2):
                            free(pool, oo[u], i, k=per)
                            pool.wait_ge(norm.done, ready(i, u))
                            pool.sem_inc(gate, 1)
                            indices(pool, i, u, ixd, IX_DSTW)
                            rows_scatter(pool, u, zN, out, 0, oo)

                    def body(i, q):
                        late(i, q, L1, n_pairs, add_d)
                        late(i, q, L2, n_pairs, lambda i, q: norm.rstd_steps(pool, i, True))
                        if edge:
                            late(i, q, L3, n_pairs, scatter)

                    pipeline(pool, n_pairs, L3, body)
                    if edge:
                        for u in range(2):
                            landed(pool, oo[u], per * EPAIR)

                @block.tensor
                def _(pe):
                    if edge:
                        def trans_f(i, q):
                            for u in range(2):
                                pe.wait_ge(fd2, ready(i, u))
                                free(pe, rd, i)
                                for j in range(J):
                                    last = nc.tensor.transpose(A[u][:, j * P:(j + 1) * P], xT[u][:, j * P:(j + 1) * P], ident[:, :])
                                last.then_inc(tpd, 1)

                        pipeline(pe, n_pairs, L3, lambda i, q: late(i, q, L1, n_pairs, trans_f))

                @block.scalar
                def _(act):
                    pipeline(act, n_pairs, L3, lambda i, q: late(i, q, L3, n_pairs, lambda i, q: norm_of(q).act_scale_steps(
                        act, i, lambda e, i, u: free(e, oo[u], i, k=per))))

                @block.vector
                def _(dve):
                    def mul_c(i, q):
                        for u in range(2):
                            landed_pair(dve, xin[q][u], i, q, 16)
                            free(dve, dd, i)
                            nc.vector.tensor_tensor(flat(yN[u]), flat(x2N[q][u]), flat(C_bc), MUL).then_inc(cd, 1)

                    def add_f(i, q):
                        for u in range(2):
                            landed_pair(dve, din[q][u], i, q, 32)
                            free(dve, tpd, i)
                            nc.vector.tensor_scalar(xT[u][:, :], d12[q][u][:, 0, :], cols["F1"], None, MUL).then_inc(fd, 1)
                        for u in range(2):
                            dve.wait_ge(fd, ready(i, u))
                            nc.vector.scalar_tensor_tensor(xT[u][:, :], d12[q][u][:, 1, :], cols["s1"], xT[u][:, :], MUL, ADD).then_inc(fd2, 1)

                    def residual(i, q):
                        for u in range(2):
                            dve.wait_ge(dd, ready(i, u))
                            dve.wait_ge(tpd, ready(i, u))
                            free(dve, norm.done, i)
                            nc.vector.tensor_tensor(flat(rN[u]), A[u][:, :], flat(xb[u]), ADD).then_inc(rd, 1)

                    def body(i, q):
                        if edge:
                            late(i, q, L2, n_pairs, residual)
                        late(i, q, L1, n_pairs, mul_c)
                        if edge:
                            late(i, q, L1, n_pairs, add_f)
                        late(i, q, L2, n_pairs, lambda i, q: norm_of(q).moments_steps(dve, i, r_done))

                    pipeline(dve, n_pairs, L3, body)

            if edge:
                for s in oo:
                    s.end(per * EPAIR)

        sorted_pool(0)
        coefficients(0)
        sorted_pool(1)
        coefficients(1)
        finish(False)
        finish(True)


_LAYOUT = (
    ("x", "x", None), ("src", "src", None), ("dst", "dst", None), ("edge_attr", "edge_attr_128", None),
    ("edge_type_8", "edge_type_8", None), ("W1a", "L0_gnn_W1a", None), ("b1a", "L0_gnn_b1a", None),
    ("W1bT", "L0_gnn_W1b", (1, 0)), ("b1b", "L0_gnn_b1b", None), ("W2a", "L0_gnn_W2a", None), ("b2a", "L0_gnn_b2a", None),
    ("W2b", "L0_gnn_W2b", None), ("b2b", "L0_gnn_b2b", None), ("WL1", "L1_gnn_W", (1, 0)),
    ("Wp", "L2_gnn_node_proj_w", (1, 0)), ("bp", "L2_gnn_node_proj_b", None), ("We", "L2_gnn_edge_W", (0, 1, 3, 2)),
    ("Wih", "L2_gnn_gru_wih", (0, 2, 1)), ("Whh", "L2_gnn_gru_whh", (0, 2, 1)), ("bih", "L2_gnn_gru_bih", None),
    ("bhh", "L2_gnn_gru_bhh", None), ("Wo", "L2_gnn_out_w", (1, 0)), ("bo", "L2_gnn_out_b", None),
    ("W3", ("L3_gnn_W0", "L3_gnn_W1"), (0, 2, 1)),
    *((f"{n}{l}", f"L3_gnn_{n}{l}", None) for l in range(2) for n in ("b", "cw", "cb", "a", "g", "be", "blank")),
)


def kernel(**inputs):
    from concourse import bacc
    from concourse.bass_utils import run_bass_kernel_spmd

    nc = bacc.Bacc("TRN2", target_bir_lowering=False, num_devices=1)
    arrays, args = {}, {}
    for name, source, order in _LAYOUT:
        if isinstance(source, tuple):
            x = np.stack([np.asarray(inputs[s]) for s in source])
        else:
            x = np.asarray(inputs[source])
        if order:
            x = x.transpose(order)
        if name == "We":
            x = x.reshape(NLAYER * NTYPE, D, D)
        x = np.ascontiguousarray(x)
        arrays["in_" + name] = x
        args[name] = nc.dram_tensor("in_" + name, x.shape, mybir.dt.from_np(x.dtype), kind="ExternalInput").ap()
    out = nc.dram_tensor("out", (N, D), F32, kind="ExternalOutput").ap()
    build(nc, args, out)
    return run_bass_kernel_spmd(nc, [arrays], core_ids=[0]).results[0]["out"]
```
